# Optimizing a Trainium2 kernel written in Bass

```python
import numpy as np
import jax
import jax.numpy as jnp

def _softmax(x, axis=-1):
    return jax.nn.softmax(x, axis=axis)

def _gelu(x):
    return jax.nn.gelu(x, approximate=True)

def _silu(x):
    return jax.nn.silu(x)

def _sigmoid(x):
    return jax.nn.sigmoid(x)

def _layernorm(x, axis=-1, eps=1e-05):
    m = jnp.mean(x, axis=axis, keepdims=True)
    v = jnp.var(x, axis=axis, keepdims=True)
    return (x - m) / jnp.sqrt(v + eps)

def _scatter_add(tgt, idx, src, axis=0):
    return tgt.at[idx].add(src)

def _segment_sum(src, seg, n):
    return jax.ops.segment_sum(src, seg, n)
kernel_name = 'mk_xattn_seq_d1_seqx_r4_390bbe'

def setup_inputs(seed: int=0):
    np.random.seed(seed)
    _w = jnp.asarray

    def _rec_inputs():
        import jax
        import jax.numpy as jnp
        _rk = jax.random.key(seed)
        x = -0.0001233 + 1 * jax.random.normal(jax.random.fold_in(_rk, 1), (64, 256, 320), jnp.float32)
        _lenS = 256 - jax.random.randint(jax.random.fold_in(_rk, 7), (64,), 0, max(1, 256 // 4) + 1, jnp.int32)
        _lenS2 = 77 - jax.random.randint(jax.random.fold_in(_rk, 8), (64,), 0, max(1, 77 // 4) + 1, jnp.int32)
        _ctx_768P = jax.random.normal(jax.random.fold_in(_rk, 11), (64, 16, 192), jnp.float32)
        _ctx_768c = jax.random.dirichlet(jax.random.fold_in(_rk, 511), 0.3 * jnp.ones((16,), jnp.float32), (64, 77))
        _ctx_768t = jnp.einsum('bsk,bkd->bsd', _ctx_768c, _ctx_768P)
        _ctx_768t = _ctx_768t * jax.lax.rsqrt(jnp.mean(jnp.square(_ctx_768t)) + 1e-12) * 0.953939
        ctx_768 = 0.00272024 + 0.999456 * (_ctx_768t + 0.3 * jax.random.normal(jax.random.fold_in(_rk, 611), (64, 77, 192), jnp.float32))
        return (x, ctx_768)
    x, ctx_768 = _rec_inputs()

    def _L0_xattn_setup():
        import jax, jax.numpy as jnp
        import numpy as np
        D = 320
        H = 20
        DH = D // H
        CTX = 192
        FF_IN = 4 * D
        EPS = 1e-05

        def _ln(x, g, b):
            m = jnp.mean(x, axis=-1, keepdims=True)
            v = jnp.mean(jnp.square(x - m), axis=-1, keepdims=True)
            return (x - m) * jax.lax.rsqrt(v + EPS) * g + b

        def _attn(x, ctx, wq, wk, wv, wo, bo, heads):
            b, n, _ = x.shape
            j = ctx.shape[1]
            dh = wq.shape[1] // heads
            scale = dh ** (-0.5)
            q = (x @ wq).reshape(b, n, heads, dh).transpose(0, 2, 1, 3)
            k = (ctx @ wk).reshape(b, j, heads, dh).transpose(0, 2, 1, 3)
            v = (ctx @ wv).reshape(b, j, heads, dh).transpose(0, 2, 1, 3)
            sim = jnp.einsum('bhid,bhjd->bhij', q, k) * scale
            a = jax.nn.softmax(sim, axis=-1)
            out = jnp.einsum('bhij,bhjd->bhid', a, v)
            out = out.transpose(0, 2, 1, 3).reshape(b, n, heads * dh)
            return out @ wo + bo
        key = jax.random.key(seed)
        ks = jax.random.split(key, 24)
        r = lambda k, shp, s: jax.random.normal(k, shp, dtype=jnp.float32) * s
        d = {'x': r(ks[0], (8, 256, D), 1.0), 'context': r(ks[1], (8, 77, CTX), 1.0), 'heads': H, 'n1_g': jnp.ones((D,), jnp.float32), 'n1_b': jnp.zeros((D,), jnp.float32), 'q1': r(ks[2], (D, D), D ** (-0.5)), 'k1': r(ks[3], (D, D), D ** (-0.5)), 'v1': r(ks[4], (D, D), D ** (-0.5)), 'o1_w': r(ks[5], (D, D), D ** (-0.5)), 'o1_b': jnp.zeros((D,), jnp.float32), 'n2_g': jnp.ones((D,), jnp.float32), 'n2_b': jnp.zeros((D,), jnp.float32), 'q2': r(ks[6], (D, D), D ** (-0.5)), 'k2': r(ks[7], (CTX, D), CTX ** (-0.5)), 'v2': r(ks[8], (CTX, D), CTX ** (-0.5)), 'o2_w': r(ks[9], (D, D), D ** (-0.5)), 'o2_b': jnp.zeros((D,), jnp.float32), 'n3_g': jnp.ones((D,), jnp.float32), 'n3_b': jnp.zeros((D,), jnp.float32), 'ff_w1': r(ks[10], (D, 2 * FF_IN), D ** (-0.5)), 'ff_b1': jnp.zeros((2 * FF_IN,), jnp.float32), 'ff_w2': r(ks[11], (FF_IN, D), FF_IN ** (-0.5)), 'ff_b2': jnp.zeros((D,), jnp.float32)}
        return d
    _L0_xattn_all = _L0_xattn_setup()
    _L0_xattn_in = {k: v for k, v in _L0_xattn_all.items() if k in ('n1_g', 'n1_b', 'q1', 'k1', 'v1', 'o1_w', 'o1_b', 'n2_g', 'n2_b', 'q2', 'k2', 'v2', 'o2_w', 'o2_b', 'n3_g', 'n3_b', 'ff_w1', 'ff_b1', 'ff_w2', 'ff_b2')}
    del _L0_xattn_all
    return {'x': x, 'ctx_768': ctx_768, 'L0_xattn_n1_g': _L0_xattn_in['n1_g'], 'L0_xattn_n1_b': _L0_xattn_in['n1_b'], 'L0_xattn_q1': _L0_xattn_in['q1'], 'L0_xattn_k1': _L0_xattn_in['k1'], 'L0_xattn_v1': _L0_xattn_in['v1'], 'L0_xattn_o1_w': _L0_xattn_in['o1_w'], 'L0_xattn_o1_b': _L0_xattn_in['o1_b'], 'L0_xattn_n2_g': _L0_xattn_in['n2_g'], 'L0_xattn_n2_b': _L0_xattn_in['n2_b'], 'L0_xattn_q2': _L0_xattn_in['q2'], 'L0_xattn_k2': _L0_xattn_in['k2'], 'L0_xattn_v2': _L0_xattn_in['v2'], 'L0_xattn_o2_w': _L0_xattn_in['o2_w'], 'L0_xattn_o2_b': _L0_xattn_in['o2_b'], 'L0_xattn_n3_g': _L0_xattn_in['n3_g'], 'L0_xattn_n3_b': _L0_xattn_in['n3_b'], 'L0_xattn_ff_w1': _L0_xattn_in['ff_w1'], 'L0_xattn_ff_b1': _L0_xattn_in['ff_b1'], 'L0_xattn_ff_w2': _L0_xattn_in['ff_w2'], 'L0_xattn_ff_b2': _L0_xattn_in['ff_b2']}

def reference(x, ctx_768, L0_xattn_n1_g, L0_xattn_n1_b, L0_xattn_q1, L0_xattn_k1, L0_xattn_v1, L0_xattn_o1_w, L0_xattn_o1_b, L0_xattn_n2_g, L0_xattn_n2_b, L0_xattn_q2, L0_xattn_k2, L0_xattn_v2, L0_xattn_o2_w, L0_xattn_o2_b, L0_xattn_n3_g, L0_xattn_n3_b, L0_xattn_ff_w1, L0_xattn_ff_b1, L0_xattn_ff_w2, L0_xattn_ff_b2):
    import jax
    import jax.numpy as jnp

    def _L0_xattn_ref(x, context, heads, n1_g, n1_b, q1, k1, v1, o1_w, o1_b, n2_g, n2_b, q2, k2, v2, o2_w, o2_b, n3_g, n3_b, ff_w1, ff_b1, ff_w2, ff_b2):
        import jax, jax.numpy as jnp
        import numpy as np
        D = 320
        H = 20
        DH = D // H
        CTX = 192
        FF_IN = 4 * D
        EPS = 1e-05

        def _ln(x, g, b):
            m = jnp.mean(x, axis=-1, keepdims=True)
            v = jnp.mean(jnp.square(x - m), axis=-1, keepdims=True)
            return (x - m) * jax.lax.rsqrt(v + EPS) * g + b

        def _attn(x, ctx, wq, wk, wv, wo, bo, heads):
            b, n, _ = x.shape
            j = ctx.shape[1]
            dh = wq.shape[1] // heads
            scale = dh ** (-0.5)
            q = (x @ wq).reshape(b, n, heads, dh).transpose(0, 2, 1, 3)
            k = (ctx @ wk).reshape(b, j, heads, dh).transpose(0, 2, 1, 3)
            v = (ctx @ wv).reshape(b, j, heads, dh).transpose(0, 2, 1, 3)
            sim = jnp.einsum('bhid,bhjd->bhij', q, k) * scale
            a = jax.nn.softmax(sim, axis=-1)
            out = jnp.einsum('bhij,bhjd->bhid', a, v)
            out = out.transpose(0, 2, 1, 3).reshape(b, n, heads * dh)
            return out @ wo + bo
        h1 = _ln(x, n1_g, n1_b)
        x = _attn(h1, h1, q1, k1, v1, o1_w, o1_b, heads) + x
        h2 = _ln(x, n2_g, n2_b)
        x = _attn(h2, context, q2, k2, v2, o2_w, o2_b, heads) + x
        h3 = _ln(x, n3_g, n3_b)
        proj = h3 @ ff_w1 + ff_b1
        a, g = jnp.split(proj, 2, axis=-1)
        ff = a * jax.nn.gelu(g, approximate=False) @ ff_w2 + ff_b2
        return ff + x
    x = _L0_xattn_ref(x, ctx_768, 20, L0_xattn_n1_g, L0_xattn_n1_b, L0_xattn_q1, L0_xattn_k1, L0_xattn_v1, L0_xattn_o1_w, L0_xattn_o1_b, L0_xattn_n2_g, L0_xattn_n2_b, L0_xattn_q2, L0_xattn_k2, L0_xattn_v2, L0_xattn_o2_w, L0_xattn_o2_b, L0_xattn_n3_g, L0_xattn_n3_b, L0_xattn_ff_w1, L0_xattn_ff_b1, L0_xattn_ff_w2, L0_xattn_ff_b2)
    return x

_drawn_inputs = setup_inputs


def setup_inputs(seed=0):
    import zlib

    import numpy as np

    out = dict(_drawn_inputs(seed))
    spreads = {'L0_xattn_n1_g': (1.0, 0.2),
     'L0_xattn_n1_b': (0.0, 0.1),
     'L0_xattn_o1_b': (0.0, 0.1),
     'L0_xattn_n2_g': (1.0, 0.2),
     'L0_xattn_n2_b': (0.0, 0.346),
     'L0_xattn_o2_b': (0.0, 0.1),
     'L0_xattn_n3_g': (1.0, 0.2),
     'L0_xattn_n3_b': (0.0, 0.1),
     'L0_xattn_ff_b1': (0.0, 0.1),
     'L0_xattn_ff_b2': (0.0, 0.1)}
    factors = {}
    for name, (base, spread) in spreads.items():
        noise = np.random.default_rng([zlib.crc32(name.encode()), seed]).standard_normal(out[name].shape)
        drawn = base * np.exp(spread * noise) if base else spread * noise
        out[name] = jnp.asarray(drawn.astype(out[name].dtype))
    for name, factor in factors.items():
        out[name] = (out[name] * factor).astype(out[name].dtype)
    return out
```

```python
import concourse.bass as bass
from concourse import mybir
from contextlib import ExitStack

B, N, D = 64, 256, 320
H, DH = 20, 16
J, CTX = 77, 192
FF = 4 * D
EPS = 1e-5
P = 128
KT = N // P
NT = H // 2
NG = H // 4
NM = FF // P
AUG = 32768.0
NP = 4
NSTAGE = 3
STW = 3 * D


def xattn_block(nc, t, out):
    f32, f32r, f16, u32 = mybir.dt.float32, mybir.dt.float32r, mybir.dt.float16, mybir.dt.uint32
    ACT, ALU, AX = mybir.ActivationFunctionType, mybir.AluOpType, mybir.AxisListType
    ctx = ExitStack()

    def sb(name, shape, dt):
        return ctx.enter_context(nc.sbuf_tensor(name, shape, dt))

    class Event:

        def __init__(self, name, n):
            self.sem, self.n = ctx.enter_context(nc.semaphore(name)), n

        def at(self, e, k=None):
            value = e * self.n + (self.n if k is None else k)
            return max(value, 0) if isinstance(value, int) else value

    with ctx:
        wqkv_h, wqkv_l = sb("wqkv_h", [P, 3, 3 * D], f16), sb("wqkv_l", [P, 3, 3 * D], f16)
        wo1_h, wo1_l = sb("wo1_h", [P, 3, D], f16), sb("wo1_l", [P, 3, D], f16)
        wq2_h, wq2_l = sb("wq2_h", [P, 3, D], f16), sb("wq2_l", [P, 3, D], f16)
        wo2_h, wo2_l = sb("wo2_h", [P, 3, D], f16), sb("wo2_l", [P, 3, D], f16)
        wkv2_h, wkv2_l = sb("wkv2_h", [P, 2, 2 * D], f16), sb("wkv2_l", [P, 2, 2 * D], f16)
        w1_h, w1_l = sb("w1_h", [P, 3, 2 * FF], f16), sb("w1_l", [P, 3, 2 * FF], f16)
        w2_h, w2_l = sb("w2_h", [P, NM, D], f32r), sb("w2_l", [P, NM, D], f32r)
        ident = sb("ident", [P, P], f32)
        sel = sb("sel", [H, 3 * P], f32r)
        ones = sb("ones", [8, P], f32)
        gb = sb("gb", [P, 6, 3], f32)
        cvec = sb("cvec", [P, 32], f32)
        b1c = sb("b1c", [P, 2 * NM], f32)
        bias1, bias2, bias3 = (sb(f"bias{k}", [P, D], f32) for k in (1, 2, 3))
        mx = sb("mx", [P, 40], f32)
        mxm = sb("mxm", [P, 8], f32)
        mxr, mxd = sb("mxr", [8, 4], f32), sb("mxd", [8, 8], f32)
        rp = sb("rp", [P, 8], f32)
        sc = sb("sc", [P, 16], f32)
        halfneg = sb("halfneg", [P, KT], f32)
        pace = sb("pace", [P, 1], f32)
        x_in, xb1, x1, xb2, x2, xb3, out_sb = (
            sb(n, [P, KT, D], f32) for n in ("x_in", "xb1", "x1", "xb2", "x2", "xb3", "out_sb"))
        sel_f = out_sb[0:H].rearrange("p a b -> p (a b)")[:, 0:3 * P]
        cv_rep = x2[:].rearrange("p a b -> p (a b)")[:, 0:3 * P].rearrange("p (s c) -> p s c", s=3)
        xhat = sb("xhat", [P, KT, 3 * P], f32)
        stats = [sb(f"stats{k}", [P, KT, 6], f32) for k in range(3)]
        mv = [sb(f"mv{k}", [P, KT, 2], f32) for k in range(3)]
        ve = [sb(f"ve{k}", [P, KT], f32) for k in range(3)]
        rs = [sb(f"rs{k}", [P, KT], f32) for k in range(3)]
        ah = [sb(f"ah{k}", [P, 3, N], f16) for k in range(3)]
        al = [sb(f"al{k}", [P, 2, N], f16) for k in range(3)]
        qk_h, qk_l = sb("qk_h", [P, 5, N], f16), sb("qk_l", [P, 5, N], f16)
        q4, k4 = sb("q4", [P, NT, N], f16), sb("k4", [P, NT, N], f16)
        v1 = sb("v1", [P, KT, H, 2 * DH], f32)
        c_in = sb("c_in", [J, 2 * P], f32)
        ct_h, ct_l = sb("ct_h", [P, 2, J], f16), sb("ct_l", [P, 1, J], f16)
        k2_h, k2_l = sb("k2_h", [P, 3, J], f16), sb("k2_l", [P, 3, J], f16)
        q2_h, q2_l = sb("q2_h", [P, 3, N], f16), sb("q2_l", [P, 3, N], f16)
        q42, k42 = sb("q42", [P, NT, N], f16), sb("k42", [P, NT, J], f16)
        v2 = sb("v2", [J, H, 2 * DH], f32)
        m_q = [sb(f"m_q{a}", [P, 2, NT, KT], f32) for a in range(2)]
        m_row = [sb(f"m_row{a}", [H, N], f16) for a in range(2)]
        probs = sb("probs", [P, NP, 4 * N], f32)
        stage = probs[:, :, :].rearrange("p a b -> p (a b)")
        o_raw = [sb(f"o_raw{a}", [P, NG, N], f32) for a in range(2)]
        o_c = [sb(f"o_c{a}", [P, 3, N], f32) for a in range(2)]
        o_h = [sb(f"o_h{a}", [P, 3, N], f16) for a in range(2)]
        o_l = [sb(f"o_l{a}", [P, 2, N], f16) for a in range(2)]
        den = [sb(f"den{a}", [H, N], f32) for a in range(2)]
        rec = [sb(f"rec{a}", [H, N], f32) for a in range(2)]
        rec_h = [sb(f"rec_h{a}", [H, N], f32r) for a in range(2)]
        rec_l = [sb(f"rec_l{a}", [H, N], f32r) for a in range(2)]
        ff_g, ff_p = sb("ff_g", [P, 2, N], f32), sb("ff_p", [P, 2, N], f32)
        ff_h, ff_l = sb("ff_h", [P, 2, N], f32r), sb("ff_l", [P, 2, N], f32r)

        ps = ctx.enter_context(nc.psum_tensor("ps", [P, 8, 512], f32))
        slot = [ps[:, 0:2, :], ps[:, 2:4, :]]
        flat = [s.rearrange("p a b -> p (a b)") for s in slot]
        ps_pv, ps_f1, ps_f2 = ps[:, 4, :], ps[:, 5, :], [ps[:, 6, :], ps[:, 7, :]]

        (S_QKV, S_Q2, S_W1, S_KV2, S_CTX, S_O1, S_O2, E1, E2, D1, D2, D3, T0, T1, T2) = range(15)

        x_loaded, c_loaded = Event("x_loaded", 16), Event("c_loaded", 32)
        ln_stat = [Event(f"ln_stat{k}", 3) for k in range(3)]
        ln_rstd = [Event(f"ln_rstd{k}", 1) for k in range(3)]
        ln_done = [Event(f"ln_done{k}", 1) for k in range(3)]
        tr_done = [Event(f"tr_done{k}", 1) for k in range(3)]
        tr_hi = [Event(f"tr_hi{k}", 1) for k in range(3)]
        tr_lo = [Event(f"tr_lo{k}", 1) for k in range(3)]
        qk_done, qk_hi, qk_lo = Event("qk_done", 2), Event("qk_hi", 2), Event("qk_lo", 2)
        v_done, v_copied = Event("v_done", 1), Event("v_copied", 1)
        spread = [Event(f"spread{r}", 6 * 16) for r in range(4)]
        max_done, max_red = Event("max_done", NT), Event("max_red", NT)
        max2_done, max2_red = Event("max2_done", 4), Event("max2_red", 4)
        mt_done = [Event(f"mt_done{a}", 1) for a in range(2)]
        mt_row = [Event(f"mt_row{a}", 1) for a in range(2)]
        m_spread = [Event(f"m_spread{a}", 32) for a in range(2)]
        st_done = [Event("st_done0", NT), Event("st_done1", NG)]
        exp_done = [Event("exp_done0", NT), Event("exp_done1", NG)]
        pv_done = [Event(f"pv_done{a}", NG) for a in range(2)]
        o_copied = [Event(f"o_copied{a}", NG) for a in range(2)]
        o_spread = [Event(f"o_spread{a}", 48) for a in range(2)]
        den_spread = [Event(f"den_spread{a}", 16) for a in range(2)]
        rec_done = [Event(f"rec_done{a}", 1) for a in range(2)]
        rec_hi = [Event(f"rec_hi{a}", 1) for a in range(2)]
        rec_lo = [Event(f"rec_lo{a}", 1) for a in range(2)]
        rb_done = [Event(f"rb_done{a}", 1) for a in range(2)]
        o_norm = [Event(f"o_norm{a}", 1) for a in range(2)]
        o_hi = [Event(f"o_hi{a}", 1) for a in range(2)]
        o_lo = [Event(f"o_lo{a}", 2) for a in range(2)]
        oproj_done = [Event(f"oproj_done{a}", 1) for a in range(2)]
        resid = [Event(f"resid{a}", 1) for a in range(2)]
        xb_done = [Event(f"xb_done{a}", 1) for a in range(3)]
        q2_done, q2_hi, q2_lo = Event("q2_done", 1), Event("q2_hi", 1), Event("q2_lo", 1)
        q2_spread = Event("q2_spread", 12 * 16)
        ct_done, ct_hi, ct_lo = Event("ct_done", 1), Event("ct_hi", 1), Event("ct_lo", 1)
        kv2_done, k2_hi, k2_lo = Event("kv2_done", 1), Event("k2_hi", 1), Event("k2_lo", 1)
        v2_copied, k2_spread = Event("v2_copied", 1), Event("k2_spread", 12 * 16)
        ff1_done, gelu_done, ffp_done = Event("ff1_done", NM), Event("gelu_done", NM), Event("ffp_done", NM)
        ffh_done, ffl_done, ff2_step = Event("ffh_done", NM), Event("ffl_done", NM), Event("ff2_step", NM)
        out_ready, out_stored = Event("out_ready", 1), Event("out_stored", 16)

        UNITS = [(("st", T), 1, exp_done[0], T + 1) for T in range(NT)]
        UNITS += [(("st2", g), 2, exp_done[1], g + 1) for g in range(NG)]
        UNITS += [(("tr", 0), 0, tr_lo[0], 1), (("qk", 0), 0, qk_lo, 1), (("qk", 1), 0, qk_lo, 2),
                  (("rb", 0), 1, o_norm[0], 1), (("v", 0), 0, v_copied, 1), (("oproj", 0), 1, resid[0], 1),
                  (("ct", 0), 1, ct_lo, 1), (("rb", 1), 2, o_norm[1], 1), (("kv2", 0), 1, v2_copied, 1),
                  (("oproj", 1), 2, resid[1], 1), (("tr", 1), 1, tr_lo[1], 1), (("q2", 0), 1, q2_lo, 1),
                  (("tr", 2), 2, tr_lo[2], 1)]
        UNITS += [(("max", n), 0, max_red, n + 1) for n in range(NT)]
        UNITS += [(("mt", 0), 0, mt_row[0], 1)]
        UNITS += [(("max2", n), 1, max2_red, n + 1) for n in range(4)]
        UNITS += [(("mt", 1), 1, mt_row[1], 1)]
        MAX_ORDER = [0, 4, 8, 1, 5, 9, 2, 6, 3, 7]
        MAX2_PAIRS = [(0, 3), (3, 3), (6, 3), (9, 1)]

        STREAM_STEP = (1, 0, -1)

        def ring(active, before, units=None, slots=2):
            last, table = {}, {}
            for ago, streams in ((1, before), (0, active)):
                uses = [u for u in (UNITS if units is None else units) if u[1] in streams]
                for n, (name, stream, ev, k) in enumerate(uses):
                    if ago == 0:
                        table[name] = (n % slots, last.get(n % slots))
                    last[n % slots] = (ev, STREAM_STEP[stream] - ago, k)
            return table

        PROBS = [((0, T), 1, pv_done[0], T // 2 + 1) for T in range(NT)]
        PROBS += [((1, g), 2, pv_done[1], g + 1) for g in range(NG)]

        def probs_ring(active, before):
            return ring(active, before, PROBS, NP)

        STREAM_SETS = {-1: (0,), 0: (0, 1), B - 1: (1, 2), B: (2,)}

        def streams_of(i):
            return STREAM_SETS.get(i, (0, 1, 2)) if isinstance(i, int) else (0, 1, 2)

        def before_of(i):
            return () if isinstance(i, int) and i == -1 else streams_of(i - 1 if isinstance(i, int) else i)

        def run_steps(eng, step):
            for i in (-1, 0, 1):
                step(i)
            with eng.Fori(2, B - 1) as i:
                step(i)
            for i in (B - 1, B):
                step(i)

        def split_passes(xh, xl, wh, wl, full):
            pairs = []
            for s in range(full):
                pairs += [(xh[:, s], wh[:, s]), (xl[:, s], wh[:, s]), (xh[:, s], wl[:, s])]
            return pairs + [(xh[:, full], wh[:, full]), (xh[0:64, full], wl[0:64, full])]

        CW = 256
        def slices(k):
            return 3 if k == D else 2
        MATS = [("q1", 0, D, 0, S_QKV), ("k1", 0, D, 0, S_QKV), ("v1", 0, D, 0, S_QKV), ("q2", 0, D, 1, S_Q2)]
        MATS += [("ff_w1", c * CW, CW, 2, S_W1) for c in range(2 * FF // CW)]
        LNMATS = len(MATS)
        MATS += [("k2", 0, D, None, S_KV2), ("v2", 0, D, None, S_KV2), ("o2_w", 0, D, None, S_O2),
                 ("o1_w", 0, D, None, S_O1)]
        CTXCH = [(b, min(5, B - b)) for b in range(0, B, 5)]
        W2CH = [(s, min(3, NM - s)) for s in range(0, NM, 3)]
        DEST = {"q1": (wqkv_h, wqkv_l, 0), "k1": (wqkv_h, wqkv_l, D), "v1": (wqkv_h, wqkv_l, 2 * D),
                "q2": (wq2_h, wq2_l, 0), "ff_w1": (w1_h, w1_l, 0), "k2": (wkv2_h, wkv2_l, 0),
                "v2": (wkv2_h, wkv2_l, D), "o2_w": (wo2_h, wo2_l, 0), "o1_w": (wo1_h, wo1_l, 0)}
        CHUNKS = [("ctx",) + c for c in CTXCH] + [("max",) + m for m in MATS]
        CHUNKS += [("cut",) + m for m in MATS] + [("w2",) + c for c in W2CH]
        N1 = len(CTXCH) + len(MATS)
        staged, vec_loaded = [Event(f"staged{k}", 16) for k in range(NSTAGE)], Event("vec_loaded", 16)
        stage_used, c_product = Event("stage_used", 1), Event("c_product", 1)
        pro, pro_pe, pro_act = Event("pro", 1), Event("pro_pe", 1), Event("pro_act", 1)
        pro_dve, pro_hi, maxima, cv_ready = (Event(n, 1) for n in ("pro_dve", "pro_hi", "maxima", "cv_ready"))
        tmp = stage[:, NSTAGE * STW:(NSTAGE + 1) * STW]

        def stage_buf(n):
            return stage[:, (n % NSTAGE) * STW:(n % NSTAGE + 1) * STW]

        def chunk_dmas(n):
            ch, buf = CHUNKS[n], stage_buf(n)
            if ch[0] == "ctx":
                _, b, nb = ch
                return [(buf[0:J, 0:nb * CTX].rearrange("p (b c) -> p b c", b=nb),
                         t["ctx_768"][b:b + nb].rearrange("b j c -> j b c"))]
            if ch[0] == "w2":
                _, s, ns = ch
                return [(buf[:, 0:ns * D].rearrange("p (s c) -> p s c", s=ns),
                         t["ff_w2"][s * P:(s + ns) * P, :].rearrange("(s p) c -> p s c", p=P))]
            _, name, c0, cw, _, _ = ch
            w = t[name]
            full = slices(w.shape[0]) - 1
            b3 = buf[:, 0:(full + 1) * cw].rearrange("p (s c) -> p s c", s=full + 1)
            tail = w[full * P:full * P + 64, c0:c0 + cw]
            return [(b3[:, 0:full, :], w[0:full * P, c0:c0 + cw].rearrange("(s p) c -> p s c", p=P)),
                    (b3[0:64, full, :], tail), (b3[64:P, full, :], tail)]

        stage_value, counts = [], [0] * NSTAGE
        for n in range(len(CHUNKS)):
            counts[n % NSTAGE] += 16 * len(chunk_dmas(n))
            stage_value.append(counts[n % NSTAGE])

        C_QK, C_V, C_Q2, C_W1 = 0, 5, 8, 11
        def c_places(n):
            _, name, c0, cw, _, _ = CHUNKS[n]
            if name == "q1":
                return [(0, 128, 0, C_QK), (128, 256, 0, C_QK + 1), (256, 320, 0, C_QK + 2)]
            if name == "k1":
                return [(0, 64, 64, C_QK + 2), (64, 192, 0, C_QK + 3), (192, 320, 0, C_QK + 4)]
            if name in ("v1", "q2"):
                c = C_V if name == "v1" else C_Q2
                return [(0, 128, 0, c), (128, 256, 0, c + 1), (256, 320, 0, c + 2)]
            return [(0, 128, 0, C_W1 + c0 // P), (128, 256, 0, C_W1 + c0 // P + 1)]

        NVEC_LOADS = 2 + 4 + 18 + 1 + 3
        PRO_DONE = 2

        MXCOL, MXGROUPS, col = {}, [], 0
        for scale in (S_QKV, S_Q2, S_W1, S_KV2, S_CTX, S_O1, S_O2):
            first = col
            for n in range(N1):
                if (scale == S_CTX) if CHUNKS[n][0] == "ctx" else (CHUNKS[n][5] == scale):
                    MXCOL[n], col = col, col + 1
            if scale in (S_QKV, S_Q2):
                MXCOL["qk" if scale == S_QKV else "q2"], col = col, col + 1
            MXGROUPS.append((first, col))

        MAX_AT = {1: (0, 1), 2: (2, 3), 3: (4, 5), 4: (6, 7), 5: (8,), 6: (9,)}
        MAX2_AT = {7: (0, 1), 8: (2, 3)}
        MT_AT, MT2_AT = 7, 9
        XHAT = [(0, 0, tr_done[0], 1), (1, 1, tr_done[1], 1), (2, 2, tr_done[2], 1)]

        block = ctx.enter_context(nc.Block())

        @block.sync
        def _(sp):
            loads = [(ident[:], t["c_ident"]), (sel_f, t["c_sel"]),
                     (k4[63:64, :, :].rearrange("p a b -> p (a b)"), t["c_aug"][0:1, 0:NT * N]),
                     (k4[127:128, :, :].rearrange("p a b -> p (a b)"), t["c_aug"][0:1, 0:NT * N]),
                     (k42[63:64, :, :].rearrange("p a b -> p (a b)"), t["c_aug"][0:1, 0:NT * J]),
                     (k42[127:128, :, :].rearrange("p a b -> p (a b)"), t["c_aug"][0:1, 0:NT * J])]
            for j, nm in enumerate(("n1_g", "n1_b", "n2_g", "n2_b", "n3_g", "n3_b")):
                v = t[nm]
                loads += [(gb[:, j, 0:2], v[0:2 * P].rearrange("(s p) -> p s", p=P))]
                for r in (0, 64):
                    loads += [(gb[r:r + 64, j, 2:3], v[2 * P:D].rearrange("(p o) -> p o", o=1))]
            loads += [(b1c[:, :], t["ff_b1"].rearrange("(s p) -> p s", p=P))]
            for dst, nm in ((bias1, "o1_b"), (bias2, "o2_b"), (bias3, "ff_b2")):
                loads += [(dst[:, :], t[nm].partition_broadcast(P))]
            sp.wait_ge(pro.sem, pro.at(0, 1))
            for dst, src in loads:
                sp.dma_start(dst, src, allow_slow_non_contiguous=True).then_inc(vec_loaded.sem, 16)
            for n in range(len(CHUNKS)):
                if n >= NSTAGE:
                    sp.wait_ge(stage_used.sem, stage_used.at(0, n - NSTAGE + 1))
                for dst, src in chunk_dmas(n):
                    sp.dma_start(dst, src).then_inc(staged[n % NSTAGE].sem, 16)
            assert len(loads) == NVEC_LOADS

            def load_x(e):
                sp.wait_ge(ln_done[0].sem, ln_done[0].at(e - 1))
                sp.wait_ge(xb_done[0].sem, xb_done[0].at(e - 1))
                sp.dma_start(x_in[:], t["x"][e].rearrange("(s p) c -> p s c", p=P)).then_inc(x_loaded.sem, 16)

            def load_ctx(e):
                sp.wait_ge(ct_done.sem, ct_done.at(e - 1))
                sp.dma_start(c_in[:, 0:CTX], t["ctx_768"][e]).then_inc(c_loaded.sem, 16)
                sp.dma_start(c_in[:, CTX:2 * P], t["ctx_768"][e, :, P:CTX]).then_inc(c_loaded.sem, 16)

            def spread_qk(e):
                sp.wait_ge(qk_lo.sem, qk_lo.at(e))
                sp.wait_ge(max_done.sem, max_done.at(e - 1))
                sp.wait_ge(st_done[0].sem, st_done[0].at(e - 1))
                for r in range(4):
                    nt = 3 if r < 2 else 2
                    for part, src in enumerate((qk_h, qk_h, qk_l)):
                        sp.dma_start(q4[part:P:4, r:r + 4 * (nt - 1) + 1:4, :],
                                     src[32 * r:32 * r + 32, 0:nt, :]).then_inc(spread[r].sem, 16)
                    kb = (r + 2) % 4
                    t0 = 3 if kb < 2 else 2
                    for part, src in enumerate((qk_h, qk_l, qk_h)):
                        sp.dma_start(k4[part:P:4, r:r + 4 * (4 - t0) + 1:4, :],
                                     src[32 * kb:32 * kb + 32, t0:5, :]).then_inc(spread[r].sem, 16)

            def spread_q2(e):
                sp.wait_ge(q2_lo.sem, q2_lo.at(e))
                sp.wait_ge(st_done[1].sem, st_done[1].at(e - 1))
                for r in range(4):
                    nt = 3 if r < 2 else 2
                    for part, src in enumerate((q2_h, q2_h, q2_l)):
                        sp.dma_start(q42[part:P:4, r:r + 4 * (nt - 1) + 1:4, :],
                                     src[32 * r:32 * r + 32, 0:nt, :]).then_inc(q2_spread.sem, 16)

            def spread_k2(e):
                sp.wait_ge(k2_lo.sem, k2_lo.at(e))
                sp.wait_ge(st_done[1].sem, st_done[1].at(e - 1))
                for r in range(4):
                    nt = 3 if r < 2 else 2
                    for part, src in enumerate((k2_h, k2_l, k2_h)):
                        sp.dma_start(k42[part:P:4, r:r + 4 * (nt - 1) + 1:4, :],
                                     src[32 * r:32 * r + 32, 0:nt, :]).then_inc(k2_spread.sem, 16)

            def spread_max(a, e):
                sp.wait_ge(mt_row[a].sem, mt_row[a].at(e))
                for h in range(2):
                    sp.dma_start((q4, q42)[a][64 * h + 63:64 * h + 64, :, :],
                                 m_row[a][NT * h:NT * h + NT, :]).then_inc(m_spread[a].sem, 16)

            def spread_out(a, e):
                sp.wait_ge(o_copied[a].sem, o_copied[a].at(e))
                sp.wait_ge(rec_done[a].sem, rec_done[a].at(e - 1))
                sp.wait_ge(o_lo[a].sem, o_lo[a].at(e - 1))
                sp.dma_start(den[a][:, :], o_raw[a][1:P:32, :, :]).then_inc(den_spread[a].sem, 16)
                sp.dma_start(o_c[a][0:64, 0:3, :], o_raw[a][0:P:2, 0:NG:2, :]).then_inc(o_spread[a].sem, 16)
                sp.dma_start(o_c[a][64:P, 0:2, :], o_raw[a][0:P:2, 1:NG:2, :]).then_inc(o_spread[a].sem, 16)
                sp.dma_start(o_c[a][64:P, 2, :], o_raw[a][0:P:2, NG - 1, :]).then_inc(o_spread[a].sem, 16)

            def store_out(e):
                sp.wait_ge(out_ready.sem, out_ready.at(e))
                sp.dma_start(out[e].rearrange("(s p) c -> p s c", p=P), out_sb[:]).then_inc(out_stored.sem, 16)

            def step(i):
                on = streams_of(i)
                if 0 in on:
                    load_x(i + 1)
                if 1 in on:
                    load_ctx(i)
                    spread_out(0, i)
                if 2 in on:
                    spread_out(1, i - 1)
                if 0 in on:
                    spread_qk(i + 1)
                if 1 in on:
                    spread_k2(i)
                    spread_q2(i)
                if 0 in on:
                    spread_max(0, i + 1)
                if 1 in on:
                    spread_max(1, i)
                if 2 in on:
                    store_out(i - 1)

            run_steps(sp, step)
            sp.wait_ge(out_stored.sem, out_stored.at(B - 1))

        @block.gpsimd
        def _(pool):
            nc.gpsimd.memset(halfneg[:], -0.5).then_inc(pro_act.sem, 1)
            pool.wait_ge(vec_loaded.sem, 16 * NVEC_LOADS)
            pool.wait_ge(pro_act.sem, pro_act.at(0, 1))

            def rstd(k, e):
                pool.wait_ge(ln_stat[k].sem, ln_stat[k].at(e))
                nc.gpsimd.tensor_tensor(rs[k][:], ve[k][:], halfneg[:], ALU.pow).then_inc(ln_rstd[k].sem, 1)

            def add_bias(k, e):
                src, dst, bias = ((x_in, xb1, bias1), (x1, xb2, bias2), (x2, xb3, bias3))[k]
                if k == 0:
                    pool.wait_ge(x_loaded.sem, x_loaded.at(e))
                else:
                    pool.wait_ge(resid[k - 1].sem, resid[k - 1].at(e))
                if k < 2:
                    pool.wait_ge(resid[k].sem, resid[k].at(e - 1))
                else:
                    pool.wait_ge(out_ready.sem, out_ready.at(e - 1))
                nc.gpsimd.tensor_tensor(dst[:], src[:], bias[:].unsqueeze(1).to_broadcast([P, KT, D]),
                                        ALU.add).then_inc(xb_done[k].sem, 1)

            def out_lo(a, e):
                pool.wait_ge(o_hi[a].sem, o_hi[a].at(e))
                pool.wait_ge(oproj_done[a].sem, oproj_done[a].at(e - 1))
                nc.gpsimd.tensor_tensor(o_l[a][:], o_c[a][:, 0:2], o_h[a][:, 0:2],
                                        ALU.subtract).then_inc(o_lo[a].sem, 1)
                pool.wait_ge(o_lo[a].sem, o_lo[a].at(e, 1))
                nc.gpsimd.tensor_tensor(o_h[a][64:P, 2], o_c[a][64:P, 2], o_h[a][64:P, 2],
                                        ALU.subtract).then_inc(o_lo[a].sem, 1)

            def ff_lo(m, e):
                pool.wait_ge(ffh_done.sem, ffh_done.at(e, m + 1))
                if m >= 2:
                    pool.wait_ge(ff2_step.sem, ff2_step.at(e, m - 1))
                else:
                    pool.wait_ge(ff2_step.sem, ff2_step.at(e - 1, NM - 1 + m))
                nc.gpsimd.tensor_tensor(ff_l[:, m % 2], ff_p[:, m % 2], ff_h[:, m % 2].bitcast(f32),
                                        ALU.subtract).then_inc(ffl_done.sem, 1)

            def step(i):
                on = streams_of(i)
                if 0 in on:
                    rstd(0, i + 1)
                if 1 in on:
                    out_lo(0, i)
                    rstd(1, i)
                if 0 in on:
                    add_bias(0, i + 1)
                if 2 in on:
                    out_lo(1, i - 1)
                    rstd(2, i - 1)
                    add_bias(2, i - 1)
                if 1 in on:
                    add_bias(1, i)
                if 2 in on:
                    for m in range(NM):
                        ff_lo(m, i - 1)

            pool.wait_ge(pro.sem, pro.at(0, PRO_DONE))
            run_steps(pool, step)

        @block.scalar
        def _(act):
            for n in range(N1, len(CHUNKS)):
                ch = CHUNKS[n]
                act.wait_ge(c_product.sem, c_product.at(0, n - N1 + 1))
                if ch[0] == "cut":
                    _, name, c0, cw, _, _ = ch
                    wh, _, off = DEST[name]
                    ns = slices(t[name].shape[0])
                    nc.scalar.activation(wh[:, 0:ns, off + c0:off + c0 + cw],
                                         tmp[:, 0:ns * cw].rearrange("p (s c) -> p s c", s=ns),
                                         ACT.Copy).then_inc(pro_hi.sem, 1)
                else:
                    _, s, ns = ch
                    nc.scalar.activation(w2_h[:, s:s + ns, :],
                                         tmp[:, 0:ns * D].rearrange("p (s c) -> p s c", s=ns),
                                         ACT.Copy).then_inc(pro_hi.sem, 1)
            act.wait_ge(pro.sem, pro.at(0, PRO_DONE))

            def tr_hi_part(k, e, s):
                act.wait_ge(tr_done[k].sem, tr_done[k].at(e))
                if k == 0:
                    act.wait_ge(v_done.sem, v_done.at(e - 1))
                elif k == 1:
                    act.wait_ge(q2_done.sem, q2_done.at(e - 1))
                else:
                    act.wait_ge(ff1_done.sem, ff1_done.at(e - 1))
                nc.scalar.activation(ah[k][:].rearrange("p a b -> p (a b)"), flat[s][:, 0:3 * N],
                                     ACT.Copy).then_inc(tr_hi[k].sem, 1)

            def qk_hi_part(c, e, s):
                act.wait_ge(qk_done.sem, qk_done.at(e, c + 1))
                if c == 0:
                    for r in range(4):
                        act.wait_ge(spread[r].sem, spread[r].at(e - 1))
                for m in range(4 * c, min(4 * c + 4, 5)):
                    last = nc.scalar.activation(qk_h[:, m, :], flat[s][:, (m - 4 * c) * N:(m - 4 * c + 1) * N],
                                                ACT.Identity, bias=cvec[:, C_QK + m:C_QK + m + 1])
                last.then_inc(qk_hi.sem, 1)

            def v_copy(e, s):
                act.wait_ge(v_done.sem, v_done.at(e))
                act.wait_ge(pv_done[0].sem, pv_done[0].at(e - 1))
                nc.scalar.activation(v1[:, :, :, 0:2 * DH:2],
                                     slot[s][:, :, 0:D].rearrange("p k (h d) -> p k h d", d=DH),
                                     ACT.Copy).then_inc(v_copied.sem, 1)

            def q2_hi_part(e, s):
                act.wait_ge(q2_done.sem, q2_done.at(e))
                act.wait_ge(q2_spread.sem, q2_spread.at(e - 1))
                for m in range(3):
                    r = P if m < 2 else 64
                    last = nc.scalar.activation(q2_h[0:r, m, :], flat[s][0:r, m * N:(m + 1) * N],
                                                ACT.Identity, bias=cvec[0:r, C_Q2 + m:C_Q2 + m + 1])
                last.then_inc(q2_hi.sem, 1)

            def ct_hi_part(e, s):
                act.wait_ge(ct_done.sem, ct_done.at(e))
                act.wait_ge(kv2_done.sem, kv2_done.at(e - 1))
                nc.scalar.activation(ct_h[:].rearrange("p a b -> p (a b)"), flat[s][:, 0:2 * J],
                                     ACT.Copy, scale=sc[:, S_CTX:S_CTX + 1]).then_inc(ct_hi.sem, 1)

            def k2_hi_part(e, s):
                act.wait_ge(kv2_done.sem, kv2_done.at(e))
                act.wait_ge(k2_spread.sem, k2_spread.at(e - 1))
                nc.scalar.activation(k2_h[:, 0:2, :].rearrange("p a b -> p (a b)"), flat[s][:, 0:2 * J], ACT.Copy)
                nc.scalar.activation(k2_h[0:64, 2, :], flat[s][0:64, 2 * J:3 * J],
                                     ACT.Copy).then_inc(k2_hi.sem, 1)

            def max_row(a, e, s):
                act.wait_ge(mt_done[a].sem, mt_done[a].at(e))
                act.wait_ge(m_spread[a].sem, m_spread[a].at(e - 1))
                nc.scalar.activation(m_row[a][:], flat[s][0:H, 0:N], ACT.Copy,
                                     scale=1.0 / AUG).then_inc(mt_row[a].sem, 1)

            def exps(a, n, e, i, s, ptab):
                act.wait_ge(st_done[a].sem, st_done[a].at(e, n + 1))
                b, prior = ptab[a, n]
                if prior:
                    freed, step_offset, count = prior
                    act.wait_ge(freed.sem, freed.at(i + step_offset, count))
                rows = P if a == 0 else J
                nc.scalar.activation(probs[0:rows, b, :], flat[s][0:rows, :], ACT.Exp,
                                     scale=sc[0:rows, E1 + a:E1 + a + 1]).then_inc(exp_done[a].sem, 1)

            def out_copy(a, g, e):
                act.wait_ge(pv_done[a].sem, pv_done[a].at(e, g + 1))
                if g == 0:
                    act.wait_ge(o_spread[a].sem, o_spread[a].at(e - 1))
                    act.wait_ge(den_spread[a].sem, den_spread[a].at(e - 1))
                nc.scalar.activation(o_raw[a][:, g, :], ps_pv[:, 0:N], ACT.Copy).then_inc(o_copied[a].sem, 1)

            def rec_hi_part(a, e):
                act.wait_ge(rec_done[a].sem, rec_done[a].at(e))
                act.wait_ge(rb_done[a].sem, rb_done[a].at(e - 1))
                nc.scalar.activation(rec_h[a][:], rec[a][:], ACT.Copy).then_inc(rec_hi[a].sem, 1)

            def out_hi_part(a, e):
                act.wait_ge(o_norm[a].sem, o_norm[a].at(e))
                act.wait_ge(oproj_done[a].sem, oproj_done[a].at(e - 1))
                nc.scalar.activation(o_h[a][:].rearrange("p a b -> p (a b)"),
                                     o_c[a][:].rearrange("p a b -> p (a b)"), ACT.Copy).then_inc(o_hi[a].sem, 1)

            def gelu(m, e):
                act.wait_ge(ff1_done.sem, ff1_done.at(e, m + 1))
                if m >= 2:
                    act.wait_ge(ffp_done.sem, ffp_done.at(e, m - 1))
                else:
                    act.wait_ge(ffp_done.sem, ffp_done.at(e - 1, NM - 1 + m))
                nc.scalar.activation(ff_g[:, m % 2], ps_f1[:, N:2 * N], ACT.Gelu, scale=sc[:, D3:D3 + 1],
                                     bias=cvec[:, C_W1 + NM + m:C_W1 + NM + m + 1]).then_inc(gelu_done.sem, 1)

            def ff_hi(m, e):
                act.wait_ge(ffp_done.sem, ffp_done.at(e, m + 1))
                if m >= 2:
                    act.wait_ge(ff2_step.sem, ff2_step.at(e, m - 1))
                else:
                    act.wait_ge(ff2_step.sem, ff2_step.at(e - 1, NM - 1 + m))
                nc.scalar.activation(ff_h[:, m % 2], ff_p[:, m % 2], ACT.Copy).then_inc(ffh_done.sem, 1)

            def step(i):
                on, tab = streams_of(i), ring(streams_of(i), before_of(i))
                ptab = probs_ring(streams_of(i), before_of(i))
                if 1 in on:
                    for T in range(NT):
                        exps(0, T, i, i, tab["st", T][0], ptab)
                        if T % 2 and T > 1:
                            out_copy(0, T // 2 - 1, i)
                    if 2 not in on:
                        out_copy(0, NG - 1, i)
                if 2 in on:
                    for g in range(NG):
                        exps(1, g, i - 1, i, tab["st2", g][0], ptab)
                        if g == 0 and 1 in on:
                            out_copy(0, NG - 1, i)
                        if g >= 1:
                            out_copy(1, g - 1, i - 1)
                    out_copy(1, NG - 1, i - 1)
                if 0 in on:
                    tr_hi_part(0, i + 1, tab["tr", 0][0])
                if 1 in on:
                    rec_hi_part(0, i)
                if 0 in on:
                    qk_hi_part(0, i + 1, tab["qk", 0][0])
                    qk_hi_part(1, i + 1, tab["qk", 1][0])
                if 1 in on:
                    out_hi_part(0, i)
                if 0 in on:
                    v_copy(i + 1, tab["v", 0][0])
                if 2 in on:
                    rec_hi_part(1, i - 1)
                if 1 in on:
                    ct_hi_part(i, tab["ct", 0][0])
                if 2 in on:
                    out_hi_part(1, i - 1)
                if 1 in on:
                    k2_hi_part(i, tab["kv2", 0][0])
                    tr_hi_part(1, i, tab["tr", 1][0])
                    q2_hi_part(i, tab["q2", 0][0])
                if 2 in on:
                    tr_hi_part(2, i - 1, tab["tr", 2][0])
                    for m in range(NM):
                        gelu(m, i - 1)
                        ff_hi(m, i - 1)
                        if m == MT_AT and 0 in on:
                            max_row(0, i + 1, tab["mt", 0][0])
                elif 0 in on:
                    max_row(0, i + 1, tab["mt", 0][0])
                if 1 in on:
                    max_row(1, i, tab["mt", 1][0])

            run_steps(act, step)

        @block.tensor
        def _(pe):
            mm = nc.tensor.matmul
            pe.wait_ge(vec_loaded.sem, 16 * NVEC_LOADS)
            for n in range(len(CTXCH), len(CTXCH) + LNMATS):
                _, _, _, cw, ln, _ = CHUNKS[n]
                pe.wait_ge(staged[n % NSTAGE].sem, staged[n % NSTAGE].at(0, stage_value[n]))
                w = stage_buf(n)[:, 0:3 * cw].rearrange("p (s c) -> p s c", s=3)
                for c0, c1, r0, col in c_places(n):
                    for s in range(3):
                        k = P if s < 2 else 64
                        last = mm(ps[r0:r0 + c1 - c0, 0, col:col + 1], w[0:k, s, c0:c1],
                                  gb[0:k, 2 * ln + 1, s:s + 1], start=(s == 0), stop=(s == 2))
                last.then_inc(pro_pe.sem, 1)
            pe.wait_ge(staged[(N1 - 1) % NSTAGE].sem, staged[(N1 - 1) % NSTAGE].at(0, stage_value[N1 - 1]))
            pe.wait_ge(cv_ready.sem, cv_ready.at(0))
            w = stage_buf(N1 - 1).rearrange("p (s c) -> p s c", s=3)
            for s in range(3):
                k = P if s < 2 else 64
                last = mm(ps[:, 1, 0:D], cv_rep[0:k, s, :], w[0:k, s, :], start=(s == 0), stop=(s == 2))
            last.then_inc(pro_pe.sem, 1)
            pe.wait_ge(maxima.sem, maxima.at(0, 1))
            mm(ps[0:8, 2, 0:P], mxm[:], ident[:], start=True, stop=True).then_inc(pro_pe.sem, 1)
            pe.wait_ge(maxima.sem, maxima.at(0, 2))
            mm(ps[:, 3, 0:8], ones[:], mxd[:], start=True, stop=True).then_inc(pro_pe.sem, 1)
            pe.wait_ge(pro.sem, pro.at(0, PRO_DONE))

            def take(tab, name, i):
                s, prior = tab[name]
                if prior:
                    freed, step_offset, count = prior
                    pe.wait_ge(freed.sem, freed.at(i + step_offset, count))
                return s

            def transposes(k, e, s):
                pe.wait_ge(ln_done[k].sem, ln_done[k].at(e))
                for c in range(3):
                    for q in range(KT):
                        last = nc.tensor.transpose(flat[s][:, c * N + q * P:c * N + (q + 1) * P],
                                                   xhat[:, q, c * P:(c + 1) * P], ident[:])
                last.then_inc(tr_done[k].sem, 1)

            def product(dst, pairs):
                for n, (lhs, rhs) in enumerate(pairs):
                    last = mm(dst, lhs, rhs, start=(n == 0), stop=(n == len(pairs) - 1))
                return last

            def by_feature(dst, wh, wl, c0, c1, xh, xl, full=2):
                pairs = split_passes(xh, xl, wh[:, :, c0:c1], wl[:, :, c0:c1], full)
                return product(dst, [(w, x) for x, w in pairs])

            def by_token(dst, wh, wl, c0, c1, xh, xl, full=2):
                return product(dst, split_passes(xh, xl, wh[:, :, c0:c1], wl[:, :, c0:c1], full))

            def qk(c, e, s):
                if c == 0:
                    pe.wait_ge(tr_lo[0].sem, tr_lo[0].at(e))
                for m in range(4 * c, min(4 * c + 4, 5)):
                    last = by_feature(flat[s][:, (m - 4 * c) * N:(m - 4 * c + 1) * N], wqkv_h, wqkv_l,
                                      m * P, (m + 1) * P, ah[0], al[0])
                last.then_inc(qk_done.sem, 1)

            def values(e, s):
                for q in range(KT):
                    last = by_token(slot[s][:, q, 0:D], wqkv_h, wqkv_l, 2 * D, 3 * D,
                                    ah[0][:, :, q * P:(q + 1) * P], al[0][:, :, q * P:(q + 1) * P])
                last.then_inc(v_done.sem, 1)

            def maxima1(n, e, s):
                T = MAX_ORDER[n]
                pe.wait_ge(spread[T % 4].sem, spread[T % 4].at(e))
                for h in range(2):
                    for q in range(KT):
                        last = mm(flat[s][:, (2 * h + q) * N:(2 * h + q + 1) * N],
                                  q4[64 * h:64 * h + 63, T, q * P:(q + 1) * P],
                                  k4[64 * h:64 * h + 63, T, :], start=True, stop=True)
                last.then_inc(max_done.sem, 1)

            def maxima2(n, e, s):
                T0, nt = MAX2_PAIRS[n]
                if n == 0:
                    pe.wait_ge(q2_spread.sem, q2_spread.at(e))
                    pe.wait_ge(k2_spread.sem, k2_spread.at(e))
                for h in range(2):
                    for T in range(T0, T0 + nt):
                        for q in range(KT):
                            c = ((T - T0) * KT + q) * J
                            last = mm(slot[s][:, h, c:c + J], q42[64 * h:64 * h + 63, T, q * P:(q + 1) * P],
                                      k42[64 * h:64 * h + 63, T, :], start=True, stop=True)
                last.then_inc(max2_done.sem, 1)

            def max_turn(a, e, s):
                reduced = (max_red, max2_red)[a]
                pe.wait_ge(reduced.sem, reduced.at(e))
                for q in range(KT):
                    last = mm(flat[s][0:H, q * P:(q + 1) * P],
                              m_q[a][:, :, :, q].rearrange("p h t -> p (h t)"), ident[:], start=True, stop=True)
                last.then_inc(mt_done[a].sem, 1)

            def scores1(T, e, s):
                if T == 0:
                    pe.wait_ge(m_spread[0].sem, m_spread[0].at(e))
                for h in range(2):
                    for k in range(KT):
                        last = mm(flat[s][:, (2 * h + k) * N:(2 * h + k + 1) * N],
                                  k4[64 * h:64 * h + 64, T, k * P:(k + 1) * P],
                                  q4[64 * h:64 * h + 64, T, :], start=True, stop=True)
                last.then_inc(st_done[0].sem, 1)

            def scores2(g, e, s):
                if g == 0:
                    pe.wait_ge(m_spread[1].sem, m_spread[1].at(e))
                for h in range(2):
                    for u in range(2):
                        last = mm(slot[s][0:J, h, u * N:(u + 1) * N],
                                  k42[64 * h:64 * h + 64, 2 * g + u, :],
                                  q42[64 * h:64 * h + 64, 2 * g + u, :], start=True, stop=True)
                last.then_inc(st_done[1].sem, 1)

            def pv_free(a, g, e, i, on):
                if g:
                    pe.wait_ge(o_copied[a].sem, o_copied[a].at(e, g))
                elif a == 1 and 1 in on:
                    pe.wait_ge(o_copied[0].sem, o_copied[0].at(i))
                elif a == 0 and 2 in before_of(i):
                    pe.wait_ge(o_copied[1].sem, o_copied[1].at(i - 2))
                elif a == 0:
                    pe.wait_ge(o_copied[0].sem, o_copied[0].at(i - 1))
                else:
                    pe.wait_ge(o_copied[1].sem, o_copied[1].at(i - 2))

            def values1(g, e, i, on, ptab):
                pe.wait_ge(exp_done[0].sem, exp_done[0].at(e, 2 * g + 2))
                if g == 0:
                    pe.wait_ge(v_copied.sem, v_copied.at(e))
                pv_free(0, g, e, i, on)
                for k in range(KT):
                    for r in range(4):
                        T, h = 2 * g + r // 2, r % 2
                        last = mm(ps_pv[32 * r:32 * r + 32, 0:N], v1[:, k, 4 * g + r, :],
                                  probs[:, ptab[0, T][0], (2 * h + k) * N:(2 * h + k + 1) * N],
                                  start=(k == 0), stop=(k == KT - 1), tile_position=(0, 32 * r))
                last.then_inc(pv_done[0].sem, 1)

            def values2(g, e, i, on, ptab):
                pe.wait_ge(exp_done[1].sem, exp_done[1].at(e, g + 1))
                if g == 0:
                    pe.wait_ge(v2_copied.sem, v2_copied.at(e))
                pv_free(1, g, e, i, on)
                for r in range(4):
                    u, h = r // 2, r % 2
                    last = mm(ps_pv[32 * r:32 * r + 32, 0:N], v2[:, 4 * g + r, :],
                              probs[0:J, ptab[1, g][0], (2 * h + u) * N:(2 * h + u + 1) * N],
                              start=True, stop=True, tile_position=(0, 32 * r))
                last.then_inc(pv_done[1].sem, 1)

            def spread_rec(a, e, s):
                pe.wait_ge(rec_lo[a].sem, rec_lo[a].at(e))
                for c in range(3):
                    last = product(flat[s][:, c * N:(c + 1) * N],
                                   [(sel[:, c * P:(c + 1) * P], rec_h[a][:]), (sel[:, c * P:(c + 1) * P], rec_l[a][:])])
                last.then_inc(rb_done[a].sem, 1)

            def out_proj(a, e, s):
                pe.wait_ge(o_lo[a].sem, o_lo[a].at(e))
                wh, wl = ((wo1_h, wo1_l), (wo2_h, wo2_l))[a]
                for q in range(KT):
                    last = by_token(slot[s][:, q, 0:D], wh, wl, 0, D,
                                    o_h[a][:, :, q * P:(q + 1) * P], o_l[a][:, :, q * P:(q + 1) * P])
                last.then_inc(oproj_done[a].sem, 1)

            def ctx_turn(e, s):
                pe.wait_ge(c_loaded.sem, c_loaded.at(e))
                for c in range(2):
                    last = nc.tensor.transpose(flat[s][:, c * J:(c + 1) * J], c_in[:, c * P:(c + 1) * P],
                                               ident[0:J, 0:J])
                last.then_inc(ct_done.sem, 1)

            def kv2(e, s):
                pe.wait_ge(ct_lo.sem, ct_lo.at(e))
                for m in range(3):
                    c0, c1 = m * P, min((m + 1) * P, D)
                    by_feature(flat[s][0:c1 - c0, m * J:(m + 1) * J], wkv2_h, wkv2_l, c0, c1, ct_h, ct_l, 1)
                by_token(slot[s][0:J, 1, 0:D], wkv2_h, wkv2_l, D, 2 * D, ct_h, ct_l, 1).then_inc(kv2_done.sem, 1)

            def q2(e, s):
                pe.wait_ge(tr_lo[1].sem, tr_lo[1].at(e))
                for m in range(3):
                    c0, c1 = m * P, min((m + 1) * P, D)
                    last = by_feature(flat[s][0:c1 - c0, m * N:(m + 1) * N], wq2_h, wq2_l, c0, c1, ah[1], al[1])
                last.then_inc(q2_done.sem, 1)

            def ff1(m, e):
                if m == 0:
                    pe.wait_ge(tr_lo[2].sem, tr_lo[2].at(e))
                    pe.wait_ge(ffp_done.sem, ffp_done.at(e - 1))
                else:
                    pe.wait_ge(ffp_done.sem, ffp_done.at(e, m))
                by_feature(ps_f1[:, 0:N], w1_h, w1_l, m * P, (m + 1) * P, ah[2], al[2])
                by_feature(ps_f1[:, N:2 * N], w1_h, w1_l, FF + m * P, FF + (m + 1) * P,
                           ah[2], al[2]).then_inc(ff1_done.sem, 1)

            def ff2(m, e):
                if m == 0:
                    pe.wait_ge(out_ready.sem, out_ready.at(e - 1))
                pe.wait_ge(ffl_done.sem, ffl_done.at(e, m + 1))
                for q in range(KT):
                    xh, xl = ff_h[:, m % 2, q * P:(q + 1) * P], ff_l[:, m % 2, q * P:(q + 1) * P]
                    pairs = [(xh, w2_h[:, m, :]), (xl, w2_h[:, m, :]), (xh, w2_l[:, m, :])]
                    for n, (lhs, rhs) in enumerate(pairs):
                        last = mm(ps_f2[q][:, 0:D], lhs, rhs, start=(m == 0 and n == 0), stop=(m == NM - 1 and n == 2))
                last.then_inc(ff2_step.sem, 1)

            def step(i):
                on, tab = streams_of(i), ring(streams_of(i), before_of(i))
                ptab = probs_ring(streams_of(i), before_of(i))
                if 1 in on:
                    for T in range(NT):
                        scores1(T, i, take(tab, ("st", T), i))
                        if T % 2 and T > 1:
                            values1(T // 2 - 1, i, i, on, ptab)
                if 2 in on:
                    for g in range(NG):
                        scores2(g, i - 1, take(tab, ("st2", g), i))
                        if g == 0 and 1 in on:
                            values1(NG - 1, i, i, on, ptab)
                        if g >= 1:
                            values2(g - 1, i - 1, i, on, ptab)
                    values2(NG - 1, i - 1, i, on, ptab)
                elif 1 in on:
                    values1(NG - 1, i, i, on, ptab)
                if 0 in on:
                    transposes(0, i + 1, take(tab, ("tr", 0), i))
                    qk(0, i + 1, take(tab, ("qk", 0), i))
                    qk(1, i + 1, take(tab, ("qk", 1), i))
                if 1 in on:
                    spread_rec(0, i, take(tab, ("rb", 0), i))
                if 0 in on:
                    values(i + 1, take(tab, ("v", 0), i))
                if 1 in on:
                    out_proj(0, i, take(tab, ("oproj", 0), i))
                    ctx_turn(i, take(tab, ("ct", 0), i))
                if 2 in on:
                    spread_rec(1, i - 1, take(tab, ("rb", 1), i))
                if 1 in on:
                    kv2(i, take(tab, ("kv2", 0), i))
                if 2 in on:
                    out_proj(1, i - 1, take(tab, ("oproj", 1), i))
                if 1 in on:
                    transposes(1, i, take(tab, ("tr", 1), i))
                    q2(i, take(tab, ("q2", 0), i))
                if 2 in on:
                    transposes(2, i - 1, take(tab, ("tr", 2), i))
                for m in range(NM + 1):
                    if 2 in on and m < NM:
                        ff1(m, i - 1)
                    if 2 in on and m > 0:
                        ff2(m - 1, i - 1)
                    if 0 in on:
                        for n in MAX_AT.get(m, ()):
                            maxima1(n, i + 1, take(tab, ("max", n), i))
                        if m == MT_AT:
                            max_turn(0, i + 1, take(tab, ("mt", 0), i))
                    if 1 in on:
                        for n in MAX2_AT.get(m, ()):
                            maxima2(n, i, take(tab, ("max2", n), i))
                        if m == MT2_AT:
                            max_turn(1, i, take(tab, ("mt", 1), i))

            run_steps(pe, step)

        @block.vector
        def _(dve):
            V = nc.vector
            chained = [0]

            def link(ins):
                chained[0] += 1
                ins.then_inc(pro_dve.sem, 1)
                dve.wait_ge(pro_dve.sem, pro_dve.at(0, chained[0]))

            for tile_, value in ((q4, 0.0), (k4, 0.0), (q42, 0.0), (k42, 0.0), (v1, 1.0), (v2, 1.0),
                                 (ones, 1.0), (mx, 0.0), (mxm, 0.0), (cvec, 0.0)):
                last = V.memset(tile_[:], value)
            link(last)
            V.memset(sc[:], 0.0).then_inc(pro.sem, 1)
            dve.wait_ge(pro.sem, pro.at(0, 1))
            dve.wait_ge(vec_loaded.sem, 16 * NVEC_LOADS)
            V.tensor_copy(sel[:], sel_f)
            for n in range(N1):
                ch = CHUNKS[n]
                dve.wait_ge(staged[n % NSTAGE].sem, staged[n % NSTAGE].at(0, stage_value[n]))
                if ch[0] == "ctx":
                    V.tensor_reduce(mx[0:J, MXCOL[n]:MXCOL[n] + 1], stage_buf(n)[0:J, 0:ch[2] * CTX], AX.X, ALU.max,
                                    apply_absolute_value=True).then_inc(stage_used.sem, 1)
                    continue
                _, name, c0, cw, ln, _ = ch
                ns = slices(t[name].shape[0])
                src = stage_buf(n)[:, 0:ns * cw]
                if ln is not None:
                    dve.wait_ge(stage_used.sem, stage_used.at(0, n))
                    for s in range(ns):
                        last = V.tensor_scalar(tmp[:, s * cw:(s + 1) * cw], src[:, s * cw:(s + 1) * cw],
                                               gb[:, 2 * ln, s:s + 1], None, ALU.mult)
                    link(last)
                    src = tmp[:, 0:ns * cw]
                    dve.wait_ge(pro_pe.sem, pro_pe.at(0, n - len(CTXCH) + 1))
                if n == N1 - 1:
                    dve.wait_ge(pro_pe.sem, pro_pe.at(0, LNMATS + 1))
                red = V.tensor_reduce(mx[:, MXCOL[n]:MXCOL[n] + 1], src, AX.X, ALU.max, apply_absolute_value=True)
                red.then_inc(stage_used.sem, 1)
                if n == len(CTXCH) + LNMATS - 1:
                    V.tensor_copy(cvec[:, 0:C_V + 2], ps[:, 0, 0:C_V + 2])
                    V.tensor_copy(cvec[0:64, C_V + 2:C_V + 3], ps[0:64, 0, C_V + 2:C_V + 3])
                    V.tensor_copy(cvec[:, C_Q2:C_Q2 + 2], ps[:, 0, C_Q2:C_Q2 + 2])
                    V.tensor_copy(cvec[0:64, C_Q2 + 2:C_W1], ps[0:64, 0, C_Q2 + 2:C_W1])
                    link(V.tensor_copy(cvec[:, C_W1:C_W1 + 2 * NM], ps[:, 0, C_W1:C_W1 + 2 * NM]))
                    for s in range(3):
                        last = V.tensor_scalar(cv_rep[:, s, :], ident[:], 0.0, cvec[:, C_V + s:C_V + s + 1],
                                               ALU.mult, ALU.add)
                    last.then_inc(cv_ready.sem, 1)
                    for c0, c1, col in ((C_QK, C_QK + 5, MXCOL["qk"]), (C_Q2, C_Q2 + 3, MXCOL["q2"])):
                        last = V.tensor_reduce(mx[:, col:col + 1], cvec[:, c0:c1], AX.X, ALU.max,
                                               apply_absolute_value=True)
                    link(last)
                    for col in (MXCOL["qk"], MXCOL["q2"]):
                        last = V.tensor_scalar(mx[:, col:col + 1], mx[:, col:col + 1], 1.0 / 128, None, ALU.mult)
                    link(last)
            dve.wait_ge(stage_used.sem, stage_used.at(0, N1))
            V.tensor_tensor(bias1[:], bias1[:], ps[:, 1, 0:D], ALU.add)
            for gidx, (c0, c1) in enumerate(MXGROUPS):
                last = V.tensor_reduce(mxm[:, gidx:gidx + 1], mx[:, c0:c1], AX.X, ALU.max)
            last.then_inc(maxima.sem, 1)
            dve.wait_ge(pro_pe.sem, pro_pe.at(0, LNMATS + 2))
            link(V.tensor_reduce(mxr[:, 0:1], ps[0:8, 2, 0:P], AX.X, ALU.max))
            link(V.tensor_scalar(mxr[:, 1:2], mxr[:, 0:1], 1e-30, None, ALU.max))
            link(V.tensor_scalar(mxr[:, 2:3].bitcast(u32), mxr[:, 1:2].bitcast(u32), 0x7F800000, None,
                                 ALU.bitwise_and))
            link(V.reciprocal(mxr[:, 3:4], mxr[:, 2:3]))
            V.tensor_scalar(mxd[:], ident[0:8, 0:8], mxr[:, 3:4], None, ALU.mult).then_inc(maxima.sem, 1)
            dve.wait_ge(pro_pe.sem, pro_pe.at(0, LNMATS + 3))
            link(V.tensor_scalar(sc[:, 0:7], ps[:, 3, 0:7], 4.0, None, ALU.mult))
            link(V.tensor_scalar(sc[:, S_CTX:S_CTX + 1], sc[:, S_CTX:S_CTX + 1], 2.0, None, ALU.mult))
            link(V.reciprocal(rp[:, 0:7], sc[:, 0:7]))

            def inverse(k):
                return rp[:, k:k + 1]

            def put(dst, a, b, c):
                link(V.tensor_scalar(sc[:, dst:dst + 1], a, b, c, ALU.mult, ALU.mult))

            put(E1, inverse(S_QKV), DH ** -0.5, inverse(S_QKV))
            put(T0, inverse(S_KV2), 1.0, inverse(S_CTX))
            put(E2, inverse(S_Q2), DH ** -0.5, sc[:, T0:T0 + 1])
            put(D1, inverse(S_QKV), 1.0, inverse(S_O1))
            put(D2, inverse(S_O2), 1.0, sc[:, T0:T0 + 1])
            put(D3, inverse(S_W1), 1.0, 1.0)
            V.tensor_scalar(cvec[:, 0:C_Q2], cvec[:, 0:C_Q2], sc[:, S_QKV:S_QKV + 1], None, ALU.mult)
            V.tensor_scalar(cvec[:, C_Q2:C_W1], cvec[:, C_Q2:C_W1], sc[:, S_Q2:S_Q2 + 1], None, ALU.mult)
            link(V.tensor_tensor(cvec[:, C_W1:C_W1 + 2 * NM], cvec[:, C_W1:C_W1 + 2 * NM], b1c[:], ALU.add))
            link(V.tensor_scalar(cvec[:, C_W1:C_W1 + NM], cvec[:, C_W1:C_W1 + NM], sc[:, S_W1:S_W1 + 1], None, ALU.mult))
            for n in range(N1, len(CHUNKS)):
                ch = CHUNKS[n]
                dve.wait_ge(staged[n % NSTAGE].sem, staged[n % NSTAGE].at(0, stage_value[n]))
                if ch[0] == "cut":
                    _, name, c0, cw, ln, scale = ch
                    ns = slices(t[name].shape[0])
                    wh, wl, off = DEST[name]
                    wh, wl = wh[:, 0:ns, off + c0:off + c0 + cw], wl[:, 0:ns, off + c0:off + c0 + cw]
                    s_ap = sc[:, scale:scale + 1]
                else:
                    _, s0, ns = ch
                    cw, ln, s_ap = D, None, 1.0
                    wh, wl = w2_h[:, s0:s0 + ns, :].bitcast(f32), w2_l[:, s0:s0 + ns, :]
                if n > N1:
                    dve.wait_ge(stage_used.sem, stage_used.at(0, n))
                if ln is not None:
                    for s in range(ns):
                        last = V.tensor_scalar(tmp[:, s * cw:(s + 1) * cw], stage_buf(n)[:, s * cw:(s + 1) * cw],
                                               gb[:, 2 * ln, s:s + 1], s_ap, ALU.mult, ALU.mult)
                else:
                    last = V.tensor_scalar(tmp[:, 0:ns * cw], stage_buf(n)[:, 0:ns * cw], s_ap, None, ALU.mult)
                last.then_inc(c_product.sem, 1)
                dve.wait_ge(c_product.sem, c_product.at(0, n - N1 + 1))
                dve.wait_ge(pro_hi.sem, pro_hi.at(0, n - N1 + 1))
                V.tensor_tensor(wl, tmp[:, 0:ns * cw].rearrange("p (s c) -> p s c", s=ns), wh,
                                ALU.subtract).then_inc(stage_used.sem, 1)
            dve.wait_ge(stage_used.sem, stage_used.at(0, len(CHUNKS)))
            V.memset(mxm[:, 0:1], 0.0).then_inc(pro.sem, 1)

            def layer_norm(k, e, on, i):
                src = (x_in, x1, x2)[k]
                if k == 0:
                    dve.wait_ge(x_loaded.sem, x_loaded.at(e))
                else:
                    dve.wait_ge(resid[k - 1].sem, resid[k - 1].at(e))
                for q in range(KT):
                    last = V.bn_stats(stats[k][:, q, :], src[:, q, :])
                last.then_inc(ln_stat[k].sem, 1)
                dve.wait_ge(ln_stat[k].sem, ln_stat[k].at(e, 1))
                V.tensor_copy(pace[:], stats[k][:, 0, 0:1])
                for q in range(KT):
                    last = V.bn_aggr(mv[k][:, q, :], stats[k][:, q, :])
                last.then_inc(ln_stat[k].sem, 1)
                dve.wait_ge(ln_stat[k].sem, ln_stat[k].at(e, 2))
                dve.wait_ge(ln_rstd[k].sem, ln_rstd[k].at(e - 1))
                V.tensor_scalar(ve[k][:], mv[k][:, :, 1], EPS, None, ALU.add).then_inc(ln_stat[k].sem, 1)

            def normalise(k, e, i):
                src = (x_in, x1, x2)[k]
                dve.wait_ge(ln_rstd[k].sem, ln_rstd[k].at(e))
                prior = ring(streams_of(i), before_of(i), XHAT, 1)[k][1]
                if prior:
                    freed, step_offset, count = prior
                    dve.wait_ge(freed.sem, freed.at(i + step_offset, count))
                for q in range(KT):
                    V.tensor_scalar(xhat[:, q, 0:D], src[:, q, :], mv[k][:, q, 0:1], rs[k][:, q:q + 1],
                                    ALU.subtract, ALU.mult)
                for q in range(KT):
                    last = V.tensor_scalar(xhat[:, q, D:3 * P], src[:, q, 2 * P:D], mv[k][:, q, 0:1],
                                           rs[k][:, q:q + 1], ALU.subtract, ALU.mult)
                last.then_inc(ln_done[k].sem, 1)

            def tr_lo_part(k, e, s):
                dve.wait_ge(tr_hi[k].sem, tr_hi[k].at(e))
                V.tensor_tensor(al[k][:].rearrange("p a b -> p (a b)"), flat[s][:, 0:2 * N],
                                ah[k][:, 0:2].rearrange("p a b -> p (a b)"), ALU.subtract)
                V.tensor_tensor(ah[k][64:P, 2], flat[s][64:P, 2 * N:3 * N], ah[k][64:P, 2],
                                ALU.subtract).then_inc(tr_lo[k].sem, 1)

            def qk_lo_part(c, e, s):
                dve.wait_ge(qk_hi.sem, qk_hi.at(e, c + 1))
                for m in range(4 * c, min(4 * c + 4, 5)):
                    last = V.scalar_tensor_tensor(qk_l[:, m, :], flat[s][:, (m - 4 * c) * N:(m - 4 * c + 1) * N],
                                                  cvec[:, C_QK + m:C_QK + m + 1], qk_h[:, m, :], ALU.add, ALU.subtract)
                last.then_inc(qk_lo.sem, 1)

            def q2_lo_part(e, s):
                dve.wait_ge(q2_hi.sem, q2_hi.at(e))
                for m in range(3):
                    r = P if m < 2 else 64
                    last = V.scalar_tensor_tensor(q2_l[0:r, m, :], flat[s][0:r, m * N:(m + 1) * N],
                                                  cvec[0:r, C_Q2 + m:C_Q2 + m + 1], q2_h[0:r, m, :],
                                                  ALU.add, ALU.subtract)
                last.then_inc(q2_lo.sem, 1)

            def ct_lo_part(e, s):
                dve.wait_ge(ct_hi.sem, ct_hi.at(e))
                V.scalar_tensor_tensor(ct_l[:, 0, :], flat[s][:, 0:J], sc[:, S_CTX:S_CTX + 1], ct_h[:, 0, :],
                                       ALU.mult, ALU.subtract)
                V.scalar_tensor_tensor(ct_h[64:P, 1, :], flat[s][64:P, J:2 * J], sc[64:P, S_CTX:S_CTX + 1],
                                       ct_h[64:P, 1, :], ALU.mult, ALU.subtract).then_inc(ct_lo.sem, 1)

            def kv2_parts(e, s):
                dve.wait_ge(k2_hi.sem, k2_hi.at(e))
                V.tensor_tensor(k2_l[:, 0:2, :].rearrange("p a b -> p (a b)"), flat[s][:, 0:2 * J],
                                k2_h[:, 0:2, :].rearrange("p a b -> p (a b)"), ALU.subtract)
                V.tensor_tensor(k2_l[0:64, 2, :], flat[s][0:64, 2 * J:3 * J], k2_h[0:64, 2, :],
                                ALU.subtract).then_inc(k2_lo.sem, 1)
                dve.wait_ge(pv_done[1].sem, pv_done[1].at(e - 1))
                V.tensor_copy(v2[:, :, 0:2 * DH:2],
                              slot[s][0:J, 1, 0:D].rearrange("p (h d) -> p h d", d=DH)).then_inc(v2_copied.sem, 1)

            def reduce1(n, e, s):
                dve.wait_ge(max_done.sem, max_done.at(e, n + 1))
                if n == 0:
                    dve.wait_ge(mt_done[0].sem, mt_done[0].at(e - 1))
                V.tensor_reduce(m_q[0][:, :, MAX_ORDER[n], :], flat[s].rearrange("p (g k) -> p g k", k=N),
                                AX.X, ALU.max, negate=True).then_inc(max_red.sem, 1)

            def reduce2(n, e, s):
                T0, nt = MAX2_PAIRS[n]
                dve.wait_ge(max2_done.sem, max2_done.at(e, n + 1))
                if n == 0:
                    dve.wait_ge(mt_done[1].sem, mt_done[1].at(e - 1))
                V.tensor_reduce(m_q[1][:, :, T0:T0 + nt, :].rearrange("p h t q -> p h (t q)"),
                                slot[s][:, :, 0:nt * KT * J].rearrange("p h (g k) -> p h g k", k=J),
                                AX.X, ALU.max, negate=True).then_inc(max2_red.sem, 1)

            def reciprocal(a, e):
                dve.wait_ge(den_spread[a].sem, den_spread[a].at(e))
                dve.wait_ge(rec_lo[a].sem, rec_lo[a].at(e - 1))
                V.reciprocal(rec[a][:], den[a][:]).then_inc(rec_done[a].sem, 1)

            def rec_lo_part(a, e):
                dve.wait_ge(rec_hi[a].sem, rec_hi[a].at(e))
                V.tensor_tensor(rec_l[a][:], rec[a][:], rec_h[a][:].bitcast(f32), ALU.subtract).then_inc(rec_lo[a].sem, 1)

            def out_norm(a, e, s):
                dve.wait_ge(o_spread[a].sem, o_spread[a].at(e))
                dve.wait_ge(rb_done[a].sem, rb_done[a].at(e))
                c = o_c[a][:].rearrange("p a b -> p (a b)")
                V.tensor_tensor(c, c, flat[s][:, 0:3 * N], ALU.mult).then_inc(o_norm[a].sem, 1)

            def residual(a, e, s):
                dve.wait_ge(oproj_done[a].sem, oproj_done[a].at(e))
                dve.wait_ge(xb_done[a].sem, xb_done[a].at(e))
                dve.wait_ge(xb_done[a + 1].sem, xb_done[a + 1].at(e - 1))
                dst, xb = ((x1, xb1), (x2, xb2))[a]
                V.scalar_tensor_tensor(dst[:], slot[s][:, :, 0:D], sc[:, D1 + a:D1 + a + 1], xb[:],
                                       ALU.mult, ALU.add).then_inc(resid[a].sem, 1)

            def ff_product(m, e):
                dve.wait_ge(gelu_done.sem, gelu_done.at(e, m + 1))
                if m >= 2:
                    dve.wait_ge(ffl_done.sem, ffl_done.at(e, m - 1))
                else:
                    dve.wait_ge(ffl_done.sem, ffl_done.at(e - 1, NM - 1 + m))
                V.scalar_tensor_tensor(ff_p[:, m % 2], ps_f1[:, 0:N], cvec[:, C_W1 + m:C_W1 + m + 1], ff_g[:, m % 2],
                                       ALU.add, ALU.mult).then_inc(ffp_done.sem, 1)

            def output(e):
                dve.wait_ge(ff2_step.sem, ff2_step.at(e))
                dve.wait_ge(xb_done[2].sem, xb_done[2].at(e))
                dve.wait_ge(out_stored.sem, out_stored.at(e - 1))
                V.scalar_tensor_tensor(out_sb[:], ps[:, 6:8, 0:D], sc[:, D3:D3 + 1], xb3[:],
                                       ALU.mult, ALU.add).then_inc(out_ready.sem, 1)

            def step(i):
                on, tab = streams_of(i), ring(streams_of(i), before_of(i))
                if 0 in on:
                    layer_norm(0, i + 1, on, i)
                    normalise(0, i + 1, i)
                if 0 in on:
                    tr_lo_part(0, i + 1, tab["tr", 0][0])
                if 1 in on:
                    reciprocal(0, i)
                    rec_lo_part(0, i)
                if 0 in on:
                    qk_lo_part(0, i + 1, tab["qk", 0][0])
                    qk_lo_part(1, i + 1, tab["qk", 1][0])
                if 1 in on:
                    out_norm(0, i, tab["rb", 0][0])
                if 2 in on:
                    reciprocal(1, i - 1)
                    rec_lo_part(1, i - 1)
                if 1 in on:
                    residual(0, i, tab["oproj", 0][0])
                    layer_norm(1, i, on, i)
                    ct_lo_part(i, tab["ct", 0][0])
                    normalise(1, i, i)
                if 2 in on:
                    out_norm(1, i - 1, tab["rb", 1][0])
                if 1 in on:
                    kv2_parts(i, tab["kv2", 0][0])
                if 2 in on:
                    residual(1, i - 1, tab["oproj", 1][0])
                    layer_norm(2, i - 1, on, i)
                if 1 in on:
                    tr_lo_part(1, i, tab["tr", 1][0])
                if 2 in on:
                    normalise(2, i - 1, i)
                if 1 in on:
                    q2_lo_part(i, tab["q2", 0][0])
                if 2 in on:
                    tr_lo_part(2, i - 1, tab["tr", 2][0])
                for m in range(NM + 1):
                    if 2 in on and m < NM:
                        ff_product(m, i - 1)
                    if 0 in on:
                        for n in MAX_AT.get(m, ()):
                            reduce1(n, i + 1, tab["max", n][0])
                    if 1 in on:
                        for n in MAX2_AT.get(m, ()):
                            reduce2(n, i, tab["max2", n][0])
                if 2 in on:
                    output(i - 1)

            run_steps(dve, step)


_PRE = "L0_xattn_"
_INS = ["n1_g", "n1_b", "q1", "k1", "v1", "o1_w", "o1_b", "n2_g", "n2_b", "q2", "k2", "v2", "o2_w", "o2_b",
        "n3_g", "n3_b", "ff_w1", "ff_b1", "ff_w2", "ff_b2"]


def _constants():
    import numpy as np
    sel = np.zeros((H, 3 * P), np.float32)
    for f in range(3 * P):
        h = (f if f < D else f - 64) // DH
        sel[NG * (h % 4) + h // 4, f] = 1.0
    return {"c_ident": np.eye(P, dtype=np.float32), "c_sel": sel,
            "c_aug": np.full((1, NT * N), AUG, np.float16)}


def kernel(**inputs):
    import numpy as _np
    import concourse.bacc as _bacc
    from concourse import mybir as _mybir
    from concourse.bass_utils import run_bass_kernel_spmd as _run

    nc = _bacc.Bacc("TRN2", target_bir_lowering=False, num_devices=1)
    host = {"x": inputs["x"], "ctx_768": inputs["ctx_768"]}
    host.update({n: inputs[_PRE + n] for n in _INS})
    host.update(_constants())
    arrays, aps = {}, {}
    for name, a in host.items():
        a = _np.ascontiguousarray(a)
        arrays[f"in_{name}"] = a
        aps[name] = nc.dram_tensor(f"in_{name}", a.shape, _mybir.dt.from_np(a.dtype), kind="ExternalInput").ap()
    o = nc.dram_tensor("out_0", (B, N, D), _mybir.dt.float32, kind="ExternalOutput").ap()
    xattn_block(nc, aps, o)
    r = _run(nc, [arrays], core_ids=[0])
    return r.results[0]["out_0"]
```

```python
import concourse.bass as bass
from concourse import mybir
from contextlib import ExitStack

B, N, D = 64, 256, 320
H, DH = 20, 16
J, CTX = 77, 192
FF = 4 * D
EPS = 1e-5
P = 128
KT = N // P
NT = H // 2
NG = H // 4
NM = FF // P
AUG = 32768.0
NP = 4
NSTAGE = 3
STW = 3 * D


def xattn_block(nc, t, out):
    f32, f32r, f16, u32 = mybir.dt.float32, mybir.dt.float32r, mybir.dt.float16, mybir.dt.uint32
    ACT, ALU, AX = mybir.ActivationFunctionType, mybir.AluOpType, mybir.AxisListType
    ctx = ExitStack()

    def sb(name, shape, dt):
        return ctx.enter_context(nc.sbuf_tensor(name, shape, dt))

    class Event:

        def __init__(self, name, n):
            self.sem, self.n = ctx.enter_context(nc.semaphore(name)), n

        def at(self, e, k=None):
            value = e * self.n + (self.n if k is None else k)
            return max(value, 0) if isinstance(value, int) else value

    with ctx:
        wqkv_h, wqkv_l = sb("wqkv_h", [P, 3, 3 * D], f16), sb("wqkv_l", [P, 3, 3 * D], f16)
        wo1_h, wo1_l = sb("wo1_h", [P, 3, D], f16), sb("wo1_l", [P, 3, D], f16)
        wq2_h, wq2_l = sb("wq2_h", [P, 3, D], f16), sb("wq2_l", [P, 3, D], f16)
        wo2_h, wo2_l = sb("wo2_h", [P, 3, D], f16), sb("wo2_l", [P, 3, D], f16)
        wkv2_h, wkv2_l = sb("wkv2_h", [P, 2, 2 * D], f16), sb("wkv2_l", [P, 2, 2 * D], f16)
        w1_h, w1_l = sb("w1_h", [P, 3, 2 * FF], f16), sb("w1_l", [P, 3, 2 * FF], f16)
        w2_h, w2_l = sb("w2_h", [P, NM, D], f32r), sb("w2_l", [P, NM, D], f32r)
        ident = sb("ident", [P, P], f32)
        sel = sb("sel", [H, 3 * P], f32r)
        ones = sb("ones", [8, P], f32)
        gb = sb("gb", [P, 6, 3], f32)
        cvec = sb("cvec", [P, 32], f32)
        b1c = sb("b1c", [P, 2 * NM], f32)
        bias1, bias2, bias3 = (sb(f"bias{k}", [P, D], f32) for k in (1, 2, 3))
        mx = sb("mx", [P, 40], f32)
        mxm = sb("mxm", [P, 8], f32)
        mxr, mxd = sb("mxr", [8, 4], f32), sb("mxd", [8, 8], f32)
        rp = sb("rp", [P, 8], f32)
        sc = sb("sc", [P, 16], f32)
        halfneg = sb("halfneg", [P, KT], f32)
        pace = sb("pace", [P, 1], f32)
        x_in, xb0, xb1, x1, xb2, x2, xb3, out_sb = (
            sb(n, [P, KT, D], f32) for n in ("x_in", "xb0", "xb1", "x1", "xb2", "x2", "xb3", "out_sb"))
        sel_f = out_sb[0:H].rearrange("p a b -> p (a b)")[:, 0:3 * P]
        cv_rep = x2[:].rearrange("p a b -> p (a b)")[:, 0:3 * P].rearrange("p (s c) -> p s c", s=3)
        xhat = sb("xhat", [P, KT, 3 * P], f32)
        stats = [sb(f"stats{k}", [P, KT, 6], f32) for k in range(3)]
        mv = [sb(f"mv{k}", [P, KT, 2], f32) for k in range(3)]
        ve = [sb(f"ve{k}", [P, KT], f32) for k in range(3)]
        rs = [sb(f"rs{k}", [P, KT], f32) for k in range(3)]
        ah = [sb(f"ah{k}", [P, 3, N], f16) for k in range(3)]
        al = [sb(f"al{k}", [P, 2, N], f16) for k in range(3)]
        qk_h, qk_l = sb("qk_h", [P, 5, N], f16), sb("qk_l", [P, 5, N], f16)
        q4, k4 = sb("q4", [P, NT, N], f16), sb("k4", [P, NT, N], f16)
        v1 = sb("v1", [P, KT, H, 2 * DH], f32)
        c_in = sb("c_in", [J, 2 * P], f32)
        ct_h, ct_l = sb("ct_h", [P, 2, J], f16), sb("ct_l", [P, 1, J], f16)
        k2_h, k2_l = sb("k2_h", [P, 3, J], f16), sb("k2_l", [P, 3, J], f16)
        q2_h, q2_l = sb("q2_h", [P, 3, N], f16), sb("q2_l", [P, 3, N], f16)
        q42, k42 = sb("q42", [P, NT, N], f16), sb("k42", [P, NT, J], f16)
        v2 = sb("v2", [J, H, 2 * DH], f32)
        m_q = [sb(f"m_q{a}", [P, 2, NT, KT], f32) for a in range(2)]
        m_row = [sb(f"m_row{a}", [H, N], f16) for a in range(2)]
        probs = sb("probs", [P, NP, 4 * N], f32)
        stage = probs[:, :, :].rearrange("p a b -> p (a b)")
        o_raw = [sb(f"o_raw{a}", [P, NG, N], f32) for a in range(2)]
        o_c = [sb(f"o_c{a}", [P, 3, N], f32) for a in range(2)]
        o_h = [sb(f"o_h{a}", [P, 3, N], f16) for a in range(2)]
        o_l = [sb(f"o_l{a}", [P, 2, N], f16) for a in range(2)]
        den = [sb(f"den{a}", [H, N], f32) for a in range(2)]
        rec = [sb(f"rec{a}", [H, N], f32) for a in range(2)]
        rec_h = [sb(f"rec_h{a}", [H, N], f32r) for a in range(2)]
        rec_l = [sb(f"rec_l{a}", [H, N], f32r) for a in range(2)]
        ff_g = sb("ff_g", [P, 2, N], f32)
        ff_h, ff_l = sb("ff_h", [P, 2, N], f32r), sb("ff_l", [P, 2, N], f32r)

        ps = ctx.enter_context(nc.psum_tensor("ps", [P, 8, 512], f32))
        slot = [ps[:, 0:2, :], ps[:, 2:4, :]]
        flat = [s.rearrange("p a b -> p (a b)") for s in slot]
        ps_f1, ps_f2 = ps[:, 5, :], [ps[:, 6, :], ps[:, 7, :]]
        ps_pv = [ps_f1, ps[:, 4, :]]

        (S_QKV, S_Q2, S_W1, S_KV2, S_CTX, S_O1, S_O2, E1, E2, D1, D2, D3, T0, T1, T2) = range(15)

        x_loaded, c_loaded = Event("x_loaded", 16), Event("c_loaded", 32)
        ln_stat = [Event(f"ln_stat{k}", 3) for k in range(3)]
        ln_rstd = [Event(f"ln_rstd{k}", 1) for k in range(3)]
        ln_done = [Event(f"ln_done{k}", 1) for k in range(3)]
        tr_done = [Event(f"tr_done{k}", 1) for k in range(3)]
        tr_hi = [Event(f"tr_hi{k}", 1) for k in range(3)]
        tr_lo = [Event(f"tr_lo{k}", 1) for k in range(3)]
        qk_done, qk_hi, qk_lo = Event("qk_done", 5), Event("qk_hi", 5), Event("qk_lo", 5)
        v_done, v_copied = Event("v_done", KT), Event("v_copied", KT)
        spread = [Event(f"spread{r}", 6 * 16) for r in range(4)]
        max_done, max_red = Event("max_done", NT), Event("max_red", NT)
        max2_done, max2_red = Event("max2_done", 8), Event("max2_red", 8)
        mt_done = [Event(f"mt_done{a}", 1) for a in range(2)]
        mt_row = [Event(f"mt_row{a}", 1) for a in range(2)]
        m_spread = [Event(f"m_spread{a}", 32) for a in range(2)]
        st_done = [Event("st_done0", NT), Event("st_done1", NG)]
        exp_done = [Event("exp_done0", NT), Event("exp_done1", NG)]
        pv_done = [Event(f"pv_done{a}", NG) for a in range(2)]
        o_copied = [Event(f"o_copied{a}", NG) for a in range(2)]
        o_spread = [Event(f"o_spread{a}", 48) for a in range(2)]
        den_spread = [Event(f"den_spread{a}", 16) for a in range(2)]
        rec_done = [Event(f"rec_done{a}", 1) for a in range(2)]
        rec_hi = [Event(f"rec_hi{a}", 1) for a in range(2)]
        rec_lo = [Event(f"rec_lo{a}", 1) for a in range(2)]
        rb_done = [Event(f"rb_done{a}", 1) for a in range(2)]
        o_norm = [Event(f"o_norm{a}", 1) for a in range(2)]
        o_hi = [Event(f"o_hi{a}", 1) for a in range(2)]
        o_lo = [Event(f"o_lo{a}", 2) for a in range(2)]
        oproj_done = [Event(f"oproj_done{a}", 1) for a in range(2)]
        resid = [Event(f"resid{a}", 1) for a in range(2)]
        xb0_done = Event("xb0_done", 1)
        xb_done = [Event(f"xb_done{a}", 1) for a in range(3)]
        q2_done, q2_hi, q2_lo = Event("q2_done", 1), Event("q2_hi", 1), Event("q2_lo", 1)
        q2_spread = Event("q2_spread", 12 * 16)
        ct_done, ct_hi, ct_lo = Event("ct_done", 1), Event("ct_hi", 1), Event("ct_lo", 1)
        kv2_done, k2_hi, k2_lo = Event("kv2_done", 1), Event("k2_hi", 1), Event("k2_lo", 1)
        v2_copied, k2_spread = Event("v2_copied", 1), Event("k2_spread", 12 * 16)
        ff1_done, gelu_done, ffp_done = Event("ff1_done", NM), Event("gelu_done", NM), Event("ffp_done", NM)
        ffh_done, ffl_done, ff2_step = Event("ffh_done", NM), Event("ffl_done", NM), Event("ff2_step", NM)
        gelu_table, exp_table = Event("gelu_table", 1), Event("exp_table", 1)
        table_out = {gelu_table: sb("gelu_out", [P, 1], f32), exp_table: sb("exp_out", [P, 1], f32)}
        out_ready, out_stored = Event("out_ready", 1), Event("out_stored", 16)

        MAX_AT = {"oproj": (0,), 3: (1,), "tr": (2,), "q2": (3,), 5: (4, 5), 6: (6, 7), 7: (8, 9)}
        MT_AT, TR2_AT = 8, 9

        QKV, SELF, CROSS, NORM1, FFN, LAST = range(6)
        STREAM_STEP = (1, 0, -1, 2, -2, -3)

        def max_units(key):
            return [(("max", n), QKV, max_red, n + 1) for n in MAX_AT.get(key, ())]

        UNITS = []
        for T in range(NT):
            UNITS += [(("st", T), SELF, exp_done[0], T + 1)]
            if T == 6:
                UNITS += [(("mt", 1), CROSS, mt_row[1], 1)]
            if T == 7:
                UNITS += [(("ct", 0), SELF, ct_lo, 1)]
        UNITS += [(("st2", g), CROSS, exp_done[1], g + 1) for g in range(NG)]
        UNITS += [(("tr", 0), NORM1, tr_lo[0], 1), (("rb", 0), SELF, o_norm[0], 1),
                  (("kv2", 0), SELF, v2_copied, 1), (("oproj", 0), SELF, resid[0], 1),
                  (("rb", 1), CROSS, o_norm[1], 1), (("oproj", 1), CROSS, resid[1], 1)]
        UNITS += max_units("oproj") + max_units(3) + [(("tr", 1), SELF, tr_lo[1], 1)] + max_units("tr")
        UNITS += [(("q2", 0), SELF, q2_lo, 1)] + max_units("q2")
        for m in range(5, NM + 1):
            UNITS += max_units(m)
            if m == MT_AT:
                UNITS += [(("mt", 0), QKV, mt_row[0], 1)]
            if m == TR2_AT:
                UNITS += [(("tr", 2), CROSS, tr_lo[2], 1)]
        MAX_ORDER = [0, 4, 8, 1, 5, 9, 2, 6, 3, 7]
        MAX2_PAIRS = [(0, 3), (3, 3), (6, 3), (9, 1)]

        def ring(active, before, units=None, slots=2):
            last, table = {}, {}
            for ago, streams in ((1, before), (0, active)):
                uses = [u for u in (UNITS if units is None else units) if u[1] in streams]
                for n, (name, stream, ev, k) in enumerate(uses):
                    if ago == 0:
                        table[name] = (n % slots, last.get(n % slots))
                    last[n % slots] = (ev, STREAM_STEP[stream] - ago, k)
            return table

        PROBS = [((0, T), SELF, pv_done[0], T // 2 + 1) for T in range(NT)]
        PROBS += [((1, g), CROSS, pv_done[1], g + 1) for g in range(NG)]

        def probs_ring(active, before):
            return ring(active, before, PROBS, NP)

        PV_USES = [((a, g), (SELF, CROSS)[a], o_copied[a], g + 1) for a in range(2) for g in range(NG)]

        def pv_ring(active, before):
            return ring(active, before, PV_USES, 2)

        def streams_of(i):
            if not isinstance(i, int):
                return tuple(range(6))
            return tuple(s for s in range(6) if 0 <= i + STREAM_STEP[s] < B)

        def before_of(i):
            return streams_of(i - 1)

        def run_steps(eng, step):
            for i in range(-2, 4):
                step(i)
            with eng.Fori(4, B - 2) as i:
                step(i)
            for i in range(B - 2, B + 3):
                step(i)

        def split_passes(xh, xl, wh, wl, full):
            pairs = []
            for s in range(full):
                pairs += [(xh[:, s], wh[:, s]), (xl[:, s], wh[:, s]), (xh[:, s], wl[:, s])]
            return pairs + [(xh[:, full], wh[:, full]), (xh[0:64, full], wl[0:64, full])]

        CW = 256
        def slices(k):
            return 3 if k == D else 2
        MATS = [("q1", 0, D, 0, S_QKV), ("k1", 0, D, 0, S_QKV), ("v1", 0, D, 0, S_QKV), ("q2", 0, D, 1, S_Q2)]
        MATS += [("ff_w1", c * CW, CW, 2, S_W1) for c in range(2 * FF // CW)]
        LNMATS = len(MATS)
        MATS += [("k2", 0, D, None, S_KV2), ("v2", 0, D, None, S_KV2), ("o2_w", 0, D, None, S_O2),
                 ("o1_w", 0, D, None, S_O1)]
        CTXCH = [(b, min(5, B - b)) for b in range(0, B, 5)]
        W2CH = [(s, min(3, NM - s)) for s in range(0, NM, 3)]
        DEST = {"q1": (wqkv_h, wqkv_l, 0), "k1": (wqkv_h, wqkv_l, D), "v1": (wqkv_h, wqkv_l, 2 * D),
                "q2": (wq2_h, wq2_l, 0), "ff_w1": (w1_h, w1_l, 0), "k2": (wkv2_h, wkv2_l, 0),
                "v2": (wkv2_h, wkv2_l, D), "o2_w": (wo2_h, wo2_l, 0), "o1_w": (wo1_h, wo1_l, 0)}
        CHUNKS = [("ctx",) + c for c in CTXCH] + [("max",) + m for m in MATS]
        CHUNKS += [("cut",) + m for m in MATS] + [("w2",) + c for c in W2CH]
        N1 = len(CTXCH) + len(MATS)
        staged, vec_loaded = [Event(f"staged{k}", 16) for k in range(NSTAGE)], Event("vec_loaded", 16)
        stage_used, c_product = Event("stage_used", 1), Event("c_product", 1)
        pro, pro_pe, pro_act = Event("pro", 1), Event("pro_pe", 1), Event("pro_act", 1)
        pro_dve, pro_hi, maxima, cv_ready = (Event(n, 1) for n in ("pro_dve", "pro_hi", "maxima", "cv_ready"))
        tmp = stage[:, NSTAGE * STW:(NSTAGE + 1) * STW]

        def stage_buf(n):
            return stage[:, (n % NSTAGE) * STW:(n % NSTAGE + 1) * STW]

        def chunk_dmas(n):
            ch, buf = CHUNKS[n], stage_buf(n)
            if ch[0] == "ctx":
                _, b, nb = ch
                return [(buf[0:J, 0:nb * CTX].rearrange("p (b c) -> p b c", b=nb),
                         t["ctx_768"][b:b + nb].rearrange("b j c -> j b c"))]
            if ch[0] == "w2":
                _, s, ns = ch
                return [(buf[:, 0:ns * D].rearrange("p (s c) -> p s c", s=ns),
                         t["ff_w2"][s * P:(s + ns) * P, :].rearrange("(s p) c -> p s c", p=P))]
            _, name, c0, cw, _, _ = ch
            w = t[name]
            full = slices(w.shape[0]) - 1
            b3 = buf[:, 0:(full + 1) * cw].rearrange("p (s c) -> p s c", s=full + 1)
            tail = w[full * P:full * P + 64, c0:c0 + cw]
            return [(b3[:, 0:full, :], w[0:full * P, c0:c0 + cw].rearrange("(s p) c -> p s c", p=P)),
                    (b3[0:64, full, :], tail), (b3[64:P, full, :], tail)]

        stage_value, counts = [], [0] * NSTAGE
        for n in range(len(CHUNKS)):
            counts[n % NSTAGE] += 16 * len(chunk_dmas(n))
            stage_value.append(counts[n % NSTAGE])

        C_QK, C_V, C_Q2, C_W1 = 0, 5, 8, 11
        def c_places(n):
            _, name, c0, cw, _, _ = CHUNKS[n]
            if name == "q1":
                return [(0, 128, 0, C_QK), (128, 256, 0, C_QK + 1), (256, 320, 0, C_QK + 2)]
            if name == "k1":
                return [(0, 64, 64, C_QK + 2), (64, 192, 0, C_QK + 3), (192, 320, 0, C_QK + 4)]
            if name in ("v1", "q2"):
                c = C_V if name == "v1" else C_Q2
                return [(0, 128, 0, c), (128, 256, 0, c + 1), (256, 320, 0, c + 2)]
            return [(0, 128, 0, C_W1 + c0 // P), (128, 256, 0, C_W1 + c0 // P + 1)]

        NVEC_LOADS = 2 + 4 + 18 + 1 + 3
        PRO_DONE = 2

        MXCOL, MXGROUPS, col = {}, [], 0
        for scale in (S_QKV, S_Q2, S_W1, S_KV2, S_CTX, S_O1, S_O2):
            first = col
            for n in range(N1):
                if (scale == S_CTX) if CHUNKS[n][0] == "ctx" else (CHUNKS[n][5] == scale):
                    MXCOL[n], col = col, col + 1
            if scale in (S_QKV, S_Q2):
                MXCOL["qk" if scale == S_QKV else "q2"], col = col, col + 1
            MXGROUPS.append((first, col))

        XHAT = [(0, NORM1, tr_done[0], 1), (1, SELF, tr_done[1], 1), (2, CROSS, tr_done[2], 1)]

        block = ctx.enter_context(nc.Block())

        @block.sync
        def _(sp):
            loads = [(ident[:], t["c_ident"]), (sel_f, t["c_sel"]),
                     (k4[63:64, :, :].rearrange("p a b -> p (a b)"), t["c_aug"][0:1, 0:NT * N]),
                     (k4[127:128, :, :].rearrange("p a b -> p (a b)"), t["c_aug"][0:1, 0:NT * N]),
                     (k42[63:64, :, :].rearrange("p a b -> p (a b)"), t["c_aug"][0:1, 0:NT * J]),
                     (k42[127:128, :, :].rearrange("p a b -> p (a b)"), t["c_aug"][0:1, 0:NT * J])]
            for j, nm in enumerate(("n1_g", "n1_b", "n2_g", "n2_b", "n3_g", "n3_b")):
                v = t[nm]
                loads += [(gb[:, j, 0:2], v[0:2 * P].rearrange("(s p) -> p s", p=P))]
                for r in (0, 64):
                    loads += [(gb[r:r + 64, j, 2:3], v[2 * P:D].rearrange("(p o) -> p o", o=1))]
            loads += [(b1c[:, :], t["ff_b1"].rearrange("(s p) -> p s", p=P))]
            for dst, nm in ((bias1, "o1_b"), (bias2, "o2_b"), (bias3, "ff_b2")):
                loads += [(dst[:, :], t[nm].partition_broadcast(P))]
            sp.wait_ge(pro.sem, pro.at(0, 1))
            for dst, src in loads:
                sp.dma_start(dst, src, allow_slow_non_contiguous=True).then_inc(vec_loaded.sem, 16)
            for n in range(len(CHUNKS)):
                if n >= NSTAGE:
                    sp.wait_ge(stage_used.sem, stage_used.at(0, n - NSTAGE + 1))
                for dst, src in chunk_dmas(n):
                    sp.dma_start(dst, src).then_inc(staged[n % NSTAGE].sem, 16)
            assert len(loads) == NVEC_LOADS

            def load_x(e):
                sp.wait_ge(ln_done[0].sem, ln_done[0].at(e - 1))
                sp.wait_ge(xb0_done.sem, xb0_done.at(e - 1))
                sp.dma_start(x_in[:], t["x"][e].rearrange("(s p) c -> p s c", p=P)).then_inc(x_loaded.sem, 16)

            def load_ctx(e):
                sp.wait_ge(ct_done.sem, ct_done.at(e - 1))
                sp.dma_start(c_in[:, 0:CTX], t["ctx_768"][e]).then_inc(c_loaded.sem, 16)
                sp.dma_start(c_in[:, CTX:2 * P], t["ctx_768"][e, :, P:CTX]).then_inc(c_loaded.sem, 16)

            def spread_qk(e, r):
                sp.wait_ge(qk_lo.sem, qk_lo.at(e))
                sp.wait_ge(max_done.sem, max_done.at(e - 1))
                sp.wait_ge(st_done[0].sem, st_done[0].at(e - 1))
                nt = 3 if r < 2 else 2
                for part, src in enumerate((qk_h, qk_h, qk_l)):
                    sp.dma_start(q4[part:P:4, r:r + 4 * (nt - 1) + 1:4, :],
                                 src[32 * r:32 * r + 32, 0:nt, :]).then_inc(spread[r].sem, 16)
                kb = (r + 2) % 4
                t0 = 3 if kb < 2 else 2
                for part, src in enumerate((qk_h, qk_l, qk_h)):
                    sp.dma_start(k4[part:P:4, r:r + 4 * (4 - t0) + 1:4, :],
                                 src[32 * kb:32 * kb + 32, t0:5, :]).then_inc(spread[r].sem, 16)

            def spread_q2(e):
                sp.wait_ge(q2_lo.sem, q2_lo.at(e))
                sp.wait_ge(st_done[1].sem, st_done[1].at(e - 1))
                for r in range(4):
                    nt = 3 if r < 2 else 2
                    for part, src in enumerate((q2_h, q2_h, q2_l)):
                        sp.dma_start(q42[part:P:4, r:r + 4 * (nt - 1) + 1:4, :],
                                     src[32 * r:32 * r + 32, 0:nt, :]).then_inc(q2_spread.sem, 16)

            def spread_k2(e):
                sp.wait_ge(k2_lo.sem, k2_lo.at(e))
                sp.wait_ge(st_done[1].sem, st_done[1].at(e - 1))
                for r in range(4):
                    nt = 3 if r < 2 else 2
                    for part, src in enumerate((k2_h, k2_l, k2_h)):
                        sp.dma_start(k42[part:P:4, r:r + 4 * (nt - 1) + 1:4, :],
                                     src[32 * r:32 * r + 32, 0:nt, :]).then_inc(k2_spread.sem, 16)

            def spread_max(a, e):
                sp.wait_ge(mt_row[a].sem, mt_row[a].at(e))
                for h in range(2):
                    sp.dma_start((q4, q42)[a][64 * h + 63:64 * h + 64, :, :],
                                 m_row[a][NT * h:NT * h + NT, :]).then_inc(m_spread[a].sem, 16)

            def spread_out(a, e):
                sp.wait_ge(o_copied[a].sem, o_copied[a].at(e))
                sp.wait_ge(rec_done[a].sem, rec_done[a].at(e - 1))
                sp.wait_ge(o_lo[a].sem, o_lo[a].at(e - 1))
                sp.dma_start(den[a][:, :], o_raw[a][1:P:32, :, :]).then_inc(den_spread[a].sem, 16)
                sp.dma_start(o_c[a][0:64, 0:3, :], o_raw[a][0:P:2, 0:NG:2, :]).then_inc(o_spread[a].sem, 16)
                sp.dma_start(o_c[a][64:P, 0:2, :], o_raw[a][0:P:2, 1:NG:2, :]).then_inc(o_spread[a].sem, 16)
                sp.dma_start(o_c[a][64:P, 2, :], o_raw[a][0:P:2, NG - 1, :]).then_inc(o_spread[a].sem, 16)

            def store_out(e):
                sp.wait_ge(out_ready.sem, out_ready.at(e))
                sp.dma_start(out[e].rearrange("(s p) c -> p s c", p=P), out_sb[:]).then_inc(out_stored.sem, 16)

            def step(i):
                on = streams_of(i)
                if NORM1 in on:
                    load_x(i + 2)
                if SELF in on:
                    load_ctx(i)
                if LAST in on:
                    store_out(i - 3)
                if CROSS in on:
                    spread_max(1, i - 1)
                if SELF in on:
                    spread_out(0, i)
                if QKV in on:
                    spread_qk(i + 1, 0)
                if CROSS in on:
                    spread_out(1, i - 1)
                if QKV in on:
                    for r in range(1, 4):
                        spread_qk(i + 1, r)
                if SELF in on:
                    spread_k2(i)
                    spread_q2(i)
                if QKV in on:
                    spread_max(0, i + 1)

            run_steps(sp, step)
            sp.wait_ge(out_stored.sem, out_stored.at(B - 1))

        @block.gpsimd
        def _(pool):
            nc.gpsimd.memset(halfneg[:], -0.5).then_inc(pro_act.sem, 1)
            pool.wait_ge(vec_loaded.sem, 16 * NVEC_LOADS)
            pool.wait_ge(pro_act.sem, pro_act.at(0, 1))

            def rstd(k, e):
                pool.wait_ge(ln_stat[k].sem, ln_stat[k].at(e))
                nc.gpsimd.tensor_tensor(rs[k][:], ve[k][:], halfneg[:], ALU.pow).then_inc(ln_rstd[k].sem, 1)

            def add_bias(k, e):
                src, dst, bias = ((x_in, xb0, bias1), (x1, xb2, bias2), (x2, xb3, bias3))[k]
                if k == 0:
                    pool.wait_ge(x_loaded.sem, x_loaded.at(e))
                else:
                    pool.wait_ge(resid[k - 1].sem, resid[k - 1].at(e))
                if k == 0:
                    pool.wait_ge(xb_done[0].sem, xb_done[0].at(e - 1))
                elif k == 1:
                    pool.wait_ge(resid[1].sem, resid[1].at(e - 1))
                else:
                    pool.wait_ge(out_ready.sem, out_ready.at(e - 1))
                nc.gpsimd.tensor_tensor(dst[:], src[:], bias[:].unsqueeze(1).to_broadcast([P, KT, D]),
                                        ALU.add).then_inc((xb0_done, xb_done[1], xb_done[2])[k].sem, 1)

            def out_lo(a, e):
                pool.wait_ge(o_hi[a].sem, o_hi[a].at(e))
                pool.wait_ge(oproj_done[a].sem, oproj_done[a].at(e - 1))
                nc.gpsimd.tensor_tensor(o_l[a][:], o_c[a][:, 0:2], o_h[a][:, 0:2],
                                        ALU.subtract).then_inc(o_lo[a].sem, 1)
                pool.wait_ge(o_lo[a].sem, o_lo[a].at(e, 1))
                nc.gpsimd.tensor_tensor(o_h[a][64:P, 2], o_c[a][64:P, 2], o_h[a][64:P, 2],
                                        ALU.subtract).then_inc(o_lo[a].sem, 1)
                pool.wait_ge(o_lo[a].sem, o_lo[a].at(e))

            def ff_lo(m, e):
                pool.wait_ge(ffh_done.sem, ffh_done.at(e, m + 1))
                if m >= 2:
                    pool.wait_ge(ff2_step.sem, ff2_step.at(e, m - 1))
                else:
                    pool.wait_ge(ff2_step.sem, ff2_step.at(e - 1, NM - 1 + m))
                nc.gpsimd.tensor_tensor(ff_l[:, m % 2], ff_g[:, m % 2], ff_h[:, m % 2].bitcast(f32),
                                        ALU.subtract).then_inc(ffl_done.sem, 1)

            def step(i):
                on = streams_of(i)

                def tile(m):
                    if FFN in on:
                        ff_lo(m, i - 2)

                if FFN in on:
                    add_bias(2, i - 2)
                if NORM1 in on:
                    rstd(0, i + 2)
                tile(0)
                if SELF in on:
                    out_lo(0, i)
                tile(1)
                if CROSS in on:
                    out_lo(1, i - 1)
                if SELF in on:
                    rstd(1, i)
                tile(2)
                tile(3)
                if CROSS in on:
                    rstd(2, i - 1)
                if NORM1 in on:
                    add_bias(0, i + 2)
                tile(4)
                tile(5)
                if SELF in on:
                    add_bias(1, i)
                for m in range(6, NM):
                    tile(m)

            pool.wait_ge(pro.sem, pro.at(0, PRO_DONE))
            run_steps(pool, step)

        @block.scalar
        def _(act):
            for n in range(N1, len(CHUNKS)):
                ch = CHUNKS[n]
                act.wait_ge(c_product.sem, c_product.at(0, n - N1 + 1))
                if ch[0] == "cut":
                    _, name, c0, cw, _, _ = ch
                    wh, _, off = DEST[name]
                    ns = slices(t[name].shape[0])
                    nc.scalar.activation(wh[:, 0:ns, off + c0:off + c0 + cw],
                                         tmp[:, 0:ns * cw].rearrange("p (s c) -> p s c", s=ns),
                                         ACT.Copy).then_inc(pro_hi.sem, 1)
                else:
                    _, s, ns = ch
                    nc.scalar.activation(w2_h[:, s:s + ns, :],
                                         tmp[:, 0:ns * D].rearrange("p (s c) -> p s c", s=ns),
                                         ACT.Copy).then_inc(pro_hi.sem, 1)
            act.wait_ge(pro.sem, pro.at(0, PRO_DONE))

            def tr_hi_part(k, e, s):
                act.wait_ge(tr_done[k].sem, tr_done[k].at(e))
                if k == 0:
                    act.wait_ge(v_done.sem, v_done.at(e - 1))
                elif k == 1:
                    act.wait_ge(q2_done.sem, q2_done.at(e - 1))
                else:
                    act.wait_ge(ff1_done.sem, ff1_done.at(e - 1))
                nc.scalar.activation(ah[k][:].rearrange("p a b -> p (a b)"), flat[s][:, 0:3 * N],
                                     ACT.Copy).then_inc(tr_hi[k].sem, 1)

            def qk_hi_part(m, e):
                act.wait_ge(qk_done.sem, qk_done.at(e, m + 1))
                if m == 0:
                    for r in range(4):
                        act.wait_ge(spread[r].sem, spread[r].at(e - 1))
                nc.scalar.activation(qk_h[:, m, :], ps_f2[m % 2][:, 0:N], ACT.Identity,
                                     bias=cvec[:, C_QK + m:C_QK + m + 1]).then_inc(qk_hi.sem, 1)

            def q2_hi_part(e, s):
                act.wait_ge(q2_done.sem, q2_done.at(e))
                act.wait_ge(q2_spread.sem, q2_spread.at(e - 1))
                for m in range(3):
                    r = P if m < 2 else 64
                    last = nc.scalar.activation(q2_h[0:r, m, :], flat[s][0:r, m * N:(m + 1) * N],
                                                ACT.Identity, bias=cvec[0:r, C_Q2 + m:C_Q2 + m + 1])
                last.then_inc(q2_hi.sem, 1)

            def ct_hi_part(e, s):
                act.wait_ge(ct_done.sem, ct_done.at(e))
                act.wait_ge(kv2_done.sem, kv2_done.at(e - 1))
                nc.scalar.activation(ct_h[:].rearrange("p a b -> p (a b)"), flat[s][:, 0:2 * J],
                                     ACT.Copy, scale=sc[:, S_CTX:S_CTX + 1]).then_inc(ct_hi.sem, 1)

            def k2_hi_part(e, s):
                act.wait_ge(kv2_done.sem, kv2_done.at(e))
                act.wait_ge(k2_spread.sem, k2_spread.at(e - 1))
                nc.scalar.activation(k2_h[:, 0:2, :].rearrange("p a b -> p (a b)"), flat[s][:, 0:2 * J], ACT.Copy)
                nc.scalar.activation(k2_h[0:64, 2, :], flat[s][0:64, 2 * J:3 * J],
                                     ACT.Copy).then_inc(k2_hi.sem, 1)

            def max_row(a, e, s):
                act.wait_ge(mt_done[a].sem, mt_done[a].at(e))
                act.wait_ge(m_spread[a].sem, m_spread[a].at(e - 1))
                nc.scalar.activation(m_row[a][:], flat[s][0:H, 0:N], ACT.Copy,
                                     scale=1.0 / AUG).then_inc(mt_row[a].sem, 1)

            def load_table(function, loaded, e):
                act.wait_ge(loaded.sem, loaded.at(e - 1))
                nc.scalar.activation(table_out[loaded][:], halfneg[:, 0:1], function).then_inc(loaded.sem, 1)

            def exps(a, n, e, i, s, ptab):
                act.wait_ge(st_done[a].sem, st_done[a].at(e, n + 1))
                b, prior = ptab[a, n]
                if prior:
                    freed, step_offset, count = prior
                    act.wait_ge(freed.sem, freed.at(i + step_offset, count))
                rows = P if a == 0 else J
                nc.scalar.activation(probs[0:rows, b, :], flat[s][0:rows, :], ACT.Exp,
                                     scale=sc[0:rows, E1 + a:E1 + a + 1]).then_inc(exp_done[a].sem, 1)

            def rec_hi_part(a, e):
                act.wait_ge(rec_done[a].sem, rec_done[a].at(e))
                act.wait_ge(rb_done[a].sem, rb_done[a].at(e - 1))
                nc.scalar.activation(rec_h[a][:], rec[a][:], ACT.Copy).then_inc(rec_hi[a].sem, 1)

            def out_hi_part(a, e):
                act.wait_ge(o_norm[a].sem, o_norm[a].at(e))
                act.wait_ge(oproj_done[a].sem, oproj_done[a].at(e - 1))
                nc.scalar.activation(o_h[a][:].rearrange("p a b -> p (a b)"),
                                     o_c[a][:].rearrange("p a b -> p (a b)"), ACT.Copy).then_inc(o_hi[a].sem, 1)

            def gelu(m, e):
                act.wait_ge(ff1_done.sem, ff1_done.at(e, m + 1))
                if m >= 2:
                    act.wait_ge(ffl_done.sem, ffl_done.at(e, m - 1))
                else:
                    act.wait_ge(ffl_done.sem, ffl_done.at(e - 1, NM - 1 + m))
                nc.scalar.activation(ff_g[:, m % 2], ps_f1[:, N:2 * N], ACT.Gelu, scale=sc[:, D3:D3 + 1],
                                     bias=cvec[:, C_W1 + NM + m:C_W1 + NM + m + 1]).then_inc(gelu_done.sem, 1)

            def ff_hi(m, e):
                act.wait_ge(ffp_done.sem, ffp_done.at(e, m + 1))
                if m >= 2:
                    act.wait_ge(ff2_step.sem, ff2_step.at(e, m - 1))
                else:
                    act.wait_ge(ff2_step.sem, ff2_step.at(e - 1, NM - 1 + m))
                nc.scalar.activation(ff_h[:, m % 2], ff_g[:, m % 2], ACT.Copy).then_inc(ffh_done.sem, 1)

            def step(i):
                on, tab = streams_of(i), ring(streams_of(i), before_of(i))
                ptab = probs_ring(streams_of(i), before_of(i))

                for T in range(NT):
                    if SELF in on:
                        exps(0, T, i, i, tab["st", T][0], ptab)
                    if T == 6 and CROSS in on:
                        max_row(1, i - 1, tab["mt", 1][0])
                    if QKV in on and T >= 6:
                        qk_hi_part(T - 6, i + 1)
                    if SELF in on and T == 7:
                        ct_hi_part(i, tab["ct", 0][0])
                for g in range(NG):
                    if g == NG - 1 and SELF in on:
                        rec_hi_part(0, i)
                    if CROSS in on:
                        exps(1, g, i - 1, i, tab["st2", g][0], ptab)
                    if g == 0 and QKV in on:
                        qk_hi_part(4, i + 1)
                if NORM1 in on:
                    tr_hi_part(0, i + 2, tab["tr", 0][0])
                if FFN in on:
                    load_table(ACT.Gelu, gelu_table, i - 2)
                    gelu(0, i - 2)
                if SELF in on:
                    out_hi_part(0, i)
                if FFN in on:
                    ff_hi(0, i - 2)
                if SELF in on:
                    k2_hi_part(i, tab["kv2", 0][0])
                if FFN in on:
                    gelu(1, i - 2)
                if CROSS in on:
                    rec_hi_part(1, i - 1)
                if FFN in on:
                    ff_hi(1, i - 2)
                if CROSS in on:
                    out_hi_part(1, i - 1)
                for m in range(2, NM):
                    if FFN in on:
                        gelu(m, i - 2)
                    if m == MT_AT and QKV in on:
                        max_row(0, i + 1, tab["mt", 0][0])
                    if FFN in on:
                        ff_hi(m, i - 2)
                    if m == 3 and SELF in on:
                        tr_hi_part(1, i, tab["tr", 1][0])
                    if m == 4 and SELF in on:
                        q2_hi_part(i, tab["q2", 0][0])
                    if m == TR2_AT and CROSS in on:
                        tr_hi_part(2, i - 1, tab["tr", 2][0])
                if QKV in on:
                    load_table(ACT.Exp, exp_table, i + 1)

            run_steps(act, step)

        @block.tensor
        def _(pe):
            mm = nc.tensor.matmul
            pe.wait_ge(vec_loaded.sem, 16 * NVEC_LOADS)
            for n in range(len(CTXCH), len(CTXCH) + LNMATS):
                _, _, _, cw, ln, _ = CHUNKS[n]
                pe.wait_ge(staged[n % NSTAGE].sem, staged[n % NSTAGE].at(0, stage_value[n]))
                w = stage_buf(n)[:, 0:3 * cw].rearrange("p (s c) -> p s c", s=3)
                for c0, c1, r0, col in c_places(n):
                    for s in range(3):
                        k = P if s < 2 else 64
                        last = mm(ps[r0:r0 + c1 - c0, 0, col:col + 1], w[0:k, s, c0:c1],
                                  gb[0:k, 2 * ln + 1, s:s + 1], start=(s == 0), stop=(s == 2))
                last.then_inc(pro_pe.sem, 1)
            pe.wait_ge(staged[(N1 - 1) % NSTAGE].sem, staged[(N1 - 1) % NSTAGE].at(0, stage_value[N1 - 1]))
            pe.wait_ge(cv_ready.sem, cv_ready.at(0))
            w = stage_buf(N1 - 1).rearrange("p (s c) -> p s c", s=3)
            for s in range(3):
                k = P if s < 2 else 64
                last = mm(ps[:, 1, 0:D], cv_rep[0:k, s, :], w[0:k, s, :], start=(s == 0), stop=(s == 2))
            last.then_inc(pro_pe.sem, 1)
            pe.wait_ge(maxima.sem, maxima.at(0, 1))
            mm(ps[0:8, 2, 0:P], mxm[:], ident[:], start=True, stop=True).then_inc(pro_pe.sem, 1)
            pe.wait_ge(maxima.sem, maxima.at(0, 2))
            mm(ps[:, 3, 0:8], ones[:], mxd[:], start=True, stop=True).then_inc(pro_pe.sem, 1)
            pe.wait_ge(pro.sem, pro.at(0, PRO_DONE))

            def take(tab, name, i):
                s, prior = tab[name]
                if prior:
                    freed, step_offset, count = prior
                    pe.wait_ge(freed.sem, freed.at(i + step_offset, count))
                return s

            def transposes(k, e, s):
                pe.wait_ge(ln_done[k].sem, ln_done[k].at(e))
                for c in range(3):
                    for q in range(KT):
                        last = nc.tensor.transpose(flat[s][:, c * N + q * P:c * N + (q + 1) * P],
                                                   xhat[:, q, c * P:(c + 1) * P], ident[:])
                last.then_inc(tr_done[k].sem, 1)

            def product(dst, pairs):
                for n, (lhs, rhs) in enumerate(pairs):
                    last = mm(dst, lhs, rhs, start=(n == 0), stop=(n == len(pairs) - 1))
                return last

            def by_feature(dst, wh, wl, c0, c1, xh, xl, full=2):
                pairs = split_passes(xh, xl, wh[:, :, c0:c1], wl[:, :, c0:c1], full)
                return product(dst, [(w, x) for x, w in pairs])

            def by_token(dst, wh, wl, c0, c1, xh, xl, full=2):
                return product(dst, split_passes(xh, xl, wh[:, :, c0:c1], wl[:, :, c0:c1], full))

            def qk(m, e, on):
                if m == 0:
                    if CROSS in on:
                        pe.wait_ge(max2_red.sem, max2_red.at(e - 2))
                    pe.wait_ge(tr_lo[0].sem, tr_lo[0].at(e))
                    pe.wait_ge(out_ready.sem, out_ready.at(e - 4))
                    pe.wait_ge(v_copied.sem, v_copied.at(e - 1))
                    pe.wait_ge(qk_lo.sem, qk_lo.at(e - 1))
                if m >= 2:
                    pe.wait_ge(qk_lo.sem, qk_lo.at(e, m - 1))
                by_feature(ps_f2[m % 2][:, 0:N], wqkv_h, wqkv_l,
                           m * P, (m + 1) * P, ah[0], al[0]).then_inc(qk_done.sem, 1)

            def values(q, e):
                pe.wait_ge(qk_lo.sem, qk_lo.at(e, 4 + q))
                by_token(ps_f2[1 - q][:, 0:D], wqkv_h, wqkv_l, 2 * D, 3 * D,
                         ah[0][:, :, q * P:(q + 1) * P], al[0][:, :, q * P:(q + 1) * P]).then_inc(v_done.sem, 1)

            def maxima1(n, e, s):
                T = MAX_ORDER[n]
                pe.wait_ge(spread[T % 4].sem, spread[T % 4].at(e))
                for h in range(2):
                    for q in range(KT):
                        last = mm(flat[s][:, (2 * h + q) * N:(2 * h + q + 1) * N],
                                  q4[64 * h:64 * h + 63, T, q * P:(q + 1) * P],
                                  k4[64 * h:64 * h + 63, T, :], start=True, stop=True)
                last.then_inc(max_done.sem, 1)

            def maxima2(n, e, on):
                T0, nt = MAX2_PAIRS[n]
                if n == 0:
                    pe.wait_ge(out_ready.sem, out_ready.at(e - 2))
                    if SELF in on:
                        pe.wait_ge(v_copied.sem, v_copied.at(e + 1))
                        pe.wait_ge(qk_lo.sem, qk_lo.at(e + 1))
                    pe.wait_ge(q2_spread.sem, q2_spread.at(e))
                    pe.wait_ge(k2_spread.sem, k2_spread.at(e))
                for h in range(2):
                    if n:
                        pe.wait_ge(max2_red.sem, max2_red.at(e, 2 * n - 1 + h))
                    for T in range(T0, T0 + nt):
                        for q in range(KT):
                            c = ((T - T0) * KT + q) * J
                            last = mm(ps_f2[h][:, c:c + J], q42[64 * h:64 * h + 63, T, q * P:(q + 1) * P],
                                      k42[64 * h:64 * h + 63, T, :], start=True, stop=True)
                    last.then_inc(max2_done.sem, 1)

            def max_turn(a, e, s):
                reduced = (max_red, max2_red)[a]
                pe.wait_ge(reduced.sem, reduced.at(e))
                for q in range(KT):
                    last = mm(flat[s][0:H, q * P:(q + 1) * P],
                              m_q[a][:, :, :, q].rearrange("p h t -> p (h t)"), ident[:], start=True, stop=True)
                last.then_inc(mt_done[a].sem, 1)

            def scores1(T, e, s):
                if T == 0:
                    pe.wait_ge(m_spread[0].sem, m_spread[0].at(e))
                for h in range(2):
                    for k in range(KT):
                        last = mm(flat[s][:, (2 * h + k) * N:(2 * h + k + 1) * N],
                                  k4[64 * h:64 * h + 64, T, k * P:(k + 1) * P],
                                  q4[64 * h:64 * h + 64, T, :], start=True, stop=True)
                last.then_inc(st_done[0].sem, 1)

            def scores2(g, e, s):
                if g == 0:
                    pe.wait_ge(m_spread[1].sem, m_spread[1].at(e))
                for h in range(2):
                    for u in range(2):
                        last = mm(slot[s][0:J, h, u * N:(u + 1) * N],
                                  k42[64 * h:64 * h + 64, 2 * g + u, :],
                                  q42[64 * h:64 * h + 64, 2 * g + u, :], start=True, stop=True)
                last.then_inc(st_done[1].sem, 1)

            def take_pv(a, g, i, bank_of):
                b, prior = bank_of[a, g]
                if prior:
                    freed, step_offset, count = prior
                    pe.wait_ge(freed.sem, freed.at(i + step_offset, count))
                pe.wait_ge(ffp_done.sem, ffp_done.at(i - 3))
                return ps_pv[b]

            def values1(g, e, dst, ptab):
                pe.wait_ge(exp_done[0].sem, exp_done[0].at(e, 2 * g + 2))
                if g == 0:
                    pe.wait_ge(v_copied.sem, v_copied.at(e))
                for k in range(KT):
                    for r in range(4):
                        T, h = 2 * g + r // 2, r % 2
                        last = mm(dst[32 * r:32 * r + 32, 0:N], v1[:, k, 4 * g + r, :],
                                  probs[:, ptab[0, T][0], (2 * h + k) * N:(2 * h + k + 1) * N],
                                  start=(k == 0), stop=(k == KT - 1), tile_position=(0, 32 * r))
                last.then_inc(pv_done[0].sem, 1)

            def values2(g, e, dst, ptab):
                pe.wait_ge(exp_done[1].sem, exp_done[1].at(e, g + 1))
                if g == 0:
                    pe.wait_ge(v2_copied.sem, v2_copied.at(e))
                for r in range(4):
                    u, h = r // 2, r % 2
                    last = mm(dst[32 * r:32 * r + 32, 0:N], v2[:, 4 * g + r, :],
                              probs[0:J, ptab[1, g][0], (2 * h + u) * N:(2 * h + u + 1) * N],
                              start=True, stop=True, tile_position=(0, 32 * r))
                last.then_inc(pv_done[1].sem, 1)

            def spread_rec(a, e, s):
                pe.wait_ge(rec_lo[a].sem, rec_lo[a].at(e))
                for c in range(3):
                    last = product(flat[s][:, c * N:(c + 1) * N],
                                   [(sel[:, c * P:(c + 1) * P], rec_h[a][:]), (sel[:, c * P:(c + 1) * P], rec_l[a][:])])
                last.then_inc(rb_done[a].sem, 1)

            def out_proj(a, e, s):
                pe.wait_ge(o_lo[a].sem, o_lo[a].at(e))
                wh, wl = ((wo1_h, wo1_l), (wo2_h, wo2_l))[a]
                for q in range(KT):
                    last = by_token(slot[s][:, q, 0:D], wh, wl, 0, D,
                                    o_h[a][:, :, q * P:(q + 1) * P], o_l[a][:, :, q * P:(q + 1) * P])
                last.then_inc(oproj_done[a].sem, 1)

            def ctx_turn(e, s):
                pe.wait_ge(c_loaded.sem, c_loaded.at(e))
                for c in range(2):
                    last = nc.tensor.transpose(flat[s][:, c * J:(c + 1) * J], c_in[:, c * P:(c + 1) * P],
                                               ident[0:J, 0:J])
                last.then_inc(ct_done.sem, 1)

            def kv2(e, s):
                pe.wait_ge(ct_lo.sem, ct_lo.at(e))
                for m in range(3):
                    c0, c1 = m * P, min((m + 1) * P, D)
                    by_feature(flat[s][0:c1 - c0, m * J:(m + 1) * J], wkv2_h, wkv2_l, c0, c1, ct_h, ct_l, 1)
                by_token(slot[s][0:J, 1, 0:D], wkv2_h, wkv2_l, D, 2 * D, ct_h, ct_l, 1).then_inc(kv2_done.sem, 1)

            def q2(e, s):
                pe.wait_ge(tr_lo[1].sem, tr_lo[1].at(e))
                for m in range(3):
                    c0, c1 = m * P, min((m + 1) * P, D)
                    last = by_feature(flat[s][0:c1 - c0, m * N:(m + 1) * N], wq2_h, wq2_l, c0, c1, ah[1], al[1])
                last.then_inc(q2_done.sem, 1)

            def ff1(m, e, bank_of):
                if m == 0:
                    for a, g in [use for use, (b, _) in bank_of.items() if ps_pv[b] is ps_f1][-1:]:
                        pe.wait_ge(o_copied[a].sem, o_copied[a].at(e + 2 - a, g + 1))
                    pe.wait_ge(tr_lo[2].sem, tr_lo[2].at(e))
                    pe.wait_ge(ffp_done.sem, ffp_done.at(e - 1))
                else:
                    pe.wait_ge(ffp_done.sem, ffp_done.at(e, m))
                by_feature(ps_f1[:, 0:N], w1_h, w1_l, m * P, (m + 1) * P, ah[2], al[2])
                by_feature(ps_f1[:, N:2 * N], w1_h, w1_l, FF + m * P, FF + (m + 1) * P,
                           ah[2], al[2]).then_inc(ff1_done.sem, 1)

            def ff2(m, e, on):
                if m == 0:
                    if QKV in on:
                        pe.wait_ge(qk_lo.sem, qk_lo.at(e + 3))
                        pe.wait_ge(v_copied.sem, v_copied.at(e + 3))
                    pe.wait_ge(out_ready.sem, out_ready.at(e - 1))
                pe.wait_ge(ffl_done.sem, ffl_done.at(e, m + 1))
                for q in range(KT):
                    xh, xl = ff_h[:, m % 2, q * P:(q + 1) * P], ff_l[:, m % 2, q * P:(q + 1) * P]
                    pairs = [(xh, w2_h[:, m, :]), (xl, w2_h[:, m, :]), (xh, w2_l[:, m, :])]
                    for n, (lhs, rhs) in enumerate(pairs):
                        last = mm(ps_f2[q][:, 0:D], lhs, rhs, start=(m == 0 and n == 0), stop=(m == NM - 1 and n == 2))
                last.then_inc(ff2_step.sem, 1)

            def step(i):
                on, tab = streams_of(i), ring(streams_of(i), before_of(i))
                ptab = probs_ring(streams_of(i), before_of(i))
                bank_of = pv_ring(streams_of(i), before_of(i))

                def tile(m):
                    if FFN in on:
                        ff1(m, i - 2, bank_of)
                    if FFN in on and m > 0:
                        ff2(m - 1, i - 2, on)

                def pairs_maxima(key):
                    if QKV in on:
                        for n in MAX_AT.get(key, ()):
                            maxima1(n, i + 1, take(tab, ("max", n), i))

                if LAST in on:
                    ff2(NM - 1, i - 3, on)
                for T in range(NT):
                    if SELF in on:
                        scores1(T, i, take(tab, ("st", T), i))
                    if CROSS in on and 1 <= T <= 4:
                        maxima2(T - 1, i - 1, on)
                    if CROSS in on and T == 6:
                        max_turn(1, i - 1, take(tab, ("mt", 1), i))
                    if QKV in on and T >= 6:
                        qk(T - 6, i + 1, on)
                    if SELF in on and T == 7:
                        ctx_turn(i, take(tab, ("ct", 0), i))
                    if SELF in on and T % 2 and T > 1:
                        values1(T // 2 - 1, i, take_pv(0, T // 2 - 1, i, bank_of), ptab)
                for g in range(NG):
                    if CROSS in on:
                        scores2(g, i - 1, take(tab, ("st2", g), i))
                    if g == 0 and SELF in on:
                        values1(NG - 1, i, take_pv(0, NG - 1, i, bank_of), ptab)
                    if g == 1 and QKV in on:
                        qk(4, i + 1, on)
                    if g in (2, 3) and QKV in on:
                        values(g - 2, i + 1)
                    if g == NG - 1 and NORM1 in on:
                        transposes(0, i + 2, take(tab, ("tr", 0), i))
                    if g >= 1 and CROSS in on:
                        values2(g - 1, i - 1, take_pv(1, g - 1, i, bank_of), ptab)
                if SELF in on:
                    spread_rec(0, i, take(tab, ("rb", 0), i))
                if CROSS in on:
                    values2(NG - 1, i - 1, take_pv(1, NG - 1, i, bank_of), ptab)
                tile(0)
                if SELF in on:
                    kv2(i, take(tab, ("kv2", 0), i))
                tile(1)
                if SELF in on:
                    out_proj(0, i, take(tab, ("oproj", 0), i))
                if CROSS in on:
                    spread_rec(1, i - 1, take(tab, ("rb", 1), i))
                tile(2)
                if CROSS in on:
                    out_proj(1, i - 1, take(tab, ("oproj", 1), i))
                pairs_maxima("oproj")
                tile(3)
                pairs_maxima(3)
                if SELF in on:
                    transposes(1, i, take(tab, ("tr", 1), i))
                pairs_maxima("tr")
                tile(4)
                if SELF in on:
                    q2(i, take(tab, ("q2", 0), i))
                pairs_maxima("q2")
                for m in range(5, NM):
                    tile(m)
                    pairs_maxima(m)
                    if m == MT_AT and QKV in on:
                        max_turn(0, i + 1, take(tab, ("mt", 0), i))
                    if m == TR2_AT and CROSS in on:
                        transposes(2, i - 1, take(tab, ("tr", 2), i))

            run_steps(pe, step)

        @block.vector
        def _(dve):
            V = nc.vector
            chained = [0]

            def link(ins):
                chained[0] += 1
                ins.then_inc(pro_dve.sem, 1)
                dve.wait_ge(pro_dve.sem, pro_dve.at(0, chained[0]))

            for tile_, value in ((q4, 0.0), (k4, 0.0), (q42, 0.0), (k42, 0.0), (v1, 1.0), (v2, 1.0),
                                 (ones, 1.0), (mx, 0.0), (mxm, 0.0), (cvec, 0.0)):
                last = V.memset(tile_[:], value)
            link(last)
            V.memset(sc[:], 0.0).then_inc(pro.sem, 1)
            dve.wait_ge(pro.sem, pro.at(0, 1))
            dve.wait_ge(vec_loaded.sem, 16 * NVEC_LOADS)
            V.tensor_copy(sel[:], sel_f)
            for n in range(N1):
                ch = CHUNKS[n]
                dve.wait_ge(staged[n % NSTAGE].sem, staged[n % NSTAGE].at(0, stage_value[n]))
                if ch[0] == "ctx":
                    V.tensor_reduce(mx[0:J, MXCOL[n]:MXCOL[n] + 1], stage_buf(n)[0:J, 0:ch[2] * CTX], AX.X, ALU.max,
                                    apply_absolute_value=True).then_inc(stage_used.sem, 1)
                    continue
                _, name, c0, cw, ln, _ = ch
                ns = slices(t[name].shape[0])
                src = stage_buf(n)[:, 0:ns * cw]
                if ln is not None:
                    dve.wait_ge(stage_used.sem, stage_used.at(0, n))
                    for s in range(ns):
                        last = V.tensor_scalar(tmp[:, s * cw:(s + 1) * cw], src[:, s * cw:(s + 1) * cw],
                                               gb[:, 2 * ln, s:s + 1], None, ALU.mult)
                    link(last)
                    src = tmp[:, 0:ns * cw]
                    dve.wait_ge(pro_pe.sem, pro_pe.at(0, n - len(CTXCH) + 1))
                if n == N1 - 1:
                    dve.wait_ge(pro_pe.sem, pro_pe.at(0, LNMATS + 1))
                red = V.tensor_reduce(mx[:, MXCOL[n]:MXCOL[n] + 1], src, AX.X, ALU.max, apply_absolute_value=True)
                red.then_inc(stage_used.sem, 1)
                if n == len(CTXCH) + LNMATS - 1:
                    V.tensor_copy(cvec[:, 0:C_V + 2], ps[:, 0, 0:C_V + 2])
                    V.tensor_copy(cvec[0:64, C_V + 2:C_V + 3], ps[0:64, 0, C_V + 2:C_V + 3])
                    V.tensor_copy(cvec[:, C_Q2:C_Q2 + 2], ps[:, 0, C_Q2:C_Q2 + 2])
                    V.tensor_copy(cvec[0:64, C_Q2 + 2:C_W1], ps[0:64, 0, C_Q2 + 2:C_W1])
                    link(V.tensor_copy(cvec[:, C_W1:C_W1 + 2 * NM], ps[:, 0, C_W1:C_W1 + 2 * NM]))
                    for s in range(3):
                        last = V.tensor_scalar(cv_rep[:, s, :], ident[:], 0.0, cvec[:, C_V + s:C_V + s + 1],
                                               ALU.mult, ALU.add)
                    last.then_inc(cv_ready.sem, 1)
                    for c0, c1, col in ((C_QK, C_QK + 5, MXCOL["qk"]), (C_Q2, C_Q2 + 3, MXCOL["q2"])):
                        last = V.tensor_reduce(mx[:, col:col + 1], cvec[:, c0:c1], AX.X, ALU.max,
                                               apply_absolute_value=True)
                    link(last)
                    for col in (MXCOL["qk"], MXCOL["q2"]):
                        last = V.tensor_scalar(mx[:, col:col + 1], mx[:, col:col + 1], 1.0 / 128, None, ALU.mult)
                    link(last)
            dve.wait_ge(stage_used.sem, stage_used.at(0, N1))
            V.tensor_tensor(bias1[:], bias1[:], ps[:, 1, 0:D], ALU.add)
            for gidx, (c0, c1) in enumerate(MXGROUPS):
                last = V.tensor_reduce(mxm[:, gidx:gidx + 1], mx[:, c0:c1], AX.X, ALU.max)
            last.then_inc(maxima.sem, 1)
            dve.wait_ge(pro_pe.sem, pro_pe.at(0, LNMATS + 2))
            link(V.tensor_reduce(mxr[:, 0:1], ps[0:8, 2, 0:P], AX.X, ALU.max))
            link(V.tensor_scalar(mxr[:, 1:2], mxr[:, 0:1], 1e-30, None, ALU.max))
            link(V.tensor_scalar(mxr[:, 2:3].bitcast(u32), mxr[:, 1:2].bitcast(u32), 0x7F800000, None,
                                 ALU.bitwise_and))
            link(V.reciprocal(mxr[:, 3:4], mxr[:, 2:3]))
            V.tensor_scalar(mxd[:], ident[0:8, 0:8], mxr[:, 3:4], None, ALU.mult).then_inc(maxima.sem, 1)
            dve.wait_ge(pro_pe.sem, pro_pe.at(0, LNMATS + 3))
            link(V.tensor_scalar(sc[:, 0:7], ps[:, 3, 0:7], 4.0, None, ALU.mult))
            link(V.tensor_scalar(sc[:, S_CTX:S_CTX + 1], sc[:, S_CTX:S_CTX + 1], 2.0, None, ALU.mult))
            link(V.reciprocal(rp[:, 0:7], sc[:, 0:7]))

            def inverse(k):
                return rp[:, k:k + 1]

            def put(dst, a, b, c):
                link(V.tensor_scalar(sc[:, dst:dst + 1], a, b, c, ALU.mult, ALU.mult))

            put(E1, inverse(S_QKV), DH ** -0.5, inverse(S_QKV))
            put(T0, inverse(S_KV2), 1.0, inverse(S_CTX))
            put(E2, inverse(S_Q2), DH ** -0.5, sc[:, T0:T0 + 1])
            put(D1, inverse(S_QKV), 1.0, inverse(S_O1))
            put(D2, inverse(S_O2), 1.0, sc[:, T0:T0 + 1])
            put(D3, inverse(S_W1), 1.0, 1.0)
            V.tensor_scalar(cvec[:, 0:C_Q2], cvec[:, 0:C_Q2], sc[:, S_QKV:S_QKV + 1], None, ALU.mult)
            V.tensor_scalar(cvec[:, C_Q2:C_W1], cvec[:, C_Q2:C_W1], sc[:, S_Q2:S_Q2 + 1], None, ALU.mult)
            link(V.tensor_tensor(cvec[:, C_W1:C_W1 + 2 * NM], cvec[:, C_W1:C_W1 + 2 * NM], b1c[:], ALU.add))
            link(V.tensor_scalar(cvec[:, C_W1:C_W1 + NM], cvec[:, C_W1:C_W1 + NM], sc[:, S_W1:S_W1 + 1], None, ALU.mult))
            for n in range(N1, len(CHUNKS)):
                ch = CHUNKS[n]
                dve.wait_ge(staged[n % NSTAGE].sem, staged[n % NSTAGE].at(0, stage_value[n]))
                if ch[0] == "cut":
                    _, name, c0, cw, ln, scale = ch
                    ns = slices(t[name].shape[0])
                    wh, wl, off = DEST[name]
                    wh, wl = wh[:, 0:ns, off + c0:off + c0 + cw], wl[:, 0:ns, off + c0:off + c0 + cw]
                    s_ap = sc[:, scale:scale + 1]
                else:
                    _, s0, ns = ch
                    cw, ln, s_ap = D, None, 1.0
                    wh, wl = w2_h[:, s0:s0 + ns, :].bitcast(f32), w2_l[:, s0:s0 + ns, :]
                if n > N1:
                    dve.wait_ge(stage_used.sem, stage_used.at(0, n))
                if ln is not None:
                    for s in range(ns):
                        last = V.tensor_scalar(tmp[:, s * cw:(s + 1) * cw], stage_buf(n)[:, s * cw:(s + 1) * cw],
                                               gb[:, 2 * ln, s:s + 1], s_ap, ALU.mult, ALU.mult)
                else:
                    last = V.tensor_scalar(tmp[:, 0:ns * cw], stage_buf(n)[:, 0:ns * cw], s_ap, None, ALU.mult)
                last.then_inc(c_product.sem, 1)
                dve.wait_ge(c_product.sem, c_product.at(0, n - N1 + 1))
                dve.wait_ge(pro_hi.sem, pro_hi.at(0, n - N1 + 1))
                V.tensor_tensor(wl, tmp[:, 0:ns * cw].rearrange("p (s c) -> p s c", s=ns), wh,
                                ALU.subtract).then_inc(stage_used.sem, 1)
            dve.wait_ge(stage_used.sem, stage_used.at(0, len(CHUNKS)))
            V.memset(mxm[:, 0:1], 0.0).then_inc(pro.sem, 1)

            def layer_norm(k, e):
                src = (x_in, x1, x2)[k]
                if k == 0:
                    dve.wait_ge(x_loaded.sem, x_loaded.at(e))
                else:
                    dve.wait_ge(resid[k - 1].sem, resid[k - 1].at(e))
                for q in range(KT):
                    last = V.bn_stats(stats[k][:, q, :], src[:, q, :])
                last.then_inc(ln_stat[k].sem, 1)
                dve.wait_ge(ln_stat[k].sem, ln_stat[k].at(e, 1))
                V.tensor_copy(pace[:], stats[k][:, 0, 0:1])
                for q in range(KT):
                    last = V.bn_aggr(mv[k][:, q, :], stats[k][:, q, :])
                last.then_inc(ln_stat[k].sem, 1)
                dve.wait_ge(ln_stat[k].sem, ln_stat[k].at(e, 2))
                dve.wait_ge(ln_rstd[k].sem, ln_rstd[k].at(e - 1))
                V.tensor_scalar(ve[k][:], mv[k][:, :, 1], EPS, None, ALU.add).then_inc(ln_stat[k].sem, 1)

            def normalise(k, e, i):
                src = (x_in, x1, x2)[k]
                dve.wait_ge(ln_rstd[k].sem, ln_rstd[k].at(e))
                prior = ring(streams_of(i), before_of(i), XHAT, 1)[k][1]
                if prior:
                    freed, step_offset, count = prior
                    dve.wait_ge(freed.sem, freed.at(i + step_offset, count))
                for q in range(KT):
                    V.tensor_scalar(xhat[:, q, 0:D], src[:, q, :], mv[k][:, q, 0:1], rs[k][:, q:q + 1],
                                    ALU.subtract, ALU.mult)
                for q in range(KT):
                    last = V.tensor_scalar(xhat[:, q, D:3 * P], src[:, q, 2 * P:D], mv[k][:, q, 0:1],
                                           rs[k][:, q:q + 1], ALU.subtract, ALU.mult)
                last.then_inc(ln_done[k].sem, 1)

            def tr_lo_part(k, e, s):
                dve.wait_ge(tr_hi[k].sem, tr_hi[k].at(e))
                V.tensor_tensor(al[k][:].rearrange("p a b -> p (a b)"), flat[s][:, 0:2 * N],
                                ah[k][:, 0:2].rearrange("p a b -> p (a b)"), ALU.subtract)
                V.tensor_tensor(ah[k][64:P, 2], flat[s][64:P, 2 * N:3 * N], ah[k][64:P, 2],
                                ALU.subtract).then_inc(tr_lo[k].sem, 1)

            def qk_lo_part(m, e):
                dve.wait_ge(qk_hi.sem, qk_hi.at(e, m + 1))
                V.scalar_tensor_tensor(qk_l[:, m, :], ps_f2[m % 2][:, 0:N], cvec[:, C_QK + m:C_QK + m + 1],
                                       qk_h[:, m, :], ALU.add, ALU.subtract).then_inc(qk_lo.sem, 1)

            def v_copy(q, e):
                dve.wait_ge(v_done.sem, v_done.at(e, q + 1))
                dve.wait_ge(pv_done[0].sem, pv_done[0].at(e - 1))
                V.tensor_copy(v1[:, q, :, 0:2 * DH:2],
                              ps_f2[1 - q][:, 0:D].rearrange("p (h d) -> p h d", d=DH)).then_inc(v_copied.sem, 1)

            def out_copy(a, g, e, bank_of):
                dve.wait_ge(pv_done[a].sem, pv_done[a].at(e, g + 1))
                if g == 0:
                    dve.wait_ge(o_spread[a].sem, o_spread[a].at(e - 1))
                    dve.wait_ge(den_spread[a].sem, den_spread[a].at(e - 1))
                V.tensor_copy(o_raw[a][:, g, :], ps_pv[bank_of[a, g][0]][:, 0:N]).then_inc(o_copied[a].sem, 1)

            def q2_lo_part(e, s):
                dve.wait_ge(q2_hi.sem, q2_hi.at(e))
                for m in range(3):
                    r = P if m < 2 else 64
                    last = V.scalar_tensor_tensor(q2_l[0:r, m, :], flat[s][0:r, m * N:(m + 1) * N],
                                                  cvec[0:r, C_Q2 + m:C_Q2 + m + 1], q2_h[0:r, m, :],
                                                  ALU.add, ALU.subtract)
                last.then_inc(q2_lo.sem, 1)

            def ct_lo_part(e, s):
                dve.wait_ge(ct_hi.sem, ct_hi.at(e))
                V.scalar_tensor_tensor(ct_l[:, 0, :], flat[s][:, 0:J], sc[:, S_CTX:S_CTX + 1], ct_h[:, 0, :],
                                       ALU.mult, ALU.subtract)
                V.scalar_tensor_tensor(ct_h[64:P, 1, :], flat[s][64:P, J:2 * J], sc[64:P, S_CTX:S_CTX + 1],
                                       ct_h[64:P, 1, :], ALU.mult, ALU.subtract).then_inc(ct_lo.sem, 1)

            def kv2_parts(e, s):
                dve.wait_ge(k2_hi.sem, k2_hi.at(e))
                V.tensor_tensor(k2_l[:, 0:2, :].rearrange("p a b -> p (a b)"), flat[s][:, 0:2 * J],
                                k2_h[:, 0:2, :].rearrange("p a b -> p (a b)"), ALU.subtract)
                V.tensor_tensor(k2_l[0:64, 2, :], flat[s][0:64, 2 * J:3 * J], k2_h[0:64, 2, :],
                                ALU.subtract).then_inc(k2_lo.sem, 1)
                dve.wait_ge(pv_done[1].sem, pv_done[1].at(e - 1))
                V.tensor_copy(v2[:, :, 0:2 * DH:2],
                              slot[s][0:J, 1, 0:D].rearrange("p (h d) -> p h d", d=DH)).then_inc(v2_copied.sem, 1)

            def reduce1(n, e, s):
                dve.wait_ge(max_done.sem, max_done.at(e, n + 1))
                if n == 0:
                    dve.wait_ge(mt_done[0].sem, mt_done[0].at(e - 1))
                V.tensor_reduce(m_q[0][:, :, MAX_ORDER[n], :], flat[s].rearrange("p (g k) -> p g k", k=N),
                                AX.X, ALU.max, negate=True).then_inc(max_red.sem, 1)

            def reduce2(n, e):
                T0, nt = MAX2_PAIRS[n]
                for h in range(2):
                    dve.wait_ge(max2_done.sem, max2_done.at(e, 2 * n + h + 1))
                    if n == 0 and h == 0:
                        dve.wait_ge(mt_done[1].sem, mt_done[1].at(e - 1))
                    V.tensor_reduce(m_q[1][:, h, T0:T0 + nt, :].rearrange("p t q -> p (t q)"),
                                    ps_f2[h][:, 0:nt * KT * J].rearrange("p (g k) -> p g k", k=J),
                                    AX.X, ALU.max, negate=True).then_inc(max2_red.sem, 1)

            def reciprocal(a, e):
                dve.wait_ge(den_spread[a].sem, den_spread[a].at(e))
                dve.wait_ge(rec_lo[a].sem, rec_lo[a].at(e - 1))
                V.reciprocal(rec[a][:], den[a][:]).then_inc(rec_done[a].sem, 1)

            def rec_lo_part(a, e):
                dve.wait_ge(rec_hi[a].sem, rec_hi[a].at(e))
                V.tensor_tensor(rec_l[a][:], rec[a][:], rec_h[a][:].bitcast(f32), ALU.subtract).then_inc(rec_lo[a].sem, 1)

            def out_norm(a, e, s):
                dve.wait_ge(o_spread[a].sem, o_spread[a].at(e))
                dve.wait_ge(rb_done[a].sem, rb_done[a].at(e))
                c = o_c[a][:].rearrange("p a b -> p (a b)")
                V.tensor_tensor(c, c, flat[s][:, 0:3 * N], ALU.mult).then_inc(o_norm[a].sem, 1)

            def residual(a, e, s):
                dve.wait_ge(oproj_done[a].sem, oproj_done[a].at(e))
                dve.wait_ge(xb_done[a].sem, xb_done[a].at(e))
                dve.wait_ge(xb_done[a + 1].sem, xb_done[a + 1].at(e - 1))
                dst, xb = ((x1, xb1), (x2, xb2))[a]
                V.scalar_tensor_tensor(dst[:], slot[s][:, :, 0:D], sc[:, D1 + a:D1 + a + 1], xb[:],
                                       ALU.mult, ALU.add).then_inc(resid[a].sem, 1)

            def move_x(e):
                dve.wait_ge(xb0_done.sem, xb0_done.at(e))
                dve.wait_ge(resid[0].sem, resid[0].at(e - 1))
                V.tensor_copy(xb1[:], xb0[:]).then_inc(xb_done[0].sem, 1)

            def ff_product(m, e):
                dve.wait_ge(gelu_done.sem, gelu_done.at(e, m + 1))
                if m >= 2:
                    dve.wait_ge(ffl_done.sem, ffl_done.at(e, m - 1))
                else:
                    dve.wait_ge(ffl_done.sem, ffl_done.at(e - 1, NM - 1 + m))
                V.scalar_tensor_tensor(ff_g[:, m % 2], ps_f1[:, 0:N], cvec[:, C_W1 + m:C_W1 + m + 1], ff_g[:, m % 2],
                                       ALU.add, ALU.mult).then_inc(ffp_done.sem, 1)

            def output(e):
                dve.wait_ge(ff2_step.sem, ff2_step.at(e))
                dve.wait_ge(xb_done[2].sem, xb_done[2].at(e))
                dve.wait_ge(out_stored.sem, out_stored.at(e - 1))
                V.scalar_tensor_tensor(out_sb[:], ps[:, 6:8, 0:D], sc[:, D3:D3 + 1], xb3[:],
                                       ALU.mult, ALU.add).then_inc(out_ready.sem, 1)

            def step(i):
                on, tab = streams_of(i), ring(streams_of(i), before_of(i))
                bank_of = pv_ring(streams_of(i), before_of(i))

                def tile(m):
                    if FFN in on:
                        ff_product(m, i - 2)

                def pairs_maxima(key):
                    if QKV in on:
                        for n in MAX_AT.get(key, ()):
                            reduce1(n, i + 1, tab["max", n][0])

                for T in range(NT):
                    if LAST in on and T == 0:
                        output(i - 3)
                    if CROSS in on and 1 <= T <= 4:
                        reduce2(T - 1, i - 1)
                    if NORM1 in on and T == 5:
                        layer_norm(0, i + 2)
                    if QKV in on and T >= 6:
                        qk_lo_part(T - 6, i + 1)
                    if SELF in on and T == 7:
                        ct_lo_part(i, tab["ct", 0][0])
                    if SELF in on and T % 2 and T > 1:
                        out_copy(0, T // 2 - 1, i, bank_of)
                    if NORM1 in on and T == 8:
                        normalise(0, i + 2, i)
                if SELF in on:
                    out_copy(0, NG - 1, i, bank_of)
                for g in range(NG):
                    if g == 1 and QKV in on:
                        qk_lo_part(4, i + 1)
                    if g in (2, 3) and QKV in on:
                        v_copy(g - 2, i + 1)
                    if g >= 1 and CROSS in on:
                        out_copy(1, g - 1, i - 1, bank_of)
                    if g == 2 and SELF in on:
                        reciprocal(0, i)
                    if g == 3 and SELF in on:
                        rec_lo_part(0, i)
                if CROSS in on:
                    out_copy(1, NG - 1, i - 1, bank_of)
                if SELF in on:
                    out_norm(0, i, tab["rb", 0][0])
                if NORM1 in on:
                    tr_lo_part(0, i + 2, tab["tr", 0][0])
                tile(0)
                if CROSS in on:
                    reciprocal(1, i - 1)
                if SELF in on:
                    kv2_parts(i, tab["kv2", 0][0])
                tile(1)
                if CROSS in on:
                    rec_lo_part(1, i - 1)
                if SELF in on:
                    residual(0, i, tab["oproj", 0][0])
                if CROSS in on:
                    out_norm(1, i - 1, tab["rb", 1][0])
                if SELF in on:
                    layer_norm(1, i)
                tile(2)
                if SELF in on:
                    normalise(1, i, i)
                if CROSS in on:
                    residual(1, i - 1, tab["oproj", 1][0])
                pairs_maxima("oproj")
                tile(3)
                pairs_maxima(3)
                if SELF in on:
                    tr_lo_part(1, i, tab["tr", 1][0])
                if CROSS in on:
                    layer_norm(2, i - 1)
                pairs_maxima("tr")
                tile(4)
                if QKV in on:
                    move_x(i + 1)
                pairs_maxima("q2")
                if SELF in on:
                    q2_lo_part(i, tab["q2", 0][0])
                for m in range(5, NM):
                    tile(m)
                    pairs_maxima(m)
                    if m == 8 and CROSS in on:
                        normalise(2, i - 1, i)
                    if m == TR2_AT and CROSS in on:
                        tr_lo_part(2, i - 1, tab["tr", 2][0])

            run_steps(dve, step)


_PRE = "L0_xattn_"
_INS = ["n1_g", "n1_b", "q1", "k1", "v1", "o1_w", "o1_b", "n2_g", "n2_b", "q2", "k2", "v2", "o2_w", "o2_b",
        "n3_g", "n3_b", "ff_w1", "ff_b1", "ff_w2", "ff_b2"]


def _constants():
    import numpy as np
    sel = np.zeros((H, 3 * P), np.float32)
    for f in range(3 * P):
        h = (f if f < D else f - 64) // DH
        sel[NG * (h % 4) + h // 4, f] = 1.0
    return {"c_ident": np.eye(P, dtype=np.float32), "c_sel": sel,
            "c_aug": np.full((1, NT * N), AUG, np.float16)}


def kernel(**inputs):
    import numpy as _np
    import concourse.bacc as _bacc
    from concourse import mybir as _mybir
    from concourse.bass_utils import run_bass_kernel_spmd as _run

    nc = _bacc.Bacc("TRN2", target_bir_lowering=False, num_devices=1)
    host = {"x": inputs["x"], "ctx_768": inputs["ctx_768"]}
    host.update({n: inputs[_PRE + n] for n in _INS})
    host.update(_constants())
    arrays, aps = {}, {}
    for name, a in host.items():
        a = _np.ascontiguousarray(a)
        arrays[f"in_{name}"] = a
        aps[name] = nc.dram_tensor(f"in_{name}", a.shape, _mybir.dt.from_np(a.dtype), kind="ExternalInput").ap()
    o = nc.dram_tensor("out_0", (B, N, D), _mybir.dt.float32, kind="ExternalOutput").ap()
    xattn_block(nc, aps, o)
    r = _run(nc, [arrays], core_ids=[0])
    return r.results[0]["out_0"]
```

```python
import concourse.bass as bass
from concourse import mybir
from contextlib import ExitStack

B, N, D = 64, 256, 320
H, DH = 20, 16
J, CTX = 77, 192
FF = 4 * D
EPS = 1e-5
P = 128
KT = N // P
NT = H // 2
NG = H // 4
NM = FF // P
AUG = 32768.0
NC = 4
NP = NG
NSTAGE = 3
STW = 3 * D


def xattn_block(nc, t, out):
    f32, f32r, f16, u32 = mybir.dt.float32, mybir.dt.float32r, mybir.dt.float16, mybir.dt.uint32
    bf16 = mybir.dt.bfloat16
    ACT, ALU, AX = mybir.ActivationFunctionType, mybir.AluOpType, mybir.AxisListType
    ctx = ExitStack()

    def sb(name, shape, dt):
        return ctx.enter_context(nc.sbuf_tensor(name, shape, dt))

    class Event:

        def __init__(self, name, n):
            self.sem, self.n = ctx.enter_context(nc.semaphore(name)), n

        def at(self, e, k=None):
            value = e * self.n + (self.n if k is None else k)
            return max(value, 0) if isinstance(value, int) else value

    with ctx:
        wqkv_h, wqkv_l = sb("wqkv_h", [P, 3, 3 * D], f16), sb("wqkv_l", [P, 3, 3 * D], f16)
        wo1_h, wo1_l = sb("wo1_h", [P, 3, D], f16), sb("wo1_l", [P, 3, D], f16)
        wq2_h, wq2_l = sb("wq2_h", [P, 3, D], f16), sb("wq2_l", [P, 3, D], f16)
        wo2_h, wo2_l = sb("wo2_h", [P, 3, D], f16), sb("wo2_l", [P, 3, D], f16)
        wkv2_h, wkv2_l = sb("wkv2_h", [P, 2, 2 * D], f16), sb("wkv2_l", [P, 2, 2 * D], f16)
        w1_h, w1_l = sb("w1_h", [P, 3, 2 * FF], f16), sb("w1_l", [P, 3, 2 * FF], f16)
        w2_h, w2_l = sb("w2_h", [P, NM, D], f32r), sb("w2_l", [P, NM, D], f32r)
        ident = sb("ident", [P, P], f32)
        sel = sb("sel", [NC * H, NC, 3 * P], bf16)
        ones = sb("ones", [8, P], f32)
        gs = sb("gs", [P, 3, 3], f32)
        gb = sb("gb", [P, 6, 3], f32)
        cvec = sb("cvec", [P, 32], f32)
        b1c = sb("b1c", [P, 2 * NM], f32)
        bias1, bias2, bias3 = (sb(f"bias{k}", [P, D], f32) for k in (1, 2, 3))
        mx = sb("mx", [P, 40], f32)
        mxm = sb("mxm", [P, 8], f32)
        mxr, mxd = sb("mxr", [8, 4], f32), sb("mxd", [8, 8], f32)
        rp = sb("rp", [P, 8], f32)
        sc = sb("sc", [P, 16], f32)
        c_quarter = sb("c_quarter", [NC * H, NC], f32)
        halfneg = sb("halfneg", [P, KT], f32)
        pace = sb("pace", [P, 1], f32)
        x_in, xb1, x1, xb2, x2, xb3, out_sb = (
            sb(n, [P, KT, D], f32) for n in ("x_in", "xb1", "x1", "xb2", "x2", "xb3", "out_sb"))
        sel_f = out_sb[0:NC * H].rearrange("p a b -> p (a b)")[:, 0:3 * P]
        cv_rep = x2[:].rearrange("p a b -> p (a b)")[:, 0:3 * P].rearrange("p (s c) -> p s c", s=3)
        xhat0, xhat12 = sb("xhat0", [P, KT, 3 * P], f32), sb("xhat12", [P, KT, 3 * P], f32)
        xhat = [xhat0, xhat12, xhat12]
        stats = [sb(f"stats{k}", [P, KT, 6], f32) for k in range(3)]
        mv = [sb(f"mv{k}", [P, KT, 2], f32) for k in range(3)]
        ve = [sb(f"ve{k}", [P, KT], f32) for k in range(3)]
        rs = [sb(f"rs{k}", [P, KT], f32) for k in range(3)]
        ah = [sb(f"ah{k}", [P, 3, N], f16) for k in range(3)]
        al = [sb(f"al{k}", [P, 2, N], f16) for k in range(3)]
        qk_h, qk_l = sb("qk_h", [P, 5, N], f16), sb("qk_l", [P, 5, N], f16)
        q4, k4 = sb("q4", [P, NT, N], f16), sb("k4", [P, NT, N], f16)
        v1 = sb("v1", [P, KT, H, 2 * DH], f32)
        c_in = sb("c_in", [J, 2 * P], f32)
        ct_h, ct_l = sb("ct_h", [P, 2, J], f16), sb("ct_l", [P, 1, J], f16)
        k2_h, k2_l = sb("k2_h", [P, 3, J], f16), sb("k2_l", [P, 3, J], f16)
        q2_h, q2_l = sb("q2_h", [P, 3, N], f16), sb("q2_l", [P, 3, N], f16)
        q42, k42 = sb("q42", [P, NT, N], f16), sb("k42", [P, NT, J], f16)
        v2 = sb("v2", [J, H, 2 * DH], f32)
        m_q = [sb(f"m_q{a}", [P, 2, NT, KT], f32) for a in range(2)]
        m_row = [sb(f"m_row{a}", [H, N], f16) for a in range(2)]
        probs = sb("probs", [P, NP, 4 * N], f32)
        stage = probs[:, :, :].rearrange("p a b -> p (a b)")
        o_raw = [sb(f"o_raw{a}", [P, NG, N], f32) for a in range(2)]
        o_c = [sb(f"o_c{a}", [P, 3, N], f32) for a in range(2)]
        o_h = [sb(f"o_h{a}", [P, 3, N], f16) for a in range(2)]
        o_l = [sb(f"o_l{a}", [P, 2, N], f16) for a in range(2)]
        den = [sb(f"den{a}", [NC * H, N // NC], f32) for a in range(2)]
        rec = [sb(f"rec{a}", [NC * H, N // NC], f32) for a in range(2)]
        rec_part = [sb(f"rec_part{a}", [NC * H, 3, N // NC], bf16) for a in range(2)]
        ff_g = sb("ff_g", [P, 2, N], f32)
        ff_h, ff_l = sb("ff_h", [P, 2, N], f32r), sb("ff_l", [P, 2, N], f32r)

        ps = ctx.enter_context(nc.psum_tensor("ps", [P, 8, 512], f32))
        slot = [ps[:, 0:2, :], ps[:, 2:4, :]]
        flat = [s.rearrange("p a b -> p (a b)") for s in slot]
        ps_f1, ps_f2 = ps[:, 5, :], [ps[:, 6, :], ps[:, 7, :]]
        ps_pv, ps_t0 = [ps_f1, ps[:, 4, :]], ps[:, 4:6, :].rearrange("p a b -> p (a b)")

        (S_QKV, S_Q2, S_W1, S_KV2, S_CTX, S_O1, S_O2, E1, E2, D1, D2, D3, KV2_CTX) = range(13)

        x_loaded, c_loaded = Event("x_loaded", 16), Event("c_loaded", 32)
        ln_stat = [Event(f"ln_stat{k}", 3) for k in range(3)]
        ln_rstd = [Event(f"ln_rstd{k}", 1) for k in range(3)]
        ln_done = [Event(f"ln_done{k}", 1) for k in range(3)]
        tr_done = [Event(f"tr_done{k}", 1) for k in range(3)]
        tr_hi = [Event(f"tr_hi{k}", 1) for k in range(3)]
        tr_lo = [Event(f"tr_lo{k}", 1) for k in range(3)]
        qk_done, qk_hi, qk_lo = Event("qk_done", 5), Event("qk_hi", 5), Event("qk_lo", 5)
        v_done, v_copied = Event("v_done", KT), Event("v_copied", KT)
        spread = [Event(f"spread{r}", 6 * 16) for r in range(4)]
        max_done, max_red = Event("max_done", NT), Event("max_red", NT)
        max2_done, max2_red = Event("max2_done", 8), Event("max2_red", 8)
        mt_done = [Event(f"mt_done{a}", 1) for a in range(2)]
        mt_row = [Event(f"mt_row{a}", 1) for a in range(2)]
        m_spread = [Event(f"m_spread{a}", 32) for a in range(2)]
        st_done = [Event("st_done0", NT), Event("st_done1", NG)]
        exp_done = [Event("exp_done0", NT), Event("exp_done1", NG)]
        pv_done = [Event(f"pv_done{a}", NG) for a in range(2)]
        o_copied = [Event(f"o_copied{a}", NG) for a in range(2)]
        o_spread = [Event(f"o_spread{a}", 48) for a in range(2)]
        den_spread = [Event(f"den_spread{a}", 16) for a in range(2)]
        rec_done = [Event(f"rec_done{a}", 6) for a in range(2)]
        rb_done = [Event(f"rb_done{a}", 1) for a in range(2)]
        o_norm = [Event(f"o_norm{a}", 1) for a in range(2)]
        o_hi = [Event(f"o_hi{a}", 1) for a in range(2)]
        o_lo = [Event(f"o_lo{a}", 2) for a in range(2)]
        oproj_done = [Event(f"oproj_done{a}", 1) for a in range(2)]
        resid = [Event(f"resid{a}", 1) for a in range(2)]
        xb_done = [Event(f"xb_done{a}", 1) for a in range(3)]
        q2_done, q2_hi, q2_lo = Event("q2_done", 1), Event("q2_hi", 1), Event("q2_lo", 1)
        q2_spread = Event("q2_spread", 12 * 16)
        ct_done, ct_hi, ct_lo = Event("ct_done", 1), Event("ct_hi", 1), Event("ct_lo", 1)
        kv2_done, k2_hi, k2_lo = Event("kv2_done", 1), Event("k2_hi", 1), Event("k2_lo", 1)
        v2_copied, k2_spread = Event("v2_copied", 1), Event("k2_spread", 12 * 16)
        ff1_done, gelu_done, ffp_done = Event("ff1_done", NM), Event("gelu_done", NM), Event("ffp_done", NM)
        ffh_done, ffl_done, ff2_step = Event("ffh_done", NM), Event("ffl_done", NM), Event("ff2_step", NM)
        gelu_table, exp_table = Event("gelu_table", 1), Event("exp_table", 1)
        table_out = {gelu_table: sb("gelu_out", [P, 1], f32), exp_table: sb("exp_out", [P, 1], f32)}
        out_ready, out_stored = Event("out_ready", 1), Event("out_stored", 16)

        MAX2_AT = {2: (0, 1), 3: (2,), 4: (3, 4), 5: (5,), 6: (6, 7)}
        MT2_AT = 7
        QK_SELF, QK_CROSS, CTX_AT = {7: 0, 8: 1}, {1: 2, 2: 3, 3: 4}, 4
        MAX_AT = {"oproj": (0,), 3: (1,), 4: (2,), "q2": (3,), 5: (4, 5), 6: (6, 7), 7: (8, 9)}
        MT_AT, TR2_AT = 8, 9

        QKV, SELF, CROSS, NORM1, FFN, LAST = range(6)
        STREAM_STEP = (1, 0, -1, 2, -2, -3)

        def max_units(key):
            return [(("max", n), QKV, max_red, n + 1) for n in MAX_AT.get(key, ())]

        UNITS = []
        for T in range(1, NT):
            UNITS += [(("st", T), SELF, exp_done[0], T + 1)]
        UNITS += [(("st2", g), CROSS, exp_done[1], g + 1) for g in range(NG)]
        UNITS += [(("rb", 0), SELF, o_norm[0], 1), (("kv2", 0), SELF, v2_copied, 1),
                  (("rb", 1), CROSS, o_norm[1], 1), (("oproj", 0), SELF, resid[0], 1),
                  (("oproj", 1), CROSS, resid[1], 1)]
        UNITS += max_units("oproj") + max_units(3) + [(("tr", 1), SELF, tr_lo[1], 1)] + max_units(4)
        UNITS += [(("q2", 0), SELF, q2_lo, 1)] + max_units("q2")
        for m in range(5, NM + 1):
            UNITS += max_units(m)
            if m == MT_AT:
                UNITS += [(("mt", 0), QKV, mt_row[0], 1)]
            if m == TR2_AT:
                UNITS += [(("tr", 2), CROSS, tr_lo[2], 1), (("v", 0), QKV, v_copied, KT),
                          (("st", 0), QKV, exp_done[0], 1)]
        MAX_ORDER = [0, 4, 8, 1, 5, 9, 2, 6, 3, 7]
        MAX2_PAIRS = [(0, 3), (3, 3), (6, 3), (9, 1)]

        def ring(active, before, units=None, slots=2):
            last, table = {}, {}
            for ago, streams in ((1, before), (0, active)):
                uses = [u for u in (UNITS if units is None else units) if u[1] in streams]
                for n, (name, stream, ev, k) in enumerate(uses):
                    if ago == 0:
                        table[name] = (n % slots, last.get(n % slots))
                    last[n % slots] = (ev, STREAM_STEP[stream] - ago, k)
            return table

        PV_USES = [((a, g), (SELF, CROSS)[a], o_copied[a], g + 1) for a in range(2) for g in range(NG)]

        def pv_ring(active, before):
            return ring(active, before, PV_USES, 2)

        def streams_of(i):
            if not isinstance(i, int):
                return tuple(range(6))
            return tuple(s for s in range(6) if 0 <= i + STREAM_STEP[s] < B)

        def before_of(i):
            return streams_of(i - 1)

        def run_steps(eng, step):
            for i in range(-2, 4):
                step(i)
            with eng.Fori(4, B - 2) as i:
                step(i)
            for i in range(B - 2, B + 3):
                step(i)

        def split_passes(xh, xl, wh, wl, full):
            pairs = []
            for s in range(full):
                pairs += [(xh[:, s], wh[:, s]), (xl[:, s], wh[:, s]), (xh[:, s], wl[:, s])]
            return pairs + [(xh[:, full], wh[:, full]), (xh[0:64, full], wl[0:64, full])]

        CW = 256
        def slices(k):
            return 3 if k == D else 2
        MATS = [("q1", 0, D, 0, S_QKV), ("k1", 0, D, 0, S_QKV), ("v1", 0, D, 0, S_QKV), ("q2", 0, D, 1, S_Q2)]
        MATS += [("ff_w1", c * CW, CW, 2, S_W1) for c in range(2 * FF // CW)]
        LNMATS = len(MATS)
        MATS += [("k2", 0, D, None, S_KV2), ("v2", 0, D, None, S_KV2), ("o2_w", 0, D, None, S_O2),
                 ("o1_w", 0, D, None, S_O1)]
        CTXCH = [(b, min(5, B - b)) for b in range(0, B, 5)]
        W2CH = [(s, min(3, NM - s)) for s in range(0, NM, 3)]
        DEST = {"q1": (wqkv_h, wqkv_l, 0), "k1": (wqkv_h, wqkv_l, D), "v1": (wqkv_h, wqkv_l, 2 * D),
                "q2": (wq2_h, wq2_l, 0), "ff_w1": (w1_h, w1_l, 0), "k2": (wkv2_h, wkv2_l, 0),
                "v2": (wkv2_h, wkv2_l, D), "o2_w": (wo2_h, wo2_l, 0), "o1_w": (wo1_h, wo1_l, 0)}
        CHUNKS = [("ctx",) + c for c in CTXCH] + [("max",) + m for m in MATS]
        CHUNKS += [("cut",) + m for m in MATS] + [("w2",) + c for c in W2CH]
        N1 = len(CTXCH) + len(MATS)
        staged, vec_loaded = [Event(f"staged{k}", 16) for k in range(NSTAGE)], Event("vec_loaded", 16)
        stage_used, scaled = Event("stage_used", 1), Event("scaled", 1)
        pro, pro_pe, pro_act = Event("pro", 1), Event("pro_pe", 1), Event("pro_act", 1)
        pro_dve, pro_hi, maxima, cv_ready = (Event(n, 1) for n in ("pro_dve", "pro_hi", "maxima", "cv_ready"))
        scales_ready = Event("scales_ready", 1)
        tmp = [stage[:, (NSTAGE + k) * STW:(NSTAGE + k + 1) * STW] for k in range(2)]

        def stage_buf(n):
            return stage[:, (n % NSTAGE) * STW:(n % NSTAGE + 1) * STW]

        def chunk_dmas(n):
            ch, buf = CHUNKS[n], stage_buf(n)
            if ch[0] == "ctx":
                _, b, nb = ch
                return [(buf[0:J, 0:nb * CTX].rearrange("p (b c) -> p b c", b=nb),
                         t["ctx_768"][b:b + nb].rearrange("b j c -> j b c"))]
            if ch[0] == "w2":
                _, s, ns = ch
                return [(buf[:, 0:ns * D].rearrange("p (s c) -> p s c", s=ns),
                         t["ff_w2"][s * P:(s + ns) * P, :].rearrange("(s p) c -> p s c", p=P))]
            _, name, c0, cw, _, _ = ch
            w = t[name]
            full = slices(w.shape[0]) - 1
            b3 = buf[:, 0:(full + 1) * cw].rearrange("p (s c) -> p s c", s=full + 1)
            tail = w[full * P:full * P + 64, c0:c0 + cw]
            return [(b3[:, 0:full, :], w[0:full * P, c0:c0 + cw].rearrange("(s p) c -> p s c", p=P)),
                    (b3[0:64, full, :], tail), (b3[64:P, full, :], tail)]

        def times_scaled(n):
            return sum(1 for c in CHUNKS[:n] if c[0] in ("cut", "w2") or (c[0] == "max" and c[4] is not None))

        stage_value, counts = [], [0] * NSTAGE
        for n in range(len(CHUNKS)):
            counts[n % NSTAGE] += 16 * len(chunk_dmas(n))
            stage_value.append(counts[n % NSTAGE])

        C_QK, C_V, C_Q2, C_W1 = 0, 5, 8, 11
        def c_places(n):
            _, name, c0, cw, _, _ = CHUNKS[n]
            if name == "q1":
                return [(0, 128, 0, C_QK), (128, 256, 0, C_QK + 1), (256, 320, 0, C_QK + 2)]
            if name == "k1":
                return [(0, 64, 64, C_QK + 2), (64, 192, 0, C_QK + 3), (192, 320, 0, C_QK + 4)]
            if name in ("v1", "q2"):
                c = C_V if name == "v1" else C_Q2
                return [(0, 128, 0, c), (128, 256, 0, c + 1), (256, 320, 0, c + 2)]
            return [(0, 128, 0, C_W1 + c0 // P), (128, 256, 0, C_W1 + c0 // P + 1)]

        NVEC_LOADS = 3 + 4 + 18 + 1 + 3
        PRO_DONE = 2

        MXCOL, MXGROUPS, col = {}, [], 0
        for scale in (S_QKV, S_Q2, S_W1, S_KV2, S_CTX, S_O1, S_O2):
            first = col
            for n in range(N1):
                if (scale == S_CTX) if CHUNKS[n][0] == "ctx" else (CHUNKS[n][5] == scale):
                    MXCOL[n], col = col, col + 1
            if scale in (S_QKV, S_Q2):
                MXCOL["qk" if scale == S_QKV else "q2"], col = col, col + 1
            MXGROUPS.append((first, col))

        XHAT = [(1, SELF, tr_done[1], 1), (2, CROSS, tr_done[2], 1)]

        block = ctx.enter_context(nc.Block())

        @block.sync
        def _(sp):
            loads = [(ident[:], t["c_ident"]), (c_quarter[:], t["c_quarter"]), (sel_f, t["c_sel"]),
                     (k4[63:64, :, :].rearrange("p a b -> p (a b)"), t["c_aug"][0:1, 0:NT * N]),
                     (k4[127:128, :, :].rearrange("p a b -> p (a b)"), t["c_aug"][0:1, 0:NT * N]),
                     (k42[63:64, :, :].rearrange("p a b -> p (a b)"), t["c_aug"][0:1, 0:NT * J]),
                     (k42[127:128, :, :].rearrange("p a b -> p (a b)"), t["c_aug"][0:1, 0:NT * J])]
            for j, nm in enumerate(("n1_g", "n1_b", "n2_g", "n2_b", "n3_g", "n3_b")):
                v = t[nm]
                loads += [(gb[:, j, 0:2], v[0:2 * P].rearrange("(s p) -> p s", p=P))]
                for r in (0, 64):
                    loads += [(gb[r:r + 64, j, 2:3], v[2 * P:D].rearrange("(p o) -> p o", o=1))]
            loads += [(b1c[:, :], t["ff_b1"].rearrange("(s p) -> p s", p=P))]
            for dst, nm in ((bias1, "o1_b"), (bias2, "o2_b"), (bias3, "ff_b2")):
                loads += [(dst[:, :], t[nm].partition_broadcast(P))]
            for n in range(len(CHUNKS)):
                if n == NSTAGE:
                    sp.wait_ge(pro.sem, pro.at(0, 1))
                    for dst, src in loads:
                        sp.dma_start(dst, src, allow_slow_non_contiguous=True).then_inc(vec_loaded.sem, 16)
                if n >= NSTAGE + N1:
                    sp.wait_ge(scaled.sem, scaled.at(0, times_scaled(n - NSTAGE + 1)))
                elif n >= NSTAGE:
                    sp.wait_ge(stage_used.sem, stage_used.at(0, n - NSTAGE + 1))
                for dst, src in chunk_dmas(n):
                    sp.dma_start(dst, src).then_inc(staged[n % NSTAGE].sem, 16)
            assert len(loads) == NVEC_LOADS

            def load_x(e):
                sp.wait_ge(ln_done[0].sem, ln_done[0].at(e - 1))
                sp.wait_ge(xb_done[0].sem, xb_done[0].at(e - 1))
                sp.dma_start(x_in[:], t["x"][e].rearrange("(s p) c -> p s c", p=P)).then_inc(x_loaded.sem, 16)

            def load_ctx(e):
                sp.wait_ge(ct_done.sem, ct_done.at(e - 1))
                sp.dma_start(c_in[:, 0:CTX], t["ctx_768"][e]).then_inc(c_loaded.sem, 16)
                sp.dma_start(c_in[:, CTX:2 * P], t["ctx_768"][e, :, P:CTX]).then_inc(c_loaded.sem, 16)

            def spread_qk(e, r):
                sp.wait_ge(qk_lo.sem, qk_lo.at(e))
                sp.wait_ge(max_done.sem, max_done.at(e - 1))
                sp.wait_ge(st_done[0].sem, st_done[0].at(e - 1))
                nt = 3 if r < 2 else 2
                for part, src in enumerate((qk_h, qk_h, qk_l)):
                    sp.dma_start(q4[part:P:4, r:r + 4 * (nt - 1) + 1:4, :],
                                 src[32 * r:32 * r + 32, 0:nt, :]).then_inc(spread[r].sem, 16)
                kb = (r + 2) % 4
                t0 = 3 if kb < 2 else 2
                for part, src in enumerate((qk_h, qk_l, qk_h)):
                    sp.dma_start(k4[part:P:4, r:r + 4 * (4 - t0) + 1:4, :],
                                 src[32 * kb:32 * kb + 32, t0:5, :]).then_inc(spread[r].sem, 16)

            def spread_q2(e):
                sp.wait_ge(q2_lo.sem, q2_lo.at(e))
                sp.wait_ge(st_done[1].sem, st_done[1].at(e - 1))
                for r in range(4):
                    nt = 3 if r < 2 else 2
                    for part, src in enumerate((q2_h, q2_h, q2_l)):
                        sp.dma_start(q42[part:P:4, r:r + 4 * (nt - 1) + 1:4, :],
                                     src[32 * r:32 * r + 32, 0:nt, :]).then_inc(q2_spread.sem, 16)

            def spread_k2(e):
                sp.wait_ge(k2_lo.sem, k2_lo.at(e))
                sp.wait_ge(st_done[1].sem, st_done[1].at(e - 1))
                for r in range(4):
                    nt = 3 if r < 2 else 2
                    for part, src in enumerate((k2_h, k2_l, k2_h)):
                        sp.dma_start(k42[part:P:4, r:r + 4 * (nt - 1) + 1:4, :],
                                     src[32 * r:32 * r + 32, 0:nt, :]).then_inc(k2_spread.sem, 16)

            def spread_max(a, e):
                sp.wait_ge(mt_row[a].sem, mt_row[a].at(e))
                for h in range(2):
                    sp.dma_start((q4, q42)[a][64 * h + 63:64 * h + 64, :, :],
                                 m_row[a][NT * h:NT * h + NT, :]).then_inc(m_spread[a].sem, 16)

            def spread_out(a, e):
                sp.wait_ge(o_copied[a].sem, o_copied[a].at(e))
                sp.wait_ge(rec_done[a].sem, rec_done[a].at(e - 1))
                sp.wait_ge(o_lo[a].sem, o_lo[a].at(e - 1))
                sp.dma_start(den[a][:, :], o_raw[a][1:P:32].rearrange("p g (c n) -> p (g c) n", c=NC)
                             ).then_inc(den_spread[a].sem, 16)
                sp.dma_start(o_c[a][0:64, 0:3, :], o_raw[a][0:P:2, 0:NG:2, :]).then_inc(o_spread[a].sem, 16)
                sp.dma_start(o_c[a][64:P, 0:2, :], o_raw[a][0:P:2, 1:NG:2, :]).then_inc(o_spread[a].sem, 16)
                sp.dma_start(o_c[a][64:P, 2, :], o_raw[a][0:P:2, NG - 1, :]).then_inc(o_spread[a].sem, 16)

            def store_out(e):
                sp.wait_ge(out_ready.sem, out_ready.at(e))
                sp.dma_start(out[e].rearrange("(s p) c -> p s c", p=P), out_sb[:]).then_inc(out_stored.sem, 16)

            def step(i):
                on = streams_of(i)
                if SELF in on:
                    load_ctx(i)
                if LAST in on:
                    store_out(i - 3)
                if CROSS in on:
                    spread_max(1, i - 1)
                if SELF in on:
                    spread_out(0, i)
                if CROSS in on:
                    spread_out(1, i - 1)
                if QKV in on:
                    for r in range(4):
                        spread_qk(i + 1, r)
                if SELF in on:
                    spread_k2(i)
                if NORM1 in on:
                    load_x(i + 2)
                if SELF in on:
                    spread_q2(i)
                if QKV in on:
                    spread_max(0, i + 1)

            run_steps(sp, step)
            sp.wait_ge(out_stored.sem, out_stored.at(B - 1))

        @block.gpsimd
        def _(pool):
            nc.gpsimd.memset(halfneg[:], -0.5).then_inc(pro_act.sem, 1)
            pool.wait_ge(vec_loaded.sem, 16 * NVEC_LOADS)
            pool.wait_ge(pro_act.sem, pro_act.at(0, 1))

            def rstd(k, e):
                pool.wait_ge(ln_stat[k].sem, ln_stat[k].at(e))
                nc.gpsimd.tensor_tensor(rs[k][:], ve[k][:], halfneg[:], ALU.pow).then_inc(ln_rstd[k].sem, 1)

            def add_bias(k, e):
                src, dst, bias = ((x_in, xb1, bias1), (x1, xb2, bias2), (x2, xb3, bias3))[k]
                if k == 0:
                    pool.wait_ge(x_loaded.sem, x_loaded.at(e))
                else:
                    pool.wait_ge(resid[k - 1].sem, resid[k - 1].at(e))
                if k < 2:
                    pool.wait_ge(resid[k].sem, resid[k].at(e - 1))
                else:
                    pool.wait_ge(out_ready.sem, out_ready.at(e - 1))
                nc.gpsimd.tensor_tensor(dst[:], src[:], bias[:].unsqueeze(1).to_broadcast([P, KT, D]),
                                        ALU.add).then_inc(xb_done[k].sem, 1)

            def out_lo(a, e):
                pool.wait_ge(o_hi[a].sem, o_hi[a].at(e))
                pool.wait_ge(oproj_done[a].sem, oproj_done[a].at(e - 1))
                nc.gpsimd.tensor_tensor(o_l[a][:], o_c[a][:, 0:2], o_h[a][:, 0:2],
                                        ALU.subtract).then_inc(o_lo[a].sem, 1)
                pool.wait_ge(o_lo[a].sem, o_lo[a].at(e, 1))
                nc.gpsimd.tensor_tensor(o_h[a][64:P, 2], o_c[a][64:P, 2], o_h[a][64:P, 2],
                                        ALU.subtract).then_inc(o_lo[a].sem, 1)
                pool.wait_ge(o_lo[a].sem, o_lo[a].at(e))

            def ff_lo(m, e):
                pool.wait_ge(ffh_done.sem, ffh_done.at(e, m + 1))
                if m >= 2:
                    pool.wait_ge(ff2_step.sem, ff2_step.at(e, m - 1))
                else:
                    pool.wait_ge(ff2_step.sem, ff2_step.at(e - 1, NM - 1 + m))
                nc.gpsimd.tensor_tensor(ff_l[:, m % 2], ff_g[:, m % 2], ff_h[:, m % 2].bitcast(f32),
                                        ALU.subtract).then_inc(ffl_done.sem, 1)

            def step(i):
                on = streams_of(i)

                def tile(m):
                    if FFN in on:
                        ff_lo(m, i - 2)

                if FFN in on:
                    add_bias(2, i - 2)
                tile(0)
                if SELF in on:
                    out_lo(0, i)
                tile(1)
                if CROSS in on:
                    out_lo(1, i - 1)
                if SELF in on:
                    rstd(1, i)
                tile(2)
                tile(3)
                if CROSS in on:
                    rstd(2, i - 1)
                if QKV in on:
                    add_bias(0, i + 1)
                tile(4)
                tile(5)
                if SELF in on:
                    add_bias(1, i)
                for m in range(6, NM):
                    tile(m)
                    if m == 8 and NORM1 in on:
                        rstd(0, i + 2)

            pool.wait_ge(pro.sem, pro.at(0, PRO_DONE))
            run_steps(pool, step)

        @block.scalar
        def _(act):
            act.wait_ge(vec_loaded.sem, 16 * NVEC_LOADS)
            for n in range(len(CTXCH), len(CHUNKS)):
                ch = CHUNKS[n]
                if ch[0] == "max" and ch[4] is None:
                    continue
                if n == N1:
                    act.wait_ge(scales_ready.sem, scales_ready.at(0))
                act.wait_ge(staged[n % NSTAGE].sem, staged[n % NSTAGE].at(0, stage_value[n]))
                if n >= 2:
                    act.wait_ge(stage_used.sem, stage_used.at(0, n - 1))
                buf, dst = stage_buf(n), tmp[n % 2]
                if ch[0] == "w2":
                    last = nc.scalar.activation(dst[:, 0:ch[2] * D], buf[:, 0:ch[2] * D], ACT.Copy)
                else:
                    _, name, _, cw, ln, scale = ch
                    ns = slices(t[name].shape[0])
                    if ln is None:
                        last = nc.scalar.activation(dst[:, 0:ns * cw], buf[:, 0:ns * cw], ACT.Copy,
                                                    scale=sc[:, scale:scale + 1])
                    else:
                        for s in range(ns):
                            g_ap = gb[:, 2 * ln, s:s + 1] if ch[0] == "max" else gs[:, ln, s:s + 1]
                            last = nc.scalar.activation(dst[:, s * cw:(s + 1) * cw], buf[:, s * cw:(s + 1) * cw],
                                                        ACT.Copy, scale=g_ap)
                last.then_inc(scaled.sem, 1)
            act.wait_ge(pro.sem, pro.at(0, PRO_DONE))

            def tr_hi_part(k, e, src):
                act.wait_ge(tr_done[k].sem, tr_done[k].at(e))
                if k == 0:
                    act.wait_ge(v_done.sem, v_done.at(e - 1))
                elif k == 1:
                    act.wait_ge(q2_done.sem, q2_done.at(e - 1))
                else:
                    act.wait_ge(ff1_done.sem, ff1_done.at(e - 1))
                nc.scalar.activation(ah[k][:].rearrange("p a b -> p (a b)"), src[:, 0:3 * N],
                                     ACT.Copy).then_inc(tr_hi[k].sem, 1)

            def q2_hi_part(e, s):
                act.wait_ge(q2_done.sem, q2_done.at(e))
                act.wait_ge(q2_spread.sem, q2_spread.at(e - 1))
                for m in range(3):
                    r = P if m < 2 else 64
                    last = nc.scalar.activation(q2_h[0:r, m, :], flat[s][0:r, m * N:(m + 1) * N],
                                                ACT.Identity, bias=cvec[0:r, C_Q2 + m:C_Q2 + m + 1])
                last.then_inc(q2_hi.sem, 1)

            def k2_hi_part(e, s):
                act.wait_ge(kv2_done.sem, kv2_done.at(e))
                act.wait_ge(k2_spread.sem, k2_spread.at(e - 1))
                nc.scalar.activation(k2_h[:, 0:2, :].rearrange("p a b -> p (a b)"), flat[s][:, 0:2 * J], ACT.Copy)
                nc.scalar.activation(k2_h[0:64, 2, :], flat[s][0:64, 2 * J:3 * J],
                                     ACT.Copy).then_inc(k2_hi.sem, 1)

            def max_row(a, e, src):
                act.wait_ge(mt_done[a].sem, mt_done[a].at(e))
                act.wait_ge(m_spread[a].sem, m_spread[a].at(e - 1))
                nc.scalar.activation(m_row[a][:], src[0:H, 0:N], ACT.Copy,
                                     scale=1.0 / AUG).then_inc(mt_row[a].sem, 1)

            def load_table(function, loaded, e):
                act.wait_ge(loaded.sem, loaded.at(e - 1))
                nc.scalar.activation(table_out[loaded][:], halfneg[:, 0:1], function).then_inc(loaded.sem, 1)

            def exps1(T, e, s):
                act.wait_ge(st_done[0].sem, st_done[0].at(e, T + 1))
                if T < NP:
                    act.wait_ge(pv_done[0].sem, pv_done[0].at(e - 1))
                    act.wait_ge(pv_done[1].sem, pv_done[1].at(e - 2, T + 1))
                else:
                    act.wait_ge(pv_done[0].sem, pv_done[0].at(e, (T - NP) // 2 + 1))
                nc.scalar.activation(probs[:, T % NP, :], flat[s][:, :], ACT.Exp,
                                     scale=sc[:, E1:E1 + 1]).then_inc(exp_done[0].sem, 1)

            def exps2(g, e, s, on):
                act.wait_ge(st_done[1].sem, st_done[1].at(e, g + 1))
                act.wait_ge(pv_done[1].sem, pv_done[1].at(e - 1, g + 1))
                if SELF in on:
                    act.wait_ge(pv_done[0].sem, pv_done[0].at(e + 1, (NP + g) // 2 + 1))
                nc.scalar.activation(probs[0:J, g, :], flat[s][0:J, :], ACT.Exp,
                                     scale=sc[0:J, E2:E2 + 1]).then_inc(exp_done[1].sem, 1)

            def out_hi_part(a, e):
                act.wait_ge(o_norm[a].sem, o_norm[a].at(e))
                act.wait_ge(oproj_done[a].sem, oproj_done[a].at(e - 1))
                nc.scalar.activation(o_h[a][:].rearrange("p a b -> p (a b)"),
                                     o_c[a][:].rearrange("p a b -> p (a b)"), ACT.Copy).then_inc(o_hi[a].sem, 1)

            def gelu(m, e):
                act.wait_ge(ff1_done.sem, ff1_done.at(e, m + 1))
                if m >= 2:
                    act.wait_ge(ffl_done.sem, ffl_done.at(e, m - 1))
                else:
                    act.wait_ge(ffl_done.sem, ffl_done.at(e - 1, NM - 1 + m))
                nc.scalar.activation(ff_g[:, m % 2], ps_f1[:, N:2 * N], ACT.Gelu, scale=sc[:, D3:D3 + 1],
                                     bias=cvec[:, C_W1 + NM + m:C_W1 + NM + m + 1]).then_inc(gelu_done.sem, 1)

            def ff_hi(m, e):
                act.wait_ge(ffp_done.sem, ffp_done.at(e, m + 1))
                if m >= 2:
                    act.wait_ge(ff2_step.sem, ff2_step.at(e, m - 1))
                else:
                    act.wait_ge(ff2_step.sem, ff2_step.at(e - 1, NM - 1 + m))
                nc.scalar.activation(ff_h[:, m % 2], ff_g[:, m % 2], ACT.Copy).then_inc(ffh_done.sem, 1)

            def step(i):
                on, tab = streams_of(i), ring(streams_of(i), before_of(i))

                for T in range(NT):
                    if SELF in on and T:
                        exps1(T, i, tab["st", T][0])
                    if T == MT2_AT and CROSS in on:
                        max_row(1, i - 1, ps_f2[1])
                for g in range(NG):
                    if CROSS in on:
                        exps2(g, i - 1, tab["st2", g][0], on)
                if FFN in on:
                    load_table(ACT.Gelu, gelu_table, i - 2)
                    gelu(0, i - 2)
                if FFN in on:
                    ff_hi(0, i - 2)
                if SELF in on:
                    out_hi_part(0, i)
                if SELF in on:
                    k2_hi_part(i, tab["kv2", 0][0])
                if FFN in on:
                    gelu(1, i - 2)
                    ff_hi(1, i - 2)
                if CROSS in on:
                    out_hi_part(1, i - 1)
                for m in range(2, NM):
                    if FFN in on:
                        gelu(m, i - 2)
                    if m == MT_AT and QKV in on:
                        max_row(0, i + 1, flat[tab["mt", 0][0]])
                    if FFN in on:
                        ff_hi(m, i - 2)
                    if m == 3 and SELF in on:
                        tr_hi_part(1, i, flat[tab["tr", 1][0]])
                    if m == 4 and SELF in on:
                        q2_hi_part(i, tab["q2", 0][0])
                    if m == TR2_AT and CROSS in on:
                        tr_hi_part(2, i - 1, flat[tab["tr", 2][0]])
                if QKV in on:
                    load_table(ACT.Exp, exp_table, i + 1)
                    exps1(0, i + 1, tab["st", 0][0])
                if NORM1 in on:
                    tr_hi_part(0, i + 2, ps_t0)

            run_steps(act, step)

        @block.tensor
        def _(pe):
            mm = nc.tensor.matmul
            pe.wait_ge(vec_loaded.sem, 16 * NVEC_LOADS)
            for n in range(len(CTXCH), len(CTXCH) + LNMATS):
                _, _, _, cw, ln, _ = CHUNKS[n]
                pe.wait_ge(staged[n % NSTAGE].sem, staged[n % NSTAGE].at(0, stage_value[n]))
                w = stage_buf(n)[:, 0:3 * cw].rearrange("p (s c) -> p s c", s=3)
                for c0, c1, r0, col in c_places(n):
                    for s in range(3):
                        k = P if s < 2 else 64
                        last = mm(ps[r0:r0 + c1 - c0, 0, col:col + 1], w[0:k, s, c0:c1],
                                  gb[0:k, 2 * ln + 1, s:s + 1], start=(s == 0), stop=(s == 2))
                last.then_inc(pro_pe.sem, 1)
            pe.wait_ge(staged[(N1 - 1) % NSTAGE].sem, staged[(N1 - 1) % NSTAGE].at(0, stage_value[N1 - 1]))
            pe.wait_ge(cv_ready.sem, cv_ready.at(0))
            w = stage_buf(N1 - 1).rearrange("p (s c) -> p s c", s=3)
            for s in range(3):
                k = P if s < 2 else 64
                last = mm(ps[:, 1, 0:D], cv_rep[0:k, s, :], w[0:k, s, :], start=(s == 0), stop=(s == 2))
            last.then_inc(pro_pe.sem, 1)
            pe.wait_ge(maxima.sem, maxima.at(0, 1))
            mm(ps[0:8, 2, 0:P], mxm[:], ident[:], start=True, stop=True).then_inc(pro_pe.sem, 1)
            pe.wait_ge(maxima.sem, maxima.at(0, 2))
            mm(ps[:, 3, 0:8], ones[:], mxd[:], start=True, stop=True).then_inc(pro_pe.sem, 1)
            pe.wait_ge(pro.sem, pro.at(0, PRO_DONE))

            def take(tab, name, i):
                s, prior = tab[name]
                if prior:
                    freed, step_offset, count = prior
                    pe.wait_ge(freed.sem, freed.at(i + step_offset, count))
                return s

            def transposes(k, e, dst):
                pe.wait_ge(ln_done[k].sem, ln_done[k].at(e))
                for c in range(3):
                    for q in range(KT):
                        last = nc.tensor.transpose(dst[:, c * N + q * P:c * N + (q + 1) * P],
                                                   xhat[k][:, q, c * P:(c + 1) * P], ident[:])
                last.then_inc(tr_done[k].sem, 1)

            def product(dst, pairs):
                for n, (lhs, rhs) in enumerate(pairs):
                    last = mm(dst, lhs, rhs, start=(n == 0), stop=(n == len(pairs) - 1))
                return last

            def by_feature(dst, wh, wl, c0, c1, xh, xl, full=2):
                pairs = split_passes(xh, xl, wh[:, :, c0:c1], wl[:, :, c0:c1], full)
                return product(dst, [(w, x) for x, w in pairs])

            def by_token(dst, wh, wl, c0, c1, xh, xl, full=2):
                return product(dst, split_passes(xh, xl, wh[:, :, c0:c1], wl[:, :, c0:c1], full))

            def qk(m, e, on):
                if m == 0:
                    if CROSS in on:
                        pe.wait_ge(max2_red.sem, max2_red.at(e - 2))
                    pe.wait_ge(tr_lo[0].sem, tr_lo[0].at(e))
                    pe.wait_ge(out_ready.sem, out_ready.at(e - 4))
                    if SELF in on:
                        pe.wait_ge(ct_lo.sem, ct_lo.at(e - 2))
                    pe.wait_ge(qk_lo.sem, qk_lo.at(e - 1))
                if m == 1 and CROSS in on:
                    pe.wait_ge(mt_row[1].sem, mt_row[1].at(e - 2))
                if m >= 2:
                    pe.wait_ge(qk_lo.sem, qk_lo.at(e, m - 1))
                by_feature(ps_f2[m % 2][:, 0:N], wqkv_h, wqkv_l,
                           m * P, (m + 1) * P, ah[0], al[0]).then_inc(qk_done.sem, 1)

            def values(e, s):
                for q in range(KT):
                    by_token(slot[s][:, q, 0:D], wqkv_h, wqkv_l, 2 * D, 3 * D, ah[0][:, :, q * P:(q + 1) * P],
                             al[0][:, :, q * P:(q + 1) * P]).then_inc(v_done.sem, 1)

            def maxima1(n, e, s):
                T = MAX_ORDER[n]
                pe.wait_ge(spread[T % 4].sem, spread[T % 4].at(e))
                for h in range(2):
                    for q in range(KT):
                        last = mm(flat[s][:, (2 * h + q) * N:(2 * h + q + 1) * N],
                                  q4[64 * h:64 * h + 63, T, q * P:(q + 1) * P],
                                  k4[64 * h:64 * h + 63, T, :], start=True, stop=True)
                last.then_inc(max_done.sem, 1)

            def maxima2(u, e, on):
                (first, nt), h = MAX2_PAIRS[u // 2], u % 2
                if u == 0:
                    pe.wait_ge(out_ready.sem, out_ready.at(e - 2))
                    if SELF in on:
                        pe.wait_ge(qk_lo.sem, qk_lo.at(e + 1))
                    pe.wait_ge(ct_lo.sem, ct_lo.at(e))
                    pe.wait_ge(q2_spread.sem, q2_spread.at(e))
                    pe.wait_ge(k2_spread.sem, k2_spread.at(e))
                if u >= 2:
                    pe.wait_ge(max2_red.sem, max2_red.at(e, u - 1))
                for T in range(first, first + nt):
                    for q in range(KT):
                        c = ((T - first) * KT + q) * J
                        last = mm(ps_f2[h][:, c:c + J], q42[64 * h:64 * h + 63, T, q * P:(q + 1) * P],
                                  k42[64 * h:64 * h + 63, T, :], start=True, stop=True)
                last.then_inc(max2_done.sem, 1)

            def max_turn(a, e, dst):
                reduced = (max_red, max2_red)[a]
                pe.wait_ge(reduced.sem, reduced.at(e))
                for q in range(KT):
                    last = mm(dst[0:H, q * P:(q + 1) * P],
                              m_q[a][:, :, :, q].rearrange("p h t -> p (h t)"), ident[:], start=True, stop=True)
                last.then_inc(mt_done[a].sem, 1)

            def scores1(T, e, s):
                if T == 0:
                    pe.wait_ge(m_spread[0].sem, m_spread[0].at(e))
                for h in range(2):
                    for k in range(KT):
                        last = mm(flat[s][:, (2 * h + k) * N:(2 * h + k + 1) * N],
                                  k4[64 * h:64 * h + 64, T, k * P:(k + 1) * P],
                                  q4[64 * h:64 * h + 64, T, :], start=True, stop=True)
                last.then_inc(st_done[0].sem, 1)

            def scores2(g, e, s):
                if g == 0:
                    pe.wait_ge(m_spread[1].sem, m_spread[1].at(e))
                for h in range(2):
                    for u in range(2):
                        last = mm(slot[s][0:J, h, u * N:(u + 1) * N],
                                  k42[64 * h:64 * h + 64, 2 * g + u, :],
                                  q42[64 * h:64 * h + 64, 2 * g + u, :], start=True, stop=True)
                last.then_inc(st_done[1].sem, 1)

            def take_pv(a, g, i, on, bank_of):
                b, prior = bank_of[a, g]
                if prior:
                    freed, step_offset, count = prior
                    pe.wait_ge(freed.sem, freed.at(i + step_offset, count))
                pe.wait_ge(ffp_done.sem, ffp_done.at(i - 3))
                if QKV in on:
                    pe.wait_ge(tr_lo[0].sem, tr_lo[0].at(i + 1))
                return ps_pv[b]

            def values1(g, e, dst):
                pe.wait_ge(exp_done[0].sem, exp_done[0].at(e, 2 * g + 2))
                if g == 0:
                    pe.wait_ge(v_copied.sem, v_copied.at(e))
                for k in range(KT):
                    for r in range(4):
                        T, h = 2 * g + r // 2, r % 2
                        last = mm(dst[32 * r:32 * r + 32, 0:N], v1[:, k, 4 * g + r, :],
                                  probs[:, T % NP, (2 * h + k) * N:(2 * h + k + 1) * N],
                                  start=(k == 0), stop=(k == KT - 1), tile_position=(0, 32 * r))
                last.then_inc(pv_done[0].sem, 1)

            def values2(g, e, dst):
                pe.wait_ge(exp_done[1].sem, exp_done[1].at(e, g + 1))
                if g == 0:
                    pe.wait_ge(v2_copied.sem, v2_copied.at(e))
                for r in range(4):
                    u, h = r // 2, r % 2
                    last = mm(dst[32 * r:32 * r + 32, 0:N], v2[:, 4 * g + r, :],
                              probs[0:J, g, (2 * h + u) * N:(2 * h + u + 1) * N],
                              start=True, stop=True, tile_position=(0, 32 * r))
                last.then_inc(pv_done[1].sem, 1)

            def spread_rec(a, e, s):
                pe.wait_ge(rec_done[a].sem, rec_done[a].at(e))
                for c in range(3):
                    for quarter in range(NC):
                        n0, row = c * N + quarter * (N // NC), sel[:, quarter, c * P:(c + 1) * P]
                        last = product(flat[s][:, n0:n0 + N // NC], [(row, rec_part[a][:, k, :]) for k in range(3)])
                last.then_inc(rb_done[a].sem, 1)

            def out_proj(a, e, s):
                pe.wait_ge(o_lo[a].sem, o_lo[a].at(e))
                wh, wl = ((wo1_h, wo1_l), (wo2_h, wo2_l))[a]
                for q in range(KT):
                    last = by_token(slot[s][:, q, 0:D], wh, wl, 0, D,
                                    o_h[a][:, :, q * P:(q + 1) * P], o_l[a][:, :, q * P:(q + 1) * P])
                last.then_inc(oproj_done[a].sem, 1)

            def ctx_turn(e, on):
                if CROSS in on:
                    pe.wait_ge(mt_row[1].sem, mt_row[1].at(e - 1))
                if QKV in on:
                    pe.wait_ge(qk_lo.sem, qk_lo.at(e + 1, 4))
                pe.wait_ge(c_loaded.sem, c_loaded.at(e))
                for c in range(2):
                    last = nc.tensor.transpose(ps_f2[1][:, c * J:(c + 1) * J], c_in[:, c * P:(c + 1) * P],
                                               ident[0:J, 0:J])
                last.then_inc(ct_done.sem, 1)

            def kv2(e, s):
                pe.wait_ge(ct_lo.sem, ct_lo.at(e))
                for m in range(3):
                    c0, c1 = m * P, min((m + 1) * P, D)
                    by_feature(flat[s][0:c1 - c0, m * J:(m + 1) * J], wkv2_h, wkv2_l, c0, c1, ct_h, ct_l, 1)
                by_token(slot[s][0:J, 1, 0:D], wkv2_h, wkv2_l, D, 2 * D, ct_h, ct_l, 1).then_inc(kv2_done.sem, 1)

            def q2(e, s):
                pe.wait_ge(tr_lo[1].sem, tr_lo[1].at(e))
                for m in range(3):
                    c0, c1 = m * P, min((m + 1) * P, D)
                    last = by_feature(flat[s][0:c1 - c0, m * N:(m + 1) * N], wq2_h, wq2_l, c0, c1, ah[1], al[1])
                last.then_inc(q2_done.sem, 1)

            def ff1(m, e, bank_of):
                if m == 0:
                    for a, g in [use for use, (b, _) in bank_of.items() if ps_pv[b] is ps_f1][-1:]:
                        pe.wait_ge(o_copied[a].sem, o_copied[a].at(e + 2 - a, g + 1))
                    pe.wait_ge(tr_lo[2].sem, tr_lo[2].at(e))
                    pe.wait_ge(ffp_done.sem, ffp_done.at(e - 1))
                else:
                    pe.wait_ge(ffp_done.sem, ffp_done.at(e, m))
                by_feature(ps_f1[:, 0:N], w1_h, w1_l, m * P, (m + 1) * P, ah[2], al[2])
                by_feature(ps_f1[:, N:2 * N], w1_h, w1_l, FF + m * P, FF + (m + 1) * P,
                           ah[2], al[2]).then_inc(ff1_done.sem, 1)

            def ff2(m, e, on):
                if m == 0:
                    if QKV in on:
                        pe.wait_ge(qk_lo.sem, qk_lo.at(e + 3))
                    if SELF in on:
                        pe.wait_ge(ct_lo.sem, ct_lo.at(e + 2))
                    pe.wait_ge(out_ready.sem, out_ready.at(e - 1))
                pe.wait_ge(ffl_done.sem, ffl_done.at(e, m + 1))
                for q in range(KT):
                    xh, xl = ff_h[:, m % 2, q * P:(q + 1) * P], ff_l[:, m % 2, q * P:(q + 1) * P]
                    pairs = [(xh, w2_h[:, m, :]), (xl, w2_h[:, m, :]), (xh, w2_l[:, m, :])]
                    for n, (lhs, rhs) in enumerate(pairs):
                        last = mm(ps_f2[q][:, 0:D], lhs, rhs, start=(m == 0 and n == 0), stop=(m == NM - 1 and n == 2))
                last.then_inc(ff2_step.sem, 1)

            def step(i):
                on, tab = streams_of(i), ring(streams_of(i), before_of(i))
                bank_of = pv_ring(streams_of(i), before_of(i))

                def tile(m):
                    if FFN in on:
                        ff1(m, i - 2, bank_of)
                    if FFN in on and m > 0:
                        ff2(m - 1, i - 2, on)

                def pairs_maxima(key):
                    if QKV in on:
                        for n in MAX_AT.get(key, ()):
                            maxima1(n, i + 1, take(tab, ("max", n), i))

                if LAST in on:
                    ff2(NM - 1, i - 3, on)
                for T in range(NT):
                    if SELF in on and T:
                        scores1(T, i, take(tab, ("st", T), i))
                    if CROSS in on:
                        for u in MAX2_AT.get(T, ()):
                            maxima2(u, i - 1, on)
                    if T == MT2_AT and CROSS in on:
                        max_turn(1, i - 1, ps_f2[1])
                    if T in QK_SELF and QKV in on:
                        qk(QK_SELF[T], i + 1, on)
                    if SELF in on and T % 2 and T > 1:
                        values1(T // 2 - 1, i, take_pv(0, T // 2 - 1, i, on, bank_of))
                for g in range(NG):
                    if CROSS in on:
                        scores2(g, i - 1, take(tab, ("st2", g), i))
                    if g == 0 and SELF in on:
                        values1(NG - 1, i, take_pv(0, NG - 1, i, on, bank_of))
                    if g in QK_CROSS and QKV in on:
                        qk(QK_CROSS[g], i + 1, on)
                    if g == CTX_AT and SELF in on:
                        ctx_turn(i, on)
                    if g >= 1 and CROSS in on:
                        values2(g - 1, i - 1, take_pv(1, g - 1, i, on, bank_of))
                if CROSS in on:
                    values2(NG - 1, i - 1, take_pv(1, NG - 1, i, on, bank_of))
                tile(0)
                if SELF in on:
                    spread_rec(0, i, take(tab, ("rb", 0), i))
                    kv2(i, take(tab, ("kv2", 0), i))
                tile(1)
                if CROSS in on:
                    spread_rec(1, i - 1, take(tab, ("rb", 1), i))
                if SELF in on:
                    out_proj(0, i, take(tab, ("oproj", 0), i))
                tile(2)
                if CROSS in on:
                    out_proj(1, i - 1, take(tab, ("oproj", 1), i))
                pairs_maxima("oproj")
                tile(3)
                pairs_maxima(3)
                if SELF in on:
                    transposes(1, i, flat[take(tab, ("tr", 1), i)])
                tile(4)
                pairs_maxima(4)
                if SELF in on:
                    q2(i, take(tab, ("q2", 0), i))
                pairs_maxima("q2")
                for m in range(5, NM):
                    tile(m)
                    pairs_maxima(m)
                    if m == MT_AT and QKV in on:
                        max_turn(0, i + 1, flat[take(tab, ("mt", 0), i)])
                    if m == TR2_AT and CROSS in on:
                        transposes(2, i - 1, flat[take(tab, ("tr", 2), i)])
                if QKV in on:
                    values(i + 1, take(tab, ("v", 0), i))
                    scores1(0, i + 1, take(tab, ("st", 0), i))
                if NORM1 in on:
                    for b in range(2):
                        for a, g in [use for use, (bank, _) in bank_of.items() if bank == b][-1:]:
                            pe.wait_ge(o_copied[a].sem, o_copied[a].at(i - a, g + 1))
                    if FFN in on:
                        pe.wait_ge(ffp_done.sem, ffp_done.at(i - 2))
                    pe.wait_ge(tr_lo[0].sem, tr_lo[0].at(i + 1))
                    transposes(0, i + 2, ps_t0)

            run_steps(pe, step)

        @block.vector
        def _(dve):
            V = nc.vector
            chained = [0]

            def link(ins):
                chained[0] += 1
                ins.then_inc(pro_dve.sem, 1)
                dve.wait_ge(pro_dve.sem, pro_dve.at(0, chained[0]))

            for tile_, value in ((q4, 0.0), (k4, 0.0), (q42, 0.0), (k42, 0.0), (v1, 1.0), (v2, 1.0),
                                 (ones, 1.0), (mx, 0.0), (mxm, 0.0), (cvec, 0.0)):
                last = V.memset(tile_[:], value)
            link(last)
            V.memset(sc[:], 0.0).then_inc(pro.sem, 1)
            dve.wait_ge(pro.sem, pro.at(0, 1))
            for n in range(N1):
                ch = CHUNKS[n]
                if n == len(CTXCH):
                    dve.wait_ge(vec_loaded.sem, 16 * NVEC_LOADS)
                    for quarter in range(NC):
                        V.tensor_scalar(sel[:, quarter, :], sel_f, c_quarter[:, quarter:quarter + 1], None, ALU.mult)
                dve.wait_ge(staged[n % NSTAGE].sem, staged[n % NSTAGE].at(0, stage_value[n]))
                if ch[0] == "ctx":
                    V.tensor_reduce(mx[0:J, MXCOL[n]:MXCOL[n] + 1], stage_buf(n)[0:J, 0:ch[2] * CTX], AX.X, ALU.max,
                                    apply_absolute_value=True).then_inc(stage_used.sem, 1)
                    continue
                _, name, c0, cw, ln, _ = ch
                ns = slices(t[name].shape[0])
                src = stage_buf(n)[:, 0:ns * cw]
                if ln is not None:
                    dve.wait_ge(scaled.sem, scaled.at(0, times_scaled(n + 1)))
                    src = tmp[n % 2][:, 0:ns * cw]
                    dve.wait_ge(pro_pe.sem, pro_pe.at(0, n - len(CTXCH) + 1))
                if n == N1 - 1:
                    dve.wait_ge(pro_pe.sem, pro_pe.at(0, LNMATS + 1))
                red = V.tensor_reduce(mx[:, MXCOL[n]:MXCOL[n] + 1], src, AX.X, ALU.max, apply_absolute_value=True)
                red.then_inc(stage_used.sem, 1)
                if n == len(CTXCH) + LNMATS - 1:
                    V.tensor_copy(cvec[:, 0:C_V + 2], ps[:, 0, 0:C_V + 2])
                    V.tensor_copy(cvec[0:64, C_V + 2:C_V + 3], ps[0:64, 0, C_V + 2:C_V + 3])
                    V.tensor_copy(cvec[:, C_Q2:C_Q2 + 2], ps[:, 0, C_Q2:C_Q2 + 2])
                    V.tensor_copy(cvec[0:64, C_Q2 + 2:C_W1], ps[0:64, 0, C_Q2 + 2:C_W1])
                    link(V.tensor_copy(cvec[:, C_W1:C_W1 + 2 * NM], ps[:, 0, C_W1:C_W1 + 2 * NM]))
                    for s in range(3):
                        last = V.tensor_scalar(cv_rep[:, s, :], ident[:], 0.0, cvec[:, C_V + s:C_V + s + 1],
                                               ALU.mult, ALU.add)
                    last.then_inc(cv_ready.sem, 1)
                    for c0, c1, col in ((C_QK, C_QK + 5, MXCOL["qk"]), (C_Q2, C_Q2 + 3, MXCOL["q2"])):
                        last = V.tensor_reduce(mx[:, col:col + 1], cvec[:, c0:c1], AX.X, ALU.max,
                                               apply_absolute_value=True)
                    link(last)
                    for col in (MXCOL["qk"], MXCOL["q2"]):
                        last = V.tensor_scalar(mx[:, col:col + 1], mx[:, col:col + 1], 1.0 / 128, None, ALU.mult)
                    link(last)
            dve.wait_ge(stage_used.sem, stage_used.at(0, N1))
            V.tensor_tensor(bias1[:], bias1[:], ps[:, 1, 0:D], ALU.add)
            for gidx, (c0, c1) in enumerate(MXGROUPS):
                last = V.tensor_reduce(mxm[:, gidx:gidx + 1], mx[:, c0:c1], AX.X, ALU.max)
            last.then_inc(maxima.sem, 1)
            dve.wait_ge(pro_pe.sem, pro_pe.at(0, LNMATS + 2))
            link(V.tensor_reduce(mxr[:, 0:1], ps[0:8, 2, 0:P], AX.X, ALU.max))
            link(V.tensor_scalar(mxr[:, 1:2], mxr[:, 0:1], 1e-30, None, ALU.max))
            link(V.tensor_scalar(mxr[:, 2:3].bitcast(u32), mxr[:, 1:2].bitcast(u32), 0x7F800000, None,
                                 ALU.bitwise_and))
            link(V.reciprocal(mxr[:, 3:4], mxr[:, 2:3]))
            V.tensor_scalar(mxd[:], ident[0:8, 0:8], mxr[:, 3:4], None, ALU.mult).then_inc(maxima.sem, 1)
            dve.wait_ge(pro_pe.sem, pro_pe.at(0, LNMATS + 3))
            link(V.tensor_scalar(sc[:, 0:7], ps[:, 3, 0:7], 4.0, None, ALU.mult))
            link(V.tensor_scalar(sc[:, S_CTX:S_CTX + 1], sc[:, S_CTX:S_CTX + 1], 2.0, None, ALU.mult))
            link(V.reciprocal(rp[:, 0:7], sc[:, 0:7]))

            def inverse(k):
                return rp[:, k:k + 1]

            def put(dst, a, b, c):
                link(V.tensor_scalar(sc[:, dst:dst + 1], a, b, c, ALU.mult, ALU.mult))

            put(E1, inverse(S_QKV), DH ** -0.5, inverse(S_QKV))
            put(KV2_CTX, inverse(S_KV2), 1.0, inverse(S_CTX))
            put(E2, inverse(S_Q2), DH ** -0.5, sc[:, KV2_CTX:KV2_CTX + 1])
            put(D1, inverse(S_QKV), 1.0, inverse(S_O1))
            put(D2, inverse(S_O2), 1.0, sc[:, KV2_CTX:KV2_CTX + 1])
            put(D3, inverse(S_W1), 1.0, 1.0)
            V.tensor_scalar(cvec[:, 0:C_Q2], cvec[:, 0:C_Q2], sc[:, S_QKV:S_QKV + 1], None, ALU.mult)
            V.tensor_scalar(cvec[:, C_Q2:C_W1], cvec[:, C_Q2:C_W1], sc[:, S_Q2:S_Q2 + 1], None, ALU.mult)
            link(V.tensor_tensor(cvec[:, C_W1:C_W1 + 2 * NM], cvec[:, C_W1:C_W1 + 2 * NM], b1c[:], ALU.add))
            link(V.tensor_scalar(cvec[:, C_W1:C_W1 + NM], cvec[:, C_W1:C_W1 + NM], sc[:, S_W1:S_W1 + 1], None, ALU.mult))
            for ln, scale in ((0, S_QKV), (1, S_Q2), (2, S_W1)):
                last = V.tensor_scalar(gs[:, ln, :], gb[:, 2 * ln, :], sc[:, scale:scale + 1], None, ALU.mult)
            last.then_inc(scales_ready.sem, 1)
            for n in range(N1, len(CHUNKS)):
                ch = CHUNKS[n]
                if ch[0] == "cut":
                    _, name, c0, cw, _, _ = ch
                    ns = slices(t[name].shape[0])
                    wh, wl, off = DEST[name]
                    wh, wl = wh[:, 0:ns, off + c0:off + c0 + cw], wl[:, 0:ns, off + c0:off + c0 + cw]
                    wh_read = wh
                else:
                    _, s0, ns = ch
                    cw = D
                    wh, wl = w2_h[:, s0:s0 + ns, :], w2_l[:, s0:s0 + ns, :]
                    wh_read = wh.bitcast(f32)
                w = tmp[n % 2][:, 0:ns * cw].rearrange("p (s c) -> p s c", s=ns)
                dve.wait_ge(scaled.sem, scaled.at(0, times_scaled(n + 1)))
                V.tensor_copy(wh, w).then_inc(pro_hi.sem, 1)
                dve.wait_ge(pro_hi.sem, pro_hi.at(0, n - N1 + 1))
                V.tensor_tensor(wl, w, wh_read, ALU.subtract).then_inc(stage_used.sem, 1)
            dve.wait_ge(stage_used.sem, stage_used.at(0, len(CHUNKS)))
            V.memset(mxm[:, 0:1], 0.0).then_inc(pro.sem, 1)

            def layer_norm(k, e):
                src = (x_in, x1, x2)[k]
                if k == 0:
                    dve.wait_ge(x_loaded.sem, x_loaded.at(e))
                else:
                    dve.wait_ge(resid[k - 1].sem, resid[k - 1].at(e))
                for q in range(KT):
                    last = V.bn_stats(stats[k][:, q, :], src[:, q, :])
                last.then_inc(ln_stat[k].sem, 1)
                dve.wait_ge(ln_stat[k].sem, ln_stat[k].at(e, 1))
                V.tensor_copy(pace[:], stats[k][:, 0, 0:1])
                for q in range(KT):
                    last = V.bn_aggr(mv[k][:, q, :], stats[k][:, q, :])
                last.then_inc(ln_stat[k].sem, 1)
                dve.wait_ge(ln_stat[k].sem, ln_stat[k].at(e, 2))
                dve.wait_ge(ln_rstd[k].sem, ln_rstd[k].at(e - 1))
                V.tensor_scalar(ve[k][:], mv[k][:, :, 1], EPS, None, ALU.add).then_inc(ln_stat[k].sem, 1)

            def normalise(k, e, i):
                src = (x_in, x1, x2)[k]
                dve.wait_ge(ln_rstd[k].sem, ln_rstd[k].at(e))
                prior = (tr_done[0], 1, 1) if k == 0 else ring(streams_of(i), before_of(i), XHAT, 1)[k][1]
                if prior:
                    freed, step_offset, count = prior
                    dve.wait_ge(freed.sem, freed.at(i + step_offset, count))
                for q in range(KT):
                    V.tensor_scalar(xhat[k][:, q, 0:D], src[:, q, :], mv[k][:, q, 0:1], rs[k][:, q:q + 1],
                                    ALU.subtract, ALU.mult)
                for q in range(KT):
                    last = V.tensor_scalar(xhat[k][:, q, D:3 * P], src[:, q, 2 * P:D], mv[k][:, q, 0:1],
                                           rs[k][:, q:q + 1], ALU.subtract, ALU.mult)
                last.then_inc(ln_done[k].sem, 1)

            def tr_lo_part(k, e, src):
                dve.wait_ge(tr_hi[k].sem, tr_hi[k].at(e))
                V.tensor_tensor(al[k][:].rearrange("p a b -> p (a b)"), src[:, 0:2 * N],
                                ah[k][:, 0:2].rearrange("p a b -> p (a b)"), ALU.subtract)
                V.tensor_tensor(ah[k][64:P, 2], src[64:P, 2 * N:3 * N], ah[k][64:P, 2],
                                ALU.subtract).then_inc(tr_lo[k].sem, 1)

            def qk_parts(m, e):
                dve.wait_ge(qk_done.sem, qk_done.at(e, m + 1))
                if m == 0:
                    for r in range(4):
                        dve.wait_ge(spread[r].sem, spread[r].at(e - 1))
                V.tensor_scalar(qk_h[:, m, :], ps_f2[m % 2][:, 0:N], cvec[:, C_QK + m:C_QK + m + 1], None,
                                ALU.add).then_inc(qk_hi.sem, 1)
                dve.wait_ge(qk_hi.sem, qk_hi.at(e, m + 1))
                V.scalar_tensor_tensor(qk_l[:, m, :], ps_f2[m % 2][:, 0:N], cvec[:, C_QK + m:C_QK + m + 1],
                                       qk_h[:, m, :], ALU.add, ALU.subtract).then_inc(qk_lo.sem, 1)

            def v_copy(q, e, s):
                dve.wait_ge(v_done.sem, v_done.at(e, q + 1))
                dve.wait_ge(pv_done[0].sem, pv_done[0].at(e - 1))
                V.tensor_copy(v1[:, q, :, 0:2 * DH:2],
                              slot[s][:, q, 0:D].rearrange("p (h d) -> p h d", d=DH)).then_inc(v_copied.sem, 1)

            def out_copy(a, g, e, bank_of):
                dve.wait_ge(pv_done[a].sem, pv_done[a].at(e, g + 1))
                if g == 0:
                    dve.wait_ge(o_spread[a].sem, o_spread[a].at(e - 1))
                    dve.wait_ge(den_spread[a].sem, den_spread[a].at(e - 1))
                V.tensor_copy(o_raw[a][:, g, :], ps_pv[bank_of[a, g][0]][:, 0:N]).then_inc(o_copied[a].sem, 1)

            def q2_lo_part(e, s):
                dve.wait_ge(q2_hi.sem, q2_hi.at(e))
                for m in range(3):
                    r = P if m < 2 else 64
                    last = V.scalar_tensor_tensor(q2_l[0:r, m, :], flat[s][0:r, m * N:(m + 1) * N],
                                                  cvec[0:r, C_Q2 + m:C_Q2 + m + 1], q2_h[0:r, m, :],
                                                  ALU.add, ALU.subtract)
                last.then_inc(q2_lo.sem, 1)

            def ct_parts(e):
                dve.wait_ge(ct_done.sem, ct_done.at(e))
                dve.wait_ge(kv2_done.sem, kv2_done.at(e - 1))
                V.tensor_scalar(ct_h[:].rearrange("p a b -> p (a b)"), ps_f2[1][:, 0:2 * J],
                                sc[:, S_CTX:S_CTX + 1], None, ALU.mult).then_inc(ct_hi.sem, 1)
                dve.wait_ge(ct_hi.sem, ct_hi.at(e))
                V.scalar_tensor_tensor(ct_l[:, 0, :], ps_f2[1][:, 0:J], sc[:, S_CTX:S_CTX + 1], ct_h[:, 0, :],
                                       ALU.mult, ALU.subtract)
                V.scalar_tensor_tensor(ct_h[64:P, 1, :], ps_f2[1][64:P, J:2 * J], sc[64:P, S_CTX:S_CTX + 1],
                                       ct_h[64:P, 1, :], ALU.mult, ALU.subtract).then_inc(ct_lo.sem, 1)

            def kv2_parts(e, s):
                dve.wait_ge(k2_hi.sem, k2_hi.at(e))
                V.tensor_tensor(k2_l[:, 0:2, :].rearrange("p a b -> p (a b)"), flat[s][:, 0:2 * J],
                                k2_h[:, 0:2, :].rearrange("p a b -> p (a b)"), ALU.subtract)
                V.tensor_tensor(k2_l[0:64, 2, :], flat[s][0:64, 2 * J:3 * J], k2_h[0:64, 2, :],
                                ALU.subtract).then_inc(k2_lo.sem, 1)
                dve.wait_ge(pv_done[1].sem, pv_done[1].at(e - 1))
                V.tensor_copy(v2[:, :, 0:2 * DH:2],
                              slot[s][0:J, 1, 0:D].rearrange("p (h d) -> p h d", d=DH)).then_inc(v2_copied.sem, 1)

            def reduce1(n, e, s):
                dve.wait_ge(max_done.sem, max_done.at(e, n + 1))
                if n == 0:
                    dve.wait_ge(mt_done[0].sem, mt_done[0].at(e - 1))
                V.tensor_reduce(m_q[0][:, :, MAX_ORDER[n], :], flat[s].rearrange("p (g k) -> p g k", k=N),
                                AX.X, ALU.max, negate=True).then_inc(max_red.sem, 1)

            def reduce2(u, e):
                (first, nt), h = MAX2_PAIRS[u // 2], u % 2
                dve.wait_ge(max2_done.sem, max2_done.at(e, u + 1))
                if u == 0:
                    dve.wait_ge(mt_done[1].sem, mt_done[1].at(e - 1))
                V.tensor_reduce(m_q[1][:, h, first:first + nt, :].rearrange("p t q -> p (t q)"),
                                ps_f2[h][:, 0:nt * KT * J].rearrange("p (g k) -> p g k", k=J),
                                AX.X, ALU.max, negate=True).then_inc(max2_red.sem, 1)

            def reciprocal(a, e):
                dve.wait_ge(den_spread[a].sem, den_spread[a].at(e))
                dve.wait_ge(rb_done[a].sem, rb_done[a].at(e - 1))
                V.reciprocal(rec[a][:], den[a][:]).then_inc(rec_done[a].sem, 1)
                for k in range(3):
                    dve.wait_ge(rec_done[a].sem, rec_done[a].at(e, 2 * k + 1))
                    V.tensor_copy(rec_part[a][:, k, :], rec[a][:]).then_inc(rec_done[a].sem, 1)
                    if k < 2:
                        dve.wait_ge(rec_done[a].sem, rec_done[a].at(e, 2 * k + 2))
                        V.tensor_tensor(rec[a][:], rec[a][:], rec_part[a][:, k, :],
                                        ALU.subtract).then_inc(rec_done[a].sem, 1)

            def out_norm(a, e, s):
                dve.wait_ge(o_spread[a].sem, o_spread[a].at(e))
                dve.wait_ge(rb_done[a].sem, rb_done[a].at(e))
                c = o_c[a][:].rearrange("p a b -> p (a b)")
                V.tensor_tensor(c, c, flat[s][:, 0:3 * N], ALU.mult).then_inc(o_norm[a].sem, 1)

            def residual(a, e, s):
                dve.wait_ge(oproj_done[a].sem, oproj_done[a].at(e))
                dve.wait_ge(xb_done[a].sem, xb_done[a].at(e))
                dve.wait_ge(xb_done[a + 1].sem, xb_done[a + 1].at(e - 1))
                dst, xb = ((x1, xb1), (x2, xb2))[a]
                V.scalar_tensor_tensor(dst[:], slot[s][:, :, 0:D], sc[:, D1 + a:D1 + a + 1], xb[:],
                                       ALU.mult, ALU.add).then_inc(resid[a].sem, 1)

            def ff_product(m, e):
                dve.wait_ge(gelu_done.sem, gelu_done.at(e, m + 1))
                if m >= 2:
                    dve.wait_ge(ffl_done.sem, ffl_done.at(e, m - 1))
                else:
                    dve.wait_ge(ffl_done.sem, ffl_done.at(e - 1, NM - 1 + m))
                V.scalar_tensor_tensor(ff_g[:, m % 2], ps_f1[:, 0:N], cvec[:, C_W1 + m:C_W1 + m + 1], ff_g[:, m % 2],
                                       ALU.add, ALU.mult).then_inc(ffp_done.sem, 1)

            def output(e):
                dve.wait_ge(ff2_step.sem, ff2_step.at(e))
                dve.wait_ge(xb_done[2].sem, xb_done[2].at(e))
                dve.wait_ge(out_stored.sem, out_stored.at(e - 1))
                V.scalar_tensor_tensor(out_sb[:], ps[:, 6:8, 0:D], sc[:, D3:D3 + 1], xb3[:],
                                       ALU.mult, ALU.add).then_inc(out_ready.sem, 1)

            def step(i):
                on, tab = streams_of(i), ring(streams_of(i), before_of(i))
                bank_of = pv_ring(streams_of(i), before_of(i))

                def tile(m):
                    if FFN in on:
                        ff_product(m, i - 2)

                def pairs_maxima(key):
                    if QKV in on:
                        for n in MAX_AT.get(key, ()):
                            reduce1(n, i + 1, tab["max", n][0])

                for T in range(NT):
                    if LAST in on and T == 0:
                        output(i - 3)
                    if QKV in on and T == 0:
                        tr_lo_part(0, i + 1, ps_t0)
                    if CROSS in on:
                        for u in MAX2_AT.get(T, ()):
                            reduce2(u, i - 1)
                    if T in QK_SELF and QKV in on:
                        qk_parts(QK_SELF[T], i + 1)
                    if SELF in on and T % 2 and T > 1:
                        out_copy(0, T // 2 - 1, i, bank_of)
                if SELF in on:
                    out_copy(0, NG - 1, i, bank_of)
                for g in range(NG):
                    if g in QK_CROSS and QKV in on:
                        qk_parts(QK_CROSS[g], i + 1)
                    if g == CTX_AT and SELF in on:
                        ct_parts(i)
                    if g >= 1 and CROSS in on:
                        out_copy(1, g - 1, i - 1, bank_of)
                    if g == NG - 1 and SELF in on:
                        reciprocal(0, i)
                if CROSS in on:
                    out_copy(1, NG - 1, i - 1, bank_of)
                tile(0)
                if SELF in on:
                    out_norm(0, i, tab["rb", 0][0])
                if CROSS in on:
                    reciprocal(1, i - 1)
                if SELF in on:
                    kv2_parts(i, tab["kv2", 0][0])
                tile(1)
                if CROSS in on:
                    out_norm(1, i - 1, tab["rb", 1][0])
                if SELF in on:
                    residual(0, i, tab["oproj", 0][0])
                if SELF in on:
                    layer_norm(1, i)
                tile(2)
                if SELF in on:
                    normalise(1, i, i)
                if CROSS in on:
                    residual(1, i - 1, tab["oproj", 1][0])
                pairs_maxima("oproj")
                tile(3)
                pairs_maxima(3)
                if SELF in on:
                    tr_lo_part(1, i, flat[tab["tr", 1][0]])
                if CROSS in on:
                    layer_norm(2, i - 1)
                tile(4)
                pairs_maxima(4)
                pairs_maxima("q2")
                if SELF in on:
                    q2_lo_part(i, tab["q2", 0][0])
                for m in range(5, NM):
                    tile(m)
                    pairs_maxima(m)
                    if m == 8 and CROSS in on:
                        normalise(2, i - 1, i)
                    if m == 8 and NORM1 in on:
                        layer_norm(0, i + 2)
                    if m == 9 and NORM1 in on:
                        normalise(0, i + 2, i)
                    if m == TR2_AT and CROSS in on:
                        tr_lo_part(2, i - 1, flat[tab["tr", 2][0]])
                if QKV in on:
                    for q in range(KT):
                        v_copy(q, i + 1, tab["v", 0][0])

            run_steps(dve, step)


_PRE = "L0_xattn_"
_INS = ["n1_g", "n1_b", "q1", "k1", "v1", "o1_w", "o1_b", "n2_g", "n2_b", "q2", "k2", "v2", "o2_w", "o2_b",
        "n3_g", "n3_b", "ff_w1", "ff_b1", "ff_w2", "ff_b2"]


def _constants():
    import numpy as np
    sel = np.zeros((NC * H, 3 * P), np.float32)
    for f in range(3 * P):
        h = (f if f < D else f - 64) // DH
        row = (NG * (h % 4) + h // 4) * NC
        sel[row:row + NC, f] = 1.0
    return {"c_ident": np.eye(P, dtype=np.float32), "c_sel": sel,
            "c_quarter": np.tile(np.eye(NC, dtype=np.float32), (H, 1)),
            "c_aug": np.full((1, NT * N), AUG, np.float16)}


def kernel(**inputs):
    import numpy as _np
    import concourse.bacc as _bacc
    from concourse import mybir as _mybir
    from concourse.bass_utils import run_bass_kernel_spmd as _run

    nc = _bacc.Bacc("TRN2", target_bir_lowering=False, num_devices=1)
    host = {"x": inputs["x"], "ctx_768": inputs["ctx_768"]}
    host.update({n: inputs[_PRE + n] for n in _INS})
    host.update(_constants())
    arrays, aps = {}, {}
    for name, a in host.items():
        a = _np.ascontiguousarray(a)
        arrays[f"in_{name}"] = a
        aps[name] = nc.dram_tensor(f"in_{name}", a.shape, _mybir.dt.from_np(a.dtype), kind="ExternalInput").ap()
    o = nc.dram_tensor("out_0", (B, N, D), _mybir.dt.float32, kind="ExternalOutput").ap()
    xattn_block(nc, aps, o)
    r = _run(nc, [arrays], core_ids=[0])
    return r.results[0]["out_0"]
```
